# Optimizing a Trainium2 kernel written in Bass

```python
import numpy as np
import jax
import jax.numpy as jnp

def _softmax(x, axis=-1):
    return jax.nn.softmax(x, axis=axis)

def _gelu(x):
    return jax.nn.gelu(x, approximate=True)

def _silu(x):
    return jax.nn.silu(x)

def _sigmoid(x):
    return jax.nn.sigmoid(x)

def _layernorm(x, axis=-1, eps=1e-05):
    m = jnp.mean(x, axis=axis, keepdims=True)
    v = jnp.var(x, axis=axis, keepdims=True)
    return (x - m) / jnp.sqrt(v + eps)

def _scatter_add(tgt, idx, src, axis=0):
    return tgt.at[idx].add(src)

def _segment_sum(src, seg, n):
    return jax.ops.segment_sum(src, seg, n)
kernel_name = 'mk_gnn_preln_d1_gnn_r32_4738a3'

def setup_inputs(seed: int=0):
    np.random.seed(seed)
    _w = jnp.asarray

    def _rec_inputs():
        import jax
        import jax.numpy as jnp
        _gk = jax.random.key(seed)
        x = -0.0006008 + 1.001 * jax.random.normal(jax.random.fold_in(_gk, 1), (3125, 128), jnp.float32)
        _s = jax.random.randint(jax.random.fold_in(_gk, 2), (50000,), 0, 3125, jnp.int32)
        _d = jax.random.randint(jax.random.fold_in(_gk, 3), (50000,), 0, 3125, jnp.int32)
        _loop = jnp.arange(3125, dtype=jnp.int32)
        src = jnp.concatenate([_s, _d, _loop])
        dst = jnp.concatenate([_d, _s, _loop])
        _o = jnp.argsort(dst, stable=True)
        src = src[_o]
        dst = dst[_o]
        return (x, src, dst)
    x, src, dst = _rec_inputs()

    def _L0_gnn_setup():
        import jax, jax.numpy as jnp
        import numpy as np
        TOPK = 2
        key = jax.random.key(seed)
        ks = jax.random.split(key, 18)
        N, E = (625, 10000)
        IN, H, OUT, L = (128, 256, 128, 3)
        NW, NS = (4, 4)
        NE = NW + NS

        def w(k, shape, fan):
            return jax.random.normal(k, shape, dtype=jnp.float32) / np.float32(np.sqrt(fan))
        inp = {'x': jax.random.normal(ks[0], (N, IN), dtype=jnp.float32), 'edge_index': jax.random.randint(ks[1], (2, E), 0, N, dtype=jnp.int64), 'W_in': w(ks[2], (IN, H), IN), 'b_in': jnp.zeros((H,), jnp.float32), 'router_W': w(ks[3], (L, 2 * H, NE), 2 * H), 'router_b': jnp.zeros((L, NE), jnp.float32), 'weak_W': w(ks[4], (L, NW, H, H), H), 'weak_b': jnp.zeros((L, NW, H), jnp.float32), 'strong_W1': w(ks[5], (L, NS, H, 2 * H), H), 'strong_b1': jnp.zeros((L, NS, 2 * H), jnp.float32), 'strong_W2': w(ks[6], (L, NS, 2 * H, H), 2 * H), 'strong_b2': jnp.zeros((L, NS, H), jnp.float32), 'conf_W': w(ks[7], (L, H, 1), H), 'conf_b': jnp.zeros((L, 1), jnp.float32), 'W_out': w(ks[8], (H, OUT), H), 'b_out': jnp.zeros((OUT,), jnp.float32)}
        return inp
    _L0_gnn_all = _L0_gnn_setup()
    _L0_gnn_in = {k: v for k, v in _L0_gnn_all.items() if k in ('W_in', 'b_in', 'router_W', 'router_b', 'weak_W', 'weak_b', 'strong_W1', 'strong_b1', 'strong_W2', 'strong_b2', 'conf_W', 'conf_b', 'W_out', 'b_out')}
    del _L0_gnn_all
    return {'x': x, 'src': src, 'dst': dst, 'L0_gnn_W_in': _L0_gnn_in['W_in'], 'L0_gnn_b_in': _L0_gnn_in['b_in'], 'L0_gnn_router_W': _L0_gnn_in['router_W'], 'L0_gnn_router_b': _L0_gnn_in['router_b'], 'L0_gnn_weak_W': _L0_gnn_in['weak_W'], 'L0_gnn_weak_b': _L0_gnn_in['weak_b'], 'L0_gnn_strong_W1': _L0_gnn_in['strong_W1'], 'L0_gnn_strong_b1': _L0_gnn_in['strong_b1'], 'L0_gnn_strong_W2': _L0_gnn_in['strong_W2'], 'L0_gnn_strong_b2': _L0_gnn_in['strong_b2'], 'L0_gnn_conf_W': _L0_gnn_in['conf_W'], 'L0_gnn_conf_b': _L0_gnn_in['conf_b'], 'L0_gnn_W_out': _L0_gnn_in['W_out'], 'L0_gnn_b_out': _L0_gnn_in['b_out']}

def reference(x, src, dst, L0_gnn_W_in, L0_gnn_b_in, L0_gnn_router_W, L0_gnn_router_b, L0_gnn_weak_W, L0_gnn_weak_b, L0_gnn_strong_W1, L0_gnn_strong_b1, L0_gnn_strong_W2, L0_gnn_strong_b2, L0_gnn_conf_W, L0_gnn_conf_b, L0_gnn_W_out, L0_gnn_b_out):
    import jax
    import jax.numpy as jnp

    def _L0_gnn_ref(x, edge_index, W_in, b_in, router_W, router_b, weak_W, weak_b, strong_W1, strong_b1, strong_W2, strong_b2, conf_W, conf_b, W_out, b_out):
        import jax, jax.numpy as jnp
        import numpy as np
        TOPK = 2
        N = x.shape[0]
        L = router_W.shape[0]
        src = edge_index[0]
        dst = edge_index[1]
        deg = jax.ops.segment_sum(jnp.ones(src.shape, x.dtype), dst, num_segments=N)
        deg = jnp.clip(deg, 1.0)[:, None]
        h = x @ W_in + b_in
        rows = jnp.arange(N)[:, None]
        for l in range(L):
            agg = jax.ops.segment_sum(h[src], dst, num_segments=N) / deg
            logits = jnp.concatenate([h, agg], axis=-1) @ router_W[l] + router_b[l]
            vals, idx = jax.lax.top_k(logits, TOPK)
            gates = jax.nn.softmax(vals, axis=-1)
            gate_dense = jnp.zeros_like(logits).at[rows, idx].set(gates)
            weak = jax.nn.relu(jnp.einsum('nh,ehf->nef', agg, weak_W[l]) + weak_b[l])
            sh = jax.nn.relu(jnp.einsum('nh,ehf->nef', agg, strong_W1[l]) + strong_b1[l])
            strong = jnp.einsum('nef,efh->neh', sh, strong_W2[l]) + strong_b2[l]
            experts = jnp.concatenate([weak, strong], axis=1)
            moe = jnp.einsum('ne,neh->nh', gate_dense, experts)
            conf = jax.nn.sigmoid(h @ conf_W[l] + conf_b[l])
            h = h + conf * moe
        return h @ W_out + b_out
    edge_index = jnp.stack([src, dst])
    h = jnp.maximum(_layernorm(x, axis=-1), 0.0)
    x = x + _L0_gnn_ref(h, edge_index, L0_gnn_W_in, L0_gnn_b_in, L0_gnn_router_W, L0_gnn_router_b, L0_gnn_weak_W, L0_gnn_weak_b, L0_gnn_strong_W1, L0_gnn_strong_b1, L0_gnn_strong_W2, L0_gnn_strong_b2, L0_gnn_conf_W, L0_gnn_conf_b, L0_gnn_W_out, L0_gnn_b_out)
    return x

_drawn_inputs = setup_inputs


def setup_inputs(seed=0):
    import zlib

    import numpy as np

    out = dict(_drawn_inputs(seed))
    spreads = {'L0_gnn_b_in': (0.0, 0.1),
     'L0_gnn_router_b': (0.0, 0.1),
     'L0_gnn_weak_b': (0.0, 0.1),
     'L0_gnn_strong_b1': (0.0, 0.1),
     'L0_gnn_strong_b2': (0.0, 0.1),
     'L0_gnn_conf_b': (0.0, 0.485),
     'L0_gnn_b_out': (0.0, 0.1)}
    factors = {}
    for name, (base, spread) in spreads.items():
        noise = np.random.default_rng([zlib.crc32(name.encode()), seed]).standard_normal(out[name].shape)
        drawn = base * np.exp(spread * noise) if base else spread * noise
        out[name] = jnp.asarray(drawn.astype(out[name].dtype))
    for name, factor in factors.items():
        out[name] = (out[name] * factor).astype(out[name].dtype)
    return out
```

```python
import concourse.bass as bass
from concourse import mybir
from contextlib import ExitStack

F32 = mybir.dt.float32
F32R = mybir.dt.float32r
BF16 = mybir.dt.bfloat16
F16 = mybir.dt.float16
I32 = mybir.dt.int32
U32 = mybir.dt.uint32
ACT = mybir.ActivationFunctionType
ALU = mybir.AluOpType
AX = mybir.AxisListType

P = 128
EPS = 1e-5


def gnn_program(nc, x, edges, dst, w_in, b_in, route_w, route_b, pieces, weak_b, b1, b2, w_out, b_out, out):
    N, IN = x.shape
    E = edges.shape[0]
    LAYERS, _, KR, NE1 = route_w.shape
    NE = NE1 - 1
    NWEAK = weak_b.shape[1]
    NSTRONG = NE - NWEAK
    WQ = pieces.shape[1]
    KH = KR // 2
    H = KH * P
    KF = b1.shape[2] // NSTRONG
    OUT = w_out.shape[2]
    NB = (N + P - 1) // P
    LROWS = N - (NB - 1) * P
    WIN = 16
    CH = 5
    CAP = CH * P
    GROUPS = (N + WIN - 1) // WIN
    GP = P // WIN
    GBODY = 2 * GP
    SLOTS = GBODY * CH
    MW = NB * WIN
    ROWS = 125
    ROWLEN = E // ROWS
    TOK = 2 * P
    REGION = -(-N // TOK) * TOK
    XROWS = NE * REGION + TOK
    TRIPS = (NB - 1) // 2
    assert ROWS * ROWLEN == E and NB % 2 == 1 and KH == 2 and WQ <= 2 * TRIPS and WQ % 2 == 0

    at_dram = nc.dram_tensor("at_scratch", (NB, P, NB * P), F16)
    starts_dram = nc.dram_tensor("starts_scratch", (2 * P,), I32)
    at_upper_dram = nc.dram_tensor("at_upper_scratch", (NB, P, NB * P), BF16)
    slot_x = nc.dram_tensor("slot_inputs", (XROWS, H), F32)
    slot_y = nc.dram_tensor("slot_results", (XROWS, H), F32)

    with ExitStack() as ctx:
        def sb(name, shape, dt, c=ctx):
            return c.enter_context(nc.sbuf_tensor(name, list(shape), dt))

        def sem(name):
            return ctx.enter_context(nc.semaphore(name))

        h_all = sb("h_all", [P, NB, H], F32)
        hparts = sb("hparts", [P, NB, 3, H], BF16)
        h_logits = sb("h_logits", [P, NB, NE1], F32)
        rdeg = sb("rdeg", [P, NB], F32)
        route_sb = sb("route_sb", [P, LAYERS, KR, NE1], F32)
        route_b_sb = sb("route_b_sb", [1, LAYERS, NE1], F32)
        identf = sb("identf", [P, P], F32)
        onesb = sb("onesb", [P, P], BF16)
        before_b = sb("before_b", [P, P], BF16)
        ones_row = sb("ones_row", [1, P], F32)
        expert_no = sb("expert_no", [P, NE], F32)
        region_0 = sb("region_0", [P, NE], F32)
        slow_flag = sb("slow_flag", [1, 1], I32)
        h_new = sb("h_new", [P, 2, H], F32)
        h_rest = sb("h_rest", [P, 2, H], F32)
        hT = sb("hT", [P, 2, KH, P], F32)
        bank = [ctx.enter_context(nc.psum_tensor(f"bank{i}", [P, 512], F32)) for i in range(8)]

        held = sem("held")

        def hold(eng, s, value):
            eng.wait_ge(s, value)
            eng.sem_inc(held, 1)

        new_ready = sem("new_ready")
        kept = sem("kept")
        parts_done = sem("parts_done")
        hT_done = sem("hT_done")
        hT_ready = sem("hT_ready")
        hl_done = sem("hl_done")
        hl_kept = sem("hl_kept")

        def parts_of_block(dve, n, b, u):
            nc.vector.tensor_copy(hparts[:, bass.ds(b, 1), 0].rearrange("p o f -> p (o f)"), h_new[:, u])
            dve.drain()
            nc.vector.tensor_tensor(h_rest[:, u], h_new[:, u],
                                    hparts[:, bass.ds(b, 1), 0].rearrange("p o f -> p (o f)"), ALU.subtract)
            dve.drain()
            nc.vector.tensor_copy(hparts[:, bass.ds(b, 1), 1].rearrange("p o f -> p (o f)"), h_rest[:, u])
            dve.drain()
            nc.vector.tensor_tensor(hparts[:, bass.ds(b, 1), 2].rearrange("p o f -> p (o f)"), h_rest[:, u],
                                    hparts[:, bass.ds(b, 1), 1].rearrange("p o f -> p (o f)"), ALU.subtract
                                    ).then_inc(parts_done, 1)

        def keep_block(act, n, b, u, logits=True):
            hold(act, new_ready, n + 1)
            nc.scalar.activation(h_all[:, bass.ds(b, 1)].rearrange("p o f -> p (o f)"), h_new[:, u], ACT.Copy
                                 ).then_inc(kept, 1)
            act.wait_ge(hT_done, n + 3)
            act.wait_ge(hl_done, n + 1)
            nc.scalar.activation(hT[:, u].rearrange("p k n -> p (k n)"), bank[6 + u][:, 0:H], ACT.Copy
                                 ).then_inc(hT_ready, 1)
            if logits:
                hold(act, hl_done, n + 3)
                nc.scalar.activation(h_logits[:, bass.ds(b, 1)].rearrange("p o e -> p (o e)"),
                                     bank[4 + u][:, 0:NE1], ACT.Copy).then_inc(hl_kept, 1)

        def transpose_block(pe, n, u):
            pe.wait_ge(new_ready, n + 1)
            pe.wait_ge(hT_ready, n + 1)
            for k in range(KH):
                last = nc.tensor.transpose(bank[6 + u][:, k * P:(k + 1) * P], h_new[:, u, k * P:(k + 1) * P], identf[:])
            last.then_inc(hT_done, 1)

        def logits_of_block(pe, n, u, layer):
            pe.wait_ge(hT_ready, n + 3)
            hold(pe, hl_kept, n + 1)
            for k in range(KH):
                nc.tensor.matmul(bank[4 + u][:, 0:NE1], hT[:, u, k, :],
                                 route_sb[:, bass.ds(layer, 1), k, :].rearrange("p o e -> p (o e)"),
                                 start=(k == 0), stop=False)
            nc.tensor.matmul(bank[4 + u][:, 0:NE1], ones_row[:],
                             route_b_sb[:, bass.ds(layer, 1)].rearrange("p o e -> p (o e)"), start=False, stop=True
                             ).then_inc(hl_done, 1)

        with ExitStack() as c1:
            def sb1(name, shape, dt):
                return sb(name, shape, dt, c1)

            x_all = sb1("x_all", [P, NB, IN], F32)
            stats = sb1("stats", [P, NB, 6], F32)
            mv = sb1("mv", [P, NB, 2], F32)
            std = sb1("std", [P, NB], F32)
            rstd = sb1("rstd", [P, NB], F32)
            epsc = sb1("epsc", [P, 1], F32)
            h0 = sb1("h0", [P, 2, P], F32)
            w_in_sb = sb1("w_in_sb", [P, H], F32)
            b_in_sb = sb1("b_in_sb", [P, H], F32)
            iota_s = sb1("iota_s", [P, P], F16)
            iota_m = sb1("iota_m", [P, MW], F16)
            gidx = sb1("gidx", [P, GROUPS, CH], F32)
            thr = sb1("thr", [P, 2 * P], F32)
            thrcol = sb1("thrcol", [P, 2], F32)
            ones1 = sb1("ones1", [P, 1], F32)
            last_i = sb1("last_i", [P, 1], I32)
            last_f = sb1("last_f", [P, 1], F32)
            before = sb1("before", [P, 2 * P], F32)
            full_rows = sb1("full_rows", [P, 2], F32)
            row_idx = sb1("row_idx", [P, 2], U32)
            rows_i = sb1("rows_i", [P, 2, ROWLEN], I32)
            rows_f = sb1("rows_f", [P, 2, ROWLEN], F32)
            cnt = sb1("cnt", [P, 2], F32)
            start_f = sb1("start_f", [P, 2], F32)
            start_i = sb1("start_i", [P, 2], I32)
            start_row = sb1("start_row", [1, 2 * P], I32)
            ed = sb1("ed", [P, 2, SLOTS, 2], I32)
            src_hi = sb1("src_hi", [P, SLOTS], I32)
            src_lo = sb1("src_lo", [P, SLOTS], I32)
            dst_lo = sb1("dst_lo", [P, SLOTS], I32)
            dst_hi = sb1("dst_hi", [P, SLOTS], I32)
            col = sb1("col", [P, SLOTS], F32)
            valid = sb1("valid", [P, SLOTS], F32)
            key_m = sb1("key_m", [P, SLOTS], F32)
            key_s = sb1("key_s", [P, 2, SLOTS], F32)
            vsum = sb1("vsum", [P, 1], F32)
            vtotal = sb1("vtotal", [P, 1], F32)
            oh_s = sb1("oh_s", [P, 4, CH, P], F16)
            oh_m = sb1("oh_m", [P, 2, CH, MW], F16)
            piece = sb1("piece", [P, 2, NB, P], F16)
            zero = sb1("zero", [P, H], F32)
            junk = sb1("junk", [P, ROWLEN], F32)

            s_const = sem("s_const")
            s_zero = sem("s_zero")
            s_cleared = sem("s_cleared")
            s_wait = sem("s_wait")
            s_last = sem("s_last")
            x_in = sem("x_in")
            var_ready = sem("var_ready")
            std_ready = sem("std_ready")
            y_ready = sem("y_ready")
            yT_done = sem("yT_done")
            h0_ready = sem("h0_ready")
            proj_done = sem("proj_done")
            before_ready = sem("before_ready")
            full_done = sem("full_done")
            idx_ready = sem("idx_ready")
            rows_in = [sem("rows_in0"), sem("rows_in1")]
            start_ready = sem("start_ready")
            start_out = sem("start_out")
            start_in = sem("start_in")
            ed_in = [sem("ed_in0"), sem("ed_in1")]
            keys_ready = sem("keys_ready")
            hot_s_ready = sem("hot_s_ready")
            hot_m_ready = sem("hot_m_ready")
            win_done = sem("win_done")
            win_evac = sem("win_evac")
            deg_done = sem("deg_done")
            rdeg_ready = sem("rdeg_ready")
            at_stored = [sem("at_stored0"), sem("at_stored1")]
            piece_free = sem("piece_free")
            vtotal_ready = sem("vtotal_ready")
            vsum_done = sem("vsum_done")
            flag_ready = sem("flag_ready")

            block = c1.enter_context(nc.Block())
            LASTG = GROUPS - 2 * TRIPS * GP
            BODIES = TRIPS

            @block.sync
            def _(sp):
                sp.dma_start(x_all[:, 0:NB - 1], x[0:(NB - 1) * P, :].rearrange("(b p) f -> p b f", p=P)).then_inc(x_in, 16)
                sp.wait_ge(s_zero, 1)
                sp.dma_start(x_all[0:LROWS, NB - 1], x[(NB - 1) * P:N, :]).then_inc(x_in, 16)
                with nc.allow_non_contiguous_dma(reason="one word a row"):
                    sp.dma_start(last_i[0:ROWS, :], dst.rearrange("(p k) -> p k", p=ROWS)[:, ROWLEN - 1:ROWLEN]
                                 ).then_inc(s_last, 16)
                sp.dma_start(w_in_sb[:], w_in).then_inc(s_wait, 16)
                sp.dma_start(b_in_sb[:], b_in.rearrange("(o f) -> o f", o=1).to_broadcast([P, H])).then_inc(s_wait, 16)
                sp.dma_start(route_sb[:], route_w.rearrange("l p k e -> p l k e")).then_inc(s_wait, 16)
                sp.dma_start(route_b_sb[:], route_b.rearrange("(o l) e -> o l e", o=1)).then_inc(s_wait, 16)

                sp.wait_ge(start_ready, 1)
                for k in range(2):
                    sp.dma_start(starts_dram[k * P:(k + 1) * P].rearrange("(p o) -> p o", o=1),
                                 start_i[:, k:k + 1]).then_inc(start_out, 16)
                sp.wait_ge(start_out, 32)
                sp.dma_start(start_row[:, :], starts_dram[:].rearrange("(o g) -> o g", o=1)).then_inc(start_in, 16)
                sp.wait_ge(start_in, 16)

                def fetch(b, par, count):
                    hold(sp, keys_ready, b + 1)
                    with sp.Fori(0, count) as g:
                        first = sp.value_load(start_row[0:1, bass.ds(b * GBODY + g, 1)], min_val=0, max_val=E - CAP)
                        sp.dma_start(ed[:, par, bass.ds(g * CH, CH), :],
                                     edges[bass.ds(first, CAP), :].rearrange("(p k) two -> p k two", k=CH)
                                     ).then_inc(ed_in[par], 16)

                def store(k, slot, uses):
                    hold(sp, rdeg_ready, k + 3)
                    sp.dma_start(at_dram[bass.ds(k, 1)].rearrange("o p c -> p (o c)"),
                                 piece[:, slot].rearrange("p s d -> p (s d)")).then_inc(at_stored[slot], 16)
                    hold(sp, at_stored[slot], 16 * uses)
                    sp.sem_inc(piece_free, 1)

                sp.sem_inc(piece_free, 2)
                fetch(0, 0, GBODY)
                fetch(1, 1, GBODY)
                with sp.Fori(0, BODIES // 2 - 1) as i:
                    for par in range(2):
                        store(4 * i + 2 * par, 0, 2 * i + par + 1)
                        store(4 * i + 2 * par + 1, 1, 2 * i + par + 1)
                        hold(sp, ed_in[par], 16 * GBODY * (i + 1))
                        fetch(2 * i + 2 + par, par, GBODY)
                for par in range(2):
                    store(NB - 5 + 2 * par, 0, BODIES - 1 + par)
                    store(NB - 4 + 2 * par, 1, BODIES - 1 + par)
                    if par == 0:
                        sp.wait_ge(ed_in[0], 16 * GBODY * (BODIES // 2))
                        fetch(BODIES, 0, LASTG)
                store(NB - 1, 0, BODIES + 1)

            @block.gpsimd
            def _(pool):
                nc.gpsimd.memset(zero[:], 0.0)
                nc.gpsimd.memset(x_all[:, NB - 1], 0.0)
                pool.drain().then_inc(s_zero, 1)
                nc.gpsimd.memset(identf[:], 0.0)
                nc.gpsimd.memset(onesb[:], 1.0)
                nc.gpsimd.memset(before_b[:], 1.0)
                nc.gpsimd.memset(ones_row[:], 1.0)
                nc.gpsimd.memset(ones1[:], 1.0)
                nc.gpsimd.memset(epsc[:], EPS)
                nc.gpsimd.memset(piece[:], 0.0)
                nc.gpsimd.memset(last_f[:], 1e9)
                nc.gpsimd.memset(vtotal[:], 0.0)
                for tile, pattern, base, per_row in (
                        (iota_s, [[1, P]], 0, 0), (iota_m, [[1, MW]], 1, 0),
                        (gidx, [[1, GROUPS], [0, CH]], 0, 0), (thr, [[WIN, 2 * P]], 0, 0),
                        (thrcol, [[WIN * P, 2]], 0, WIN), (expert_no, [[1, NE]], 0, 0),
                        (region_0, [[REGION, NE]], 0, 0)):
                    nc.gpsimd.iota(tile[:], pattern=pattern, base=base, channel_multiplier=per_row,
                                   allow_small_or_imprecise_dtypes=True)
                pool.drain()
                nc.gpsimd.affine_select(out=identf[:], in_=identf[:], compare_op=ALU.not_equal, fill=1.0,
                                        base=0, pattern=[[-1, P]], channel_multiplier=1)
                nc.gpsimd.affine_select(out=before_b[:], in_=before_b[:], compare_op=ALU.is_gt, fill=0.0,
                                        base=0, pattern=[[1, P]], channel_multiplier=-1)
                pool.drain().then_inc(s_const, 1)
                pool.wait_ge(idx_ready, 1)
                for k in range(2):
                    nc.gpsimd.indirect_dma_start(
                        out=rows_i[:, k, :], out_offset=None, in_=dst.rearrange("(p k) -> p k", p=ROWS),
                        in_offset=bass.IndirectOffsetOnAxis(ap=row_idx[:, k:k + 1], axis=0),
                        bounds_check=ROWS - 1, oob_is_err=False).then_inc(rows_in[k], 16)

                def one_hots(n, gi, par):
                    hold(pool, win_done, n + 1)
                    for c in range(CH):
                        s = gi * CH + c
                        last = nc.gpsimd.tensor_scalar(oh_s[:, gi % 4, c], iota_s[:], key_s[:, par, s:s + 1], None,
                                                       ALU.is_equal)
                    last.then_inc(hot_s_ready, 1)

                with pool.Fori(0, BODIES // 2) as i:
                    for par in range(2):
                        hold(pool, keys_ready, 2 * i + par + 3)
                        for gi in range(GBODY):
                            one_hots((2 * i + par) * GBODY + gi, gi, par)
                hold(pool, keys_ready, BODIES + 3)
                for gi in range(LASTG):
                    one_hots(BODIES * GBODY + gi, gi, 0)

            @block.scalar
            def _(act):
                act.sem_inc(win_evac, 4)
                act.sem_inc(kept, 2)
                act.sem_inc(hT_ready, 2)
                act.sem_inc(hl_kept, 2)
                act.sem_inc(h0_ready, 2)
                act.wait_ge(s_zero, 1)
                per = XROWS // P // 7
                for slots in (slot_x, slot_y):
                    for k in range(7):
                        act.dma_start(slots[k * per * P:(k + 1) * per * P, :].rearrange("(p r) f -> p r f", p=P),
                                      zero[:].unsqueeze(1).to_broadcast([P, per, H])).then_inc(s_cleared, 16)
                act.wait_ge(s_const, 1)
                act.wait_ge(var_ready, 1)
                nc.scalar.activation(std[:], mv[:, :, 1], ACT.Sqrt, bias=epsc[:, 0:1]).then_inc(std_ready, 1)

                def relu(b):
                    act.wait_ge(yT_done, b + 1)
                    act.wait_ge(proj_done, b + 1)
                    nc.scalar.activation(h0[:, b % 2], bank[b % 2][:, 0:P], ACT.Relu).then_inc(h0_ready, 1)

                relu(0)
                for b in range(NB):
                    if b + 1 < NB:
                        relu(b + 1)
                    keep_block(act, b, b, b % 2)

                def evacuate(n, gi, slot):
                    act.wait_ge(win_done, n + 5)
                    nc.scalar.activation(piece[:, slot, :, (gi % GP) * WIN:(gi % GP + 1) * WIN],
                                         bank[gi % 4][:, 0:MW].rearrange("p (s d) -> p s d", d=WIN),
                                         ACT.Copy).then_inc(win_evac, 1)

                with act.Fori(0, BODIES) as i:
                    for k in range(2):
                        act.wait_ge(piece_free, 2 * i + k + 1)
                        for gi in range(GP):
                            evacuate((2 * i + k) * GP + gi, gi, k)
                act.wait_ge(piece_free, NB)
                for gi in range(LASTG):
                    evacuate(2 * BODIES * GP + gi, gi, 0)
                act.wait_ge(s_cleared, 14 * 16)

            @block.vector
            def _(dve):
                dve.sem_inc(keys_ready, 2)
                dve.sem_inc(rdeg_ready, 2)
                dve.wait_ge(x_in, 32)
                for b in range(NB):
                    nc.vector.bn_stats(stats[:, b, :], x_all[:, b, :])
                dve.drain()
                for b in range(NB):
                    nc.vector.bn_aggr(mv[:, b, :], stats[:, b, :])
                dve.drain().then_inc(var_ready, 1)

                dve.wait_ge(s_const, 1)
                dve.wait_ge(s_last, 16)
                nc.vector.tensor_copy(last_f[0:ROWS, :], last_i[0:ROWS, :])
                dve.drain()
                nc.vector.tensor_scalar(before[:], thr[:], last_f[:, 0:1], None, ALU.is_gt).then_inc(before_ready, 1)
                dve.wait_ge(full_done, 1)
                nc.vector.tensor_copy(full_rows[:], bank[3][:, 0:2])
                dve.drain()
                nc.vector.tensor_scalar(row_idx[:], full_rows[:], float(ROWS - 1), None, ALU.min).then_inc(idx_ready, 1)

                dve.wait_ge(std_ready, 1)
                nc.vector.reciprocal(rstd[:], std[:])
                dve.drain()
                for b in range(NB):
                    nc.vector.tensor_scalar(x_all[:, b, :], x_all[:, b, :], mv[:, b, 0:1], rstd[:, b:b + 1],
                                            ALU.subtract, ALU.mult).then_inc(y_ready, 1)

                for k in range(2):
                    dve.wait_ge(rows_in[k], 16)
                    nc.vector.tensor_copy(rows_f[:, k], rows_i[:, k])
                    dve.drain()
                    nc.vector.tensor_scalar(junk[:], rows_f[:, k], thrcol[:, k:k + 1], None, ALU.is_lt, ALU.add,
                                            accum_out=cnt[:, k:k + 1])
                    dve.drain()
                nc.vector.scalar_tensor_tensor(start_f[:], full_rows[:], float(ROWLEN), cnt[:], ALU.mult, ALU.add)
                dve.drain()
                nc.vector.tensor_scalar(start_i[:], start_f[:], float(E - CAP), None, ALU.min).then_inc(start_ready, 1)

                dve.wait_ge(s_wait, 64)
                for b in range(NB):
                    dve.wait_ge(proj_done, b + 3)
                    dve.wait_ge(kept, b + 1)
                    dve.wait_ge(hT_done, b + 1)
                    nc.vector.tensor_tensor(h_new[:, b % 2], bank[2 + b % 2][:, 0:H], b_in_sb[:], ALU.add
                                            ).then_inc(new_ready, 1)
                    dve.drain()
                    parts_of_block(dve, b, b, b % 2)

                def keys(b, par, n):
                    e = ed[:, par, 0:n, :]
                    nc.vector.tensor_scalar(src_hi[:, 0:n], e[:, :, 0], 3, 0xFFF0, ALU.logical_shift_right,
                                            ALU.bitwise_and)
                    nc.vector.tensor_scalar(dst_lo[:, 0:n], e[:, :, 1], WIN - 1, None, ALU.bitwise_and)
                    nc.vector.tensor_scalar(dst_hi[:, 0:n], e[:, :, 1], 4, None, ALU.logical_shift_right)
                    nc.vector.tensor_scalar(src_lo[:, 0:n], e[:, :, 0], P - 1, None, ALU.bitwise_and)
                    dve.drain()
                    nc.vector.tensor_tensor(col[:, 0:n], src_hi[:, 0:n], dst_lo[:, 0:n], ALU.add)
                    nc.vector.tensor_tensor(valid[:, 0:n], dst_hi[:, 0:n],
                                            gidx[:].rearrange("p g c -> p (g c)")[:, bass.ds(b * SLOTS, n)],
                                            ALU.is_equal)
                    nc.vector.tensor_copy(key_s[:, par, 0:n], src_lo[:, 0:n])
                    dve.drain().then_inc(keys_ready, 1)
                    nc.vector.scalar_tensor_tensor(key_m[:, 0:n], col[:, 0:n], 1.0, valid[:, 0:n], ALU.add, ALU.mult)
                    nc.vector.tensor_reduce(vsum[:], valid[:, 0:n], AX.X, ALU.add)
                    dve.drain()
                    nc.vector.tensor_tensor(vtotal[:], vtotal[:], vsum[:], ALU.add)
                    dve.drain()

                def one_hots(n, gi):
                    dve.wait_ge(win_done, n + 3)
                    for c in range(CH):
                        s = gi * CH + c
                        last = nc.vector.tensor_scalar(oh_m[:, gi % 2, c], iota_m[:], key_m[:, s:s + 1], None,
                                                       ALU.is_equal)
                    last.then_inc(hot_m_ready, 1)

                def reciprocal_degree(k, slot):
                    dve.wait_ge(deg_done, k + 3)
                    nc.vector.tensor_scalar(rdeg[:, bass.ds(k, 1)], bank[4 + slot][:, 0:1], 1.0, None, ALU.max)
                    dve.drain()
                    nc.vector.reciprocal(rdeg[:, bass.ds(k, 1)], rdeg[:, bass.ds(k, 1)]).then_inc(rdeg_ready, 1)

                with dve.Fori(0, BODIES // 2) as i:
                    for par in range(2):
                        dve.wait_ge(ed_in[par], 16 * GBODY * (i + 1))
                        keys(2 * i + par, par, SLOTS)
                        for gi in range(GBODY):
                            one_hots((2 * i + par) * GBODY + gi, gi)
                            if gi == GP + 2:
                                reciprocal_degree(4 * i + 2 * par, 0)
                        reciprocal_degree(4 * i + 2 * par + 1, 1)
                dve.wait_ge(ed_in[0], 16 * (GBODY * (BODIES // 2) + LASTG))
                keys(BODIES, 0, LASTG * CH)
                for gi in range(LASTG):
                    one_hots(BODIES * GBODY + gi, gi)
                reciprocal_degree(NB - 1, 0)
                dve.drain().then_inc(vtotal_ready, 1)
                dve.wait_ge(vsum_done, 1)
                nc.vector.tensor_scalar(slow_flag[:], bank[6][0:1, 0:1], float(E), None, ALU.not_equal
                                        ).then_inc(flag_ready, 1)

            @block.tensor
            def _(pe):
                pe.sem_inc(win_done, 4)
                pe.sem_inc(proj_done, 2)
                pe.sem_inc(hT_done, 2)
                pe.sem_inc(hl_done, 2)
                pe.sem_inc(deg_done, 2)
                pe.wait_ge(s_const, 1)
                pe.wait_ge(before_ready, 1)
                for k in range(2):
                    last = nc.tensor.matmul(bank[3][:, k:k + 1], before[:, k * P:(k + 1) * P], ones1[:],
                                            start=True, stop=True)
                last.then_inc(full_done, 1)

                def transpose_x(b):
                    pe.wait_ge(y_ready, b + 1)
                    pe.wait_ge(h0_ready, b + 1)
                    nc.tensor.transpose(bank[b % 2][:, 0:P], x_all[:, b, :], identf[:]).then_inc(yT_done, 1)

                def project(b):
                    pe.wait_ge(h0_ready, b + 3)
                    if b >= 2:
                        pe.wait_ge(new_ready, b - 1)
                    elif b == 1:
                        pe.wait_ge(idx_ready, 1)
                    nc.tensor.matmul(bank[2 + b % 2][:, 0:H], h0[:, b % 2], w_in_sb[:], start=True, stop=True
                                     ).then_inc(proj_done, 1)

                pe.wait_ge(s_wait, 64)
                transpose_x(0)
                project(0)
                for b in range(NB):
                    if b + 1 < NB:
                        transpose_x(b + 1)
                        project(b + 1)
                    transpose_block(pe, b, b % 2)
                    logits_of_block(pe, b, b % 2, 0)
                pe.wait_ge(hl_kept, NB + 2)
                pe.wait_ge(new_ready, NB)

                def window(n, gi):
                    pe.wait_ge(hot_s_ready, n + 1)
                    pe.wait_ge(hot_m_ready, n + 1)
                    pe.wait_ge(win_evac, n + 1)
                    for c in range(CH):
                        last = nc.tensor.matmul(bank[gi % 4][:, 0:MW], oh_s[:, gi % 4, c], oh_m[:, gi % 2, c],
                                                start=(c == 0), stop=(c == CH - 1))
                    last.then_inc(win_done, 1)

                def degrees(k, slot, n):
                    pe.wait_ge(rdeg_ready, k + 1)
                    pe.wait_ge(win_evac, n + 4)
                    for s in range(NB):
                        last = nc.tensor.matmul(bank[4 + slot][:, 0:1], piece[:, slot, s, :], onesb[:, 0:1],
                                                start=(s == 0), stop=(s == NB - 1))
                    last.then_inc(deg_done, 1)

                with pe.Fori(0, BODIES) as i:
                    for k in range(2):
                        for gi in range(GP):
                            window((2 * i + k) * GP + gi, gi)
                        degrees(2 * i + k, k, (2 * i + k + 1) * GP)
                for gi in range(LASTG):
                    window(2 * BODIES * GP + gi, gi)
                degrees(NB - 1, 0, GROUPS)
                pe.wait_ge(vtotal_ready, 1)
                nc.tensor.matmul(bank[6][0:1, 0:1], vtotal[:], ones1[:], start=True, stop=True).then_inc(vsum_done, 1)


        with ExitStack() as cg:
            NCH = ROWLEN
            ROUND = 2048
            BANKS = -(-NB * P // 512)
            g_ed = sb("g_ed", [ROWS, NCH, 2], I32, cg)
            g_a = sb("g_a", [ROWS, NCH], I32, cg)
            g_b = sb("g_b", [ROWS, NCH], I32, cg)
            g_c = sb("g_c", [ROWS, NCH], I32, cg)
            g_src = sb("g_src", [ROWS, NCH], F32, cg)
            g_blk = sb("g_blk", [ROWS, NCH], F32, cg)
            g_dlo = sb("g_dlo", [ROWS, NCH], F32, cg)
            g_col = sb("g_col", [ROWS, NCH], F32, cg)
            g_now = sb("g_now", [P, 1], F32, cg)
            g_key = sb("g_key", [ROWS, NCH], F32, cg)
            g_dkey = sb("g_dkey", [ROWS, NCH], F32, cg)
            g_iota = sb("g_iota", [P, NB * P], F32, cg)
            g_hot_s = sb("g_hot_s", [ROWS, P], BF16, cg)
            g_hot_d = sb("g_hot_d", [ROWS, P], BF16, cg)
            g_hot_m = sb("g_hot_m", [ROWS, NB * P], BF16, cg)
            g_count = sb("g_count", [P, 512], I32, cg)
            g_part = sb("g_part", [P, 512], I32, cg)
            g_low = sb("g_low", [P, NB * P], F16, cg)
            g_up = sb("g_up", [P, NB * P], BF16, cg)
            g_zero = sb("g_zero", [P, 512], BF16, cg)
            g_const = sem("g_const")
            g_in = sem("g_in")
            g_cleared = sem("g_cleared")
            g_hot = sem("g_hot")
            g_mult = sem("g_mult")
            g_sum = sem("g_sum")
            g_taken = sem("g_taken")
            g_low_out = sem("g_low_out")
            g_up_out = sem("g_up_out")
            g_free = sem("g_free")

            block = cg.enter_context(nc.Block())

            @block.sync
            def _(sp):
                slow = sp.value_load(slow_flag[0:1, 0:1], min_val=0, max_val=1)
                with sp.If(slow == 0):
                    sp.nop()
                with sp.Else():
                    sp.dma_start(g_ed[:], edges.rearrange("(p k) two -> p k two", p=ROWS)).then_inc(g_in, 16)
                    sp.sem_inc(g_free, 1)
                    with sp.Fori(0, NB) as b:
                        hold(sp, g_taken, b + 2)
                        sp.dma_start(at_dram[bass.ds(b, 1)].rearrange("o p c -> p (o c)"), g_low[:]).then_inc(g_low_out, 16)
                        sp.dma_start(at_upper_dram[bass.ds(b, 1)].rearrange("o p c -> p (o c)"), g_up[:]
                                     ).then_inc(g_up_out, 16)
                        hold(sp, g_low_out, 16 * (b + 1))
                        hold(sp, g_up_out, 16 * (b + 1))
                        sp.sem_inc(g_free, 1)
                sp.nop()

            @block.gpsimd
            def _(pool):
                slow = pool.value_load(slow_flag[0:1, 0:1], min_val=0, max_val=1)
                with pool.If(slow == 0):
                    pool.nop()
                with pool.Else():
                    nc.gpsimd.iota(g_iota[:], pattern=[[1, NB * P]], base=1, channel_multiplier=0,
                                   allow_small_or_imprecise_dtypes=True)
                    nc.gpsimd.memset(g_now[:], 0.0)
                    nc.gpsimd.memset(g_zero[:], 0.0)
                    pool.drain().then_inc(g_const, 1)
                pool.nop()

            @block.vector
            def _(dve):
                slow = dve.value_load(slow_flag[0:1, 0:1], min_val=0, max_val=1)
                with dve.If(slow == 0):
                    dve.nop()
                with dve.Else():
                    dve.sem_inc(g_taken, 1)
                    dve.wait_ge(g_const, 1)
                    dve.wait_ge(g_in, 16)
                    src, to = g_ed[:, :, 0], g_ed[:, :, 1]
                    nc.vector.tensor_scalar(g_a[:], src, P - 1, None, ALU.bitwise_and)
                    nc.vector.tensor_scalar(g_b[:], to, P - 1, None, ALU.bitwise_and)
                    nc.vector.tensor_scalar(g_c[:], to, 7, None, ALU.logical_shift_right)
                    dve.drain()
                    nc.vector.tensor_scalar(g_src[:], g_a[:], 1.0, None, ALU.add)
                    nc.vector.tensor_scalar(g_dlo[:], g_b[:], 1.0, None, ALU.add)
                    nc.vector.tensor_copy(g_blk[:], g_c[:])
                    dve.drain()
                    nc.vector.tensor_tensor(g_a[:], src, g_a[:], ALU.subtract)
                    dve.drain()
                    nc.vector.tensor_tensor(g_col[:], g_a[:], g_dlo[:], ALU.add)
                    dve.drain()
                    with dve.Fori(0, NB) as b:
                        nc.vector.scalar_tensor_tensor(g_key[:], g_blk[:], g_now[0:ROWS, 0:1], g_col[:], ALU.is_equal, ALU.mult)
                        nc.vector.scalar_tensor_tensor(g_dkey[:], g_blk[:], g_now[0:ROWS, 0:1], g_dlo[:], ALU.is_equal, ALU.mult)
                        dve.drain()
                        with dve.Fori(0, NCH) as c:
                            hold(dve, g_mult, NCH * b + c + 1)
                            nc.vector.tensor_scalar(g_hot_s[:], g_iota[0:ROWS, 0:P], g_src[:, bass.ds(c, 1)], None, ALU.is_equal)
                            nc.vector.tensor_scalar(g_hot_d[:], g_iota[0:ROWS, 0:P], g_dkey[:, bass.ds(c, 1)], None, ALU.is_equal)
                            nc.vector.tensor_scalar(g_hot_m[:], g_iota[0:ROWS, :], g_key[:, bass.ds(c, 1)], None, ALU.is_equal)
                            dve.drain().then_inc(g_hot, 1)
                        hold(dve, g_sum, b + 1)
                        hold(dve, g_free, b + 1)
                        for j in range(BANKS):
                            w = min(512, NB * P - 512 * j)
                            part = slice(512 * j, 512 * j + w)
                            nc.vector.tensor_copy(g_count[:, 0:w], bank[j][:, 0:w])
                            dve.drain()
                            nc.vector.tensor_scalar(g_part[:, 0:w], g_count[:, 0:w], ROUND - 1, None, ALU.bitwise_and)
                            dve.drain()
                            nc.vector.tensor_copy(g_low[:, part], g_part[:, 0:w])
                            nc.vector.tensor_tensor(g_up[:, part], g_count[:, 0:w], g_part[:, 0:w], ALU.subtract)
                            dve.drain()
                        nc.vector.tensor_scalar(rdeg[:, bass.ds(b, 1)], bank[7][:, 0:1], 1.0, None, ALU.max)
                        nc.vector.tensor_scalar(g_now[:], g_now[:], 1.0, None, ALU.add)
                        dve.drain()
                        nc.vector.reciprocal(rdeg[:, bass.ds(b, 1)], rdeg[:, bass.ds(b, 1)])
                        dve.drain().then_inc(g_taken, 1)
                dve.nop()

            @block.tensor
            def _(pe):
                slow = pe.value_load(slow_flag[0:1, 0:1], min_val=0, max_val=1)
                with pe.If(slow == 0):
                    pe.nop()
                with pe.Else():
                    pe.sem_inc(g_mult, 1)
                    hold(pe, g_const, 1)

                    def edge_of_block(start):
                        for j in range(BANKS + 1):
                            w = 1 if j == BANKS else min(512, NB * P - 512 * j)
                            last = nc.tensor.matmul(bank[j][:, 0:w], onesb[:], g_zero[:, 0:w], start=start,
                                                    stop=not start, skip_group_check=True)
                        return last

                    with pe.Fori(0, NB) as b:
                        hold(pe, g_taken, b + 1)
                        edge_of_block(True)
                        with pe.Fori(0, NCH) as c:
                            hold(pe, g_hot, NCH * b + c + 1)
                            for j in range(BANKS):
                                w = min(512, NB * P - 512 * j)
                                nc.tensor.matmul(bank[j][:, 0:w], g_hot_s[:], g_hot_m[:, 512 * j:512 * j + w],
                                                 start=False, stop=False, skip_group_check=True)
                            nc.tensor.matmul(bank[BANKS][:, 0:1], g_hot_d[:], onesb[0:ROWS, 0:1], start=False, stop=False,
                                             skip_group_check=True).then_inc(g_mult, 1)
                        edge_of_block(False).then_inc(g_sum, 1)
                pe.nop()

        phase_end = sem("phase_end")
        g_all = sb("g_all", [P, NB, 2], F32)
        slots_all = sb("slots_all", [P, 2 * NB], U32)
        slot_get = sb("slot_get", [P, 2, 2], U32)
        y_got = sb("y_got", [P, 2, 2, H], F32)
        h_part = sb("h_part", [P, 2, H], F32)
        got = [sem("got0"), sem("got1")]
        FIRST, SECOND = TRIPS + 1, TRIPS

        def join(eng, n):
            eng.drain().then_inc(phase_end, 1)
            hold(eng, phase_end, 5 * n)

        def collect(pool, l, b, u, uses, rows=P):
            hold(pool, new_ready, NB * (l + 1) + b - 1)
            nc.gpsimd.tensor_copy(slot_get[:, u], slots_all[:, bass.ds(2 * b, 2)])
            pool.drain()
            for k in range(2):
                nc.gpsimd.indirect_dma_start(
                    out=y_got[0:rows, u, k], out_offset=None, in_=slot_y[:],
                    in_offset=bass.IndirectOffsetOnAxis(ap=slot_get[0:rows, u, k:k + 1], axis=0),
                    bounds_check=XROWS - 1, oob_is_err=False).then_inc(got[u], 16)

        def combine(dve, l, b, u, uses, rows=P):
            n = NB * (l + 1) + b
            R = slice(0, rows)
            hold(dve, got[u], 32 * (uses + 1))
            hold(dve, kept, n + 1)
            hold(dve, hT_done, n + 1)
            nc.vector.scalar_tensor_tensor(h_part[R, u], y_got[R, u, 0], g_all[R, bass.ds(b, 1), 0],
                                           h_all[R, bass.ds(b, 1)].rearrange("p o f -> p (o f)"), ALU.mult, ALU.add)
            dve.drain()
            nc.vector.scalar_tensor_tensor(h_new[R, u], y_got[R, u, 1], g_all[R, bass.ds(b, 1), 1], h_part[R, u],
                                           ALU.mult, ALU.add).then_inc(new_ready, 1)

        def in_pairs(eng, step):
            with eng.Fori(0, TRIPS) as i:
                for u in range(2):
                    step(2 * i + u, u, i)
            step(NB - 1, 0, TRIPS)

        with ExitStack() as c2:
            def sb2(name, shape, dt):
                return sb(name, shape, dt, c2)

            at_in_sb = sb2("at_in_sb", [P, 2, NB, P], F16)
            w_hi = sb2("w_hi", [P, WQ, 512], F32R)
            w_lo = sb2("w_lo", [P, WQ, 512], F32R)
            stage = sb2("stage", [P, 2, 512], F32)
            bias = sb2("bias", [P, NE, H], F32)
            b1_sb = sb2("b1_sb", [P, NSTRONG * KF], F32)
            agg = sb2("agg", [P, 2, H], F32)
            aT = sb2("aT", [P, 2, KH, P], F32)
            lg = sb2("lg", [P, NE1], F32)
            top = sb2("top", [P, 8], F32)
            idx = sb2("idx", [P, 8], U32)
            idx_f = sb2("idx_f", [P, 2], F32)
            dz = sb2("dz", [P, 2], F32)
            ex = sb2("ex", [P, 2], F32)
            den = sb2("den", [P, 2], F32)
            rec = sb2("rec", [P, 2], F32)
            gt = sb2("gt", [P, 2], F32)
            hots = sb2("hots", [P, 2, NE], F32)
            member = sb2("member", [P, NE], BF16)
            next_slot = sb2("next_slot", [P, NE], F32)
            pos = sb2("pos", [P, NE], F32)
            prod = sb2("prod", [P, 2, NE], F32)
            slot_f = sb2("slot_f", [P, 2], F32)
            slot_now = sb2("slot_now", [P, 2, 2], U32)
            taken = sb2("taken", [1, NE], F32)
            taken_i = sb2("taken_i", [1, NE], I32)
            sums = [sb2(f"sums{i}", [1, 2 * NE], F32) for i in range(2)]
            tiles_before = sb2("tiles_before", [1, 1], F32)
            strong_shift = sb2("strong_shift", [1, 1], F32)
            plan_f = sb2("plan_f", [1, 3 * NE], F32)
            plan = sb2("plan", [1, 3 * NE], I32)
            x_rows = sb2("x_rows", [P, 2, H], F32)
            x_hi = sb2("x_hi", [P, KH, TOK], F32R)
            x_lo = sb2("x_lo", [P, KH, TOK], F32R)
            v = sb2("v", [P, 2, TOK], F32)
            act_hi = sb2("act_hi", [P, KF, TOK], F32R)
            act_lo = sb2("act_lo", [P, KF, TOK], F32R)
            y_sb = sb2("y_sb", [P, 2, H], F32)

            zeroed = sem("zeroed")
            at_in = [sem("at_in0"), sem("at_in1")]
            at_used = [sem("at_used0"), sem("at_used1")]
            low_in, up_in = sem("low_in"), sem("up_in")
            low_used, up_used = sem("low_used"), sem("up_used")
            small_in = sem("small_in")
            w_in_ = [sem("w_in0"), sem("w_in1")]
            w_hi_done = sem("w_hi_done")
            w_split = sem("w_split")
            agg_done = sem("agg_done")
            agg_ready = sem("agg_ready")
            agg_free = sem("agg_free")
            aT_done = sem("aT_done")
            aT_ready = sem("aT_ready")
            lg_done = sem("lg_done")
            lg_taken = sem("lg_taken")
            dz_ready = sem("dz_ready")
            ex_ready = sem("ex_ready")
            member_ready = sem("member_ready")
            rank_done = sem("rank_done")
            slot_ready = sem("slot_ready")
            scattered = sem("scattered")
            x_in2 = sem("x_in2")
            xT_done = sem("xT_done")
            xh_ready = sem("xh_ready")
            xl_ready = sem("xl_ready")
            unit_done = sem("unit_done")
            hi_ready = sem("hi_ready")
            lo_ready = sem("lo_ready")
            y_done = sem("y_done")
            y_ready = sem("y_ready2")
            y_out = [sem("y_out0"), sem("y_out1")]

            unit_bank = (1, 2, 5, 6)

            block = c2.enter_context(nc.Block())

            def each_expert(eng, tile, last=None):
                for e in range(NE):
                    count = eng.value_load(plan[0:1, e:e + 1], min_val=1, max_val=REGION // TOK)
                    base = eng.value_load(plan[0:1, NE + e:NE + e + 1], min_val=0, max_val=LAYERS * XROWS // TOK)
                    sbase = 0
                    if e >= NWEAK:
                        sbase = eng.value_load(plan[0:1, 2 * NE + e:2 * NE + e + 1], min_val=0,
                                               max_val=LAYERS * XROWS // TOK)
                    with eng.Fori(0, count) as t:
                        tile(e, t, base + t, sbase + t)
                if last is not None:
                    last(base + count)

            def first_tile(eng):
                return eng.value_load(plan[0:1, NE:NE + 1], min_val=0, max_val=LAYERS * XROWS // TOK)

            def layers(phase_a, phase_b, phase_c, eng):
                with eng.Fori(0, LAYERS - 1) as l:
                    phase_a(l)
                    join(eng, 3 * l + 1)
                    phase_b(l)
                    join(eng, 3 * l + 2)
                    phase_c(l)
                    join(eng, 3 * l + 3)
                phase_a(LAYERS - 1)
                join(eng, 3 * LAYERS - 2)
                phase_b(LAYERS - 1)

            def after_first(eng, step):
                with eng.Fori(0, WQ // 2) as i:
                    for u in range(2):
                        step(i, 2 * i + 1 + u, 1 - u, u)
                with eng.Fori(WQ // 2, TRIPS) as i:
                    for u in range(2):
                        step(i, 2 * i + 1 + u, 1 - u, None)

            @block.sync
            def _(sp):
                slow = sp.value_load(slow_flag[0:1, 0:1], min_val=0, max_val=1)

                def phase_a(l):
                    def weights(i, q):
                        hold(sp, w_split, WQ * l + 2 * i + q + 1)
                        sp.dma_start(stage[:, q], pieces[bass.ds(l, 1), bass.ds(2 * i + q, 1)].rearrange(
                            "o k p f -> p (o k f)")).then_inc(w_in_[q], 16)

                    def load(b, u, uses):
                        hold(sp, at_used[u], uses + 1)
                        sp.dma_start(at_in_sb[:, u].rearrange("p s d -> p (s d)"),
                                     at_dram[bass.ds(b, 1)].rearrange("o p c -> p (o c)")).then_inc(at_in[u], 16)

                    def load_both(b):
                        hold(sp, low_used, NB * l + b + 1)
                        sp.dma_start(at_in_sb[:, 0].rearrange("p s d -> p (s d)"),
                                     at_dram[bass.ds(b, 1)].rearrange("o p c -> p (o c)")).then_inc(low_in, 16)
                        hold(sp, up_used, NB * l + b + 1)
                        sp.dma_start(at_in_sb[:, 1].rearrange("p s d -> p (s d)").bitcast(BF16),
                                     at_upper_dram[bass.ds(b, 1)].rearrange("o p c -> p (o c)")).then_inc(up_in, 16)

                    def steps(fetch):
                        fetch(0, 0, FIRST * l)

                        def step(i, b, u, q):
                            fetch(b, u, SECOND * l + i if u else FIRST * l + i + 1)
                            if q is not None:
                                weights(i, q)
                        after_first(sp, step)

                    with sp.If(slow == 0):
                        steps(load)
                    with sp.Else():
                        steps(lambda b, u, uses: load_both(b))
                    sp.nop()

                def phase_b(l):
                    def rows(X, first):
                        hold(sp, xT_done, X + 1)
                        sp.dma_start(x_rows[:], slot_x[bass.ds(first, TOK), :].rearrange("(s p) f -> p s f", p=P)
                                     ).then_inc(x_in2, 16)

                    each_expert(sp, lambda e, t, G, S: rows(G + l, t * TOK + REGION * e),
                                lambda G: rows(G + l, XROWS - TOK))

                layers(phase_a, phase_b, lambda l: None, sp)

            @block.gpsimd
            def _(pool):
                pool.sem_inc(agg_free, 2)
                nc.gpsimd.memset(y_sb[:], 0.0)
                for t in (sums[0], sums[1], tiles_before, strong_shift, plan_f):
                    nc.gpsimd.memset(t[:], 0.0)
                pool.drain().then_inc(zeroed, 1)
                for s in range(2):
                    nc.gpsimd.dma_start(slot_y[XROWS - TOK + s * P:XROWS - TOK + (s + 1) * P, :], y_sb[:, s]
                                        ).then_inc(y_out[s], 16)

                def phase_a(l):
                    nc.gpsimd.dma_start(bias[:, 0:NWEAK, :], weak_b[bass.ds(l, 1)].to_broadcast([P, NWEAK, H])
                                        ).then_inc(small_in, 16)
                    nc.gpsimd.dma_start(bias[:, NWEAK:NE, :], b2[bass.ds(l, 1)].to_broadcast([P, NSTRONG, H])
                                        ).then_inc(small_in, 16)
                    nc.gpsimd.dma_start(b1_sb[:], b1[bass.ds(l, 1)].rearrange("o p u -> p (o u)")).then_inc(small_in, 16)

                    def scatter(b, u, uses, rows=P):
                        n = NB * l + b
                        hold(pool, slot_ready, n + 1)
                        for k in range(2):
                            nc.gpsimd.indirect_dma_start(
                                out=slot_x[:], out_offset=bass.IndirectOffsetOnAxis(ap=slot_now[0:rows, u, k:k + 1], axis=0),
                                in_=agg[0:rows, u], in_offset=None, bounds_check=XROWS - 1, oob_is_err=False
                                ).then_inc(scattered, 16)
                        hold(pool, scattered, 32 * (n + 1))
                        pool.sem_inc(agg_free, 1)

                    with pool.Fori(0, TRIPS) as i:
                        for u in range(2):
                            scatter(2 * i + u, u, i)
                    scatter(NB - 1, 0, TRIPS, LROWS)

                def phase_b(l):
                    def store(e, t, G, S):
                        for s in range(2):
                            hold(pool, y_ready, 2 * G + s + 3)
                            nc.gpsimd.dma_start(slot_y[bass.ds(t * TOK + (REGION * e + s * P), P), :], y_sb[:, s]
                                                ).then_inc(y_out[s], 16)

                    def stored(G):
                        for s in range(2):
                            hold(pool, y_out[s], 16 * (G + 1))
                    each_expert(pool, store, stored)

                def phase_c(l):
                    with pool.Fori(0, TRIPS) as i:
                        for u in range(2):
                            collect(pool, l, 2 * i + u, u, i)
                    collect(pool, l, NB - 1, 0, TRIPS, LROWS)

                layers(phase_a, phase_b, phase_c, pool)

            @block.scalar
            def _(act):
                act.sem_inc(aT_ready, 2)
                act.sem_inc(hi_ready, KF)

                def phase_a(l):
                    def weights(i, q):
                        hold(act, w_in_[q], 16 * (WQ // 2 * l + i + 1))
                        nc.scalar.activation(w_hi[:, bass.ds(2 * i + q, 1)].rearrange("p o f -> p (o f)"), stage[:, q],
                                             ACT.Copy).then_inc(w_hi_done, 1)

                    def route(b, u):
                        n = NB * l + b
                        act.wait_ge(aT_done, n + 1)
                        nc.scalar.activation(aT[:, u].rearrange("p k n -> p (k n)"), bank[2 + u][:, 0:H], ACT.Copy
                                             ).then_inc(aT_ready, 1)
                        act.wait_ge(dz_ready, n + 1)
                        nc.scalar.activation(ex[:], dz[:], ACT.Exp).then_inc(ex_ready, 1)

                    def step(i, b, u, q):
                        if q is not None:
                            weights(i, q)
                        route(b - 1, 1 - u)
                    after_first(act, step)
                    route(NB - 1, 0)

                def phase_b(l):
                    def upper(X):
                        act.wait_ge(xT_done, X + 2)
                        nc.scalar.activation(x_hi[:].rearrange("p k n -> p (k n)"), bank[0][:], ACT.Copy
                                             ).then_inc(xh_ready, 1)

                    def tile(e, t, G, S):
                        X = G + l
                        if e < NWEAK:
                            hold(act, y_done, 2 * G + 2)
                        else:
                            for f in range(KF):
                                hold(act, unit_done, KF * S + f + 1)
                                act.wait_ge(lo_ready, KF * S + f + 1)
                                src = bank[unit_bank[f]][:, 0:TOK]
                                col = (e - NWEAK) * KF + f
                                nc.scalar.activation(v[:, f % 2], src, ACT.Relu, bias=b1_sb[:, col:col + 1])
                                nc.scalar.activation(act_hi[:, f], src, ACT.Relu, bias=b1_sb[:, col:col + 1])
                                act.drain().then_inc(hi_ready, 1)
                        upper(X + 1)

                    hold(act, small_in, 48 * (l + 1))
                    upper(first_tile(act) + l)
                    each_expert(act, tile)

                def phase_c(l):
                    in_pairs(act, lambda b, u, uses: keep_block(act, NB * (l + 1) + b, b, u))

                layers(phase_a, phase_b, phase_c, act)

            @block.vector
            def _(dve):
                dve.sem_inc(w_split, 2)
                dve.sem_inc(agg_ready, 2)
                dve.sem_inc(lg_taken, 1)
                dve.sem_inc(lo_ready, 2)
                dve.sem_inc(y_ready, 2)
                dve.wait_ge(zeroed, 1)

                def phase_a(l):
                    nc.vector.tensor_copy(next_slot[:], region_0[:])
                    dve.drain()

                    def weights(i, q):
                        hold(dve, w_hi_done, WQ * l + 2 * i + q + 1)
                        at = bass.ds(2 * i + q, 1)
                        nc.vector.tensor_tensor(w_lo[:, at].rearrange("p o f -> p (o f)"), stage[:, q],
                                                w_hi[:, at].rearrange("p o f -> p (o f)"), ALU.subtract).then_inc(w_split, 1)

                    def mean(b, u):
                        n = NB * l + b
                        hold(dve, agg_done, n + 1)
                        hold(dve, agg_free, n + 1)
                        nc.vector.tensor_scalar(agg[:, u], bank[u][:, 0:H], rdeg[:, bass.ds(b, 1)], None, ALU.mult
                                                ).then_inc(agg_ready, 1)

                    def choose(b, last=False):
                        n = NB * l + b
                        dve.wait_ge(lg_done, n + 1)
                        nc.vector.tensor_tensor(lg[:], bank[4][:, 0:NE1],
                                                h_logits[:, bass.ds(b, 1)].rearrange("p o e -> p (o e)"), ALU.add
                                                ).then_inc(lg_taken, 1)
                        dve.drain()
                        nc.vector.max(top[:], lg[:, 0:NE])
                        nc.vector.tensor_scalar(dz[:, 1:2], lg[:, NE:NE1], -1.0, None, ALU.mult)
                        dve.drain()
                        nc.vector.max_index(idx[:], top[:], lg[:, 0:NE])
                        nc.vector.tensor_tensor(dz[:, 0:1], top[:, 1:2], top[:, 0:1], ALU.subtract)
                        dve.drain().then_inc(dz_ready, 1)
                        nc.vector.tensor_copy(idx_f[:], idx[:, 0:2])
                        dve.drain()
                        nc.vector.tensor_tensor(hots[:], expert_no[:].unsqueeze(1).to_broadcast([P, 2, NE]),
                                                idx_f[:].unsqueeze(2).to_broadcast([P, 2, NE]), ALU.is_equal)
                        if last:
                            nc.vector.memset(member[:], 0.0)
                        dve.drain()
                        R = slice(0, LROWS if last else P)
                        nc.vector.tensor_tensor(member[R], hots[R, 0], hots[R, 1], ALU.add).then_inc(member_ready, 1)

                    def place(b, u):
                        n = NB * l + b
                        hold(dve, ex_ready, n + 1)
                        nc.vector.tensor_scalar(den[:], ex[:], 1.0, None, ALU.add)
                        dve.drain()
                        nc.vector.reciprocal(rec[:], den[:])
                        dve.drain()
                        nc.vector.tensor_tensor(gt[:, 0:1], rec[:, 0:1], rec[:, 1:2], ALU.mult)
                        hold(dve, rank_done, n + 1)
                        nc.vector.tensor_tensor(pos[:], bank[5][:, 0:NE], next_slot[:], ALU.add)
                        dve.drain()
                        nc.vector.tensor_tensor(gt[:, 1:2], gt[:, 0:1], ex[:, 0:1], ALU.mult)
                        nc.vector.tensor_tensor(prod[:], hots[:], pos[:].unsqueeze(1).to_broadcast([P, 2, NE]), ALU.mult)
                        nc.vector.tensor_tensor(next_slot[:], bank[5][:, NE:2 * NE], next_slot[:], ALU.add)
                        dve.drain()
                        nc.vector.tensor_reduce(slot_f[:], prod[:], AX.X, ALU.add)
                        nc.vector.tensor_copy(g_all[:, bass.ds(b, 1)].rearrange("p o k -> p (o k)"), gt[:])
                        dve.drain()
                        nc.vector.tensor_copy(slot_now[:, u], slot_f[:])
                        nc.vector.tensor_copy(slots_all[:, bass.ds(2 * b, 2)], slot_f[:])
                        dve.drain().then_inc(slot_ready, 1)

                    def step(i, b, u, q):
                        choose(b - 1)
                        if q is not None:
                            weights(i, q)
                        place(b - 1, 1 - u)
                        mean(b, u)

                    mean(0, 0)
                    after_first(dve, step)
                    choose(NB - 1, last=True)
                    place(NB - 1, 0)

                    nc.vector.tensor_tensor(taken[:], next_slot[0:1], region_0[0:1], ALU.subtract)
                    dve.drain()
                    nc.vector.tensor_scalar(taken_i[:], taken[:], float(TOK - 1), None, ALU.add)
                    dve.drain()
                    nc.vector.tensor_scalar(taken_i[:], taken_i[:], TOK.bit_length() - 1, None, ALU.logical_shift_right)
                    dve.drain()
                    nc.vector.tensor_scalar(plan_f[:, 0:NE], taken_i[:], 1.0, None, ALU.max)
                    dve.drain()
                    nc.vector.tensor_copy(sums[0][:, NE:2 * NE], plan_f[:, 0:NE])
                    dve.drain()
                    for k, shift in enumerate((1, 2, 4)):
                        a, b = sums[k % 2], sums[(k + 1) % 2]
                        nc.vector.tensor_tensor(b[:, NE:2 * NE], a[:, NE:2 * NE], a[:, NE - shift:2 * NE - shift], ALU.add)
                        dve.drain()
                    s = sums[1]
                    nc.vector.tensor_scalar(plan_f[:, NE:2 * NE], s[:, NE - 1:2 * NE - 1], tiles_before[:, 0:1], None, ALU.add)
                    nc.vector.tensor_tensor(strong_shift[:], strong_shift[:], s[:, NE + NWEAK - 1:NE + NWEAK], ALU.add)
                    dve.drain()
                    nc.vector.tensor_scalar(plan_f[:, 2 * NE + NWEAK:3 * NE], plan_f[:, NE + NWEAK:2 * NE],
                                            strong_shift[:, 0:1], None, ALU.subtract)
                    nc.vector.tensor_tensor(tiles_before[:], tiles_before[:], s[:, 2 * NE - 1:2 * NE], ALU.add)
                    dve.drain()
                    nc.vector.tensor_copy(plan[:], plan_f[:])

                def phase_b(l):
                    def lower(X):
                        hold(dve, xh_ready, X + 1)
                        nc.vector.tensor_tensor(x_lo[:].rearrange("p k n -> p (k n)"), bank[0][:],
                                                x_hi[:].rearrange("p k n -> p (k n)"), ALU.subtract).then_inc(xl_ready, 1)

                    def results(e, G):
                        for s in range(2):
                            hold(dve, y_out[s], 16 * (G + 1))
                            hold(dve, y_done, 2 * G + s + 1)
                            i = nc.vector.tensor_tensor(y_sb[:, s], bank[3 + s][:, 0:H], bias[:, e], ALU.add)
                            if e < NWEAK:
                                dve.drain()
                                i = nc.vector.tensor_scalar(y_sb[:, s], y_sb[:, s], 0.0, None, ALU.max)
                            i.then_inc(y_ready, 1)

                    def tile(e, t, G, S):
                        if e >= NWEAK:
                            for f in range(KF):
                                hold(dve, hi_ready, KF * S + f + KF + 1)
                                nc.vector.tensor_tensor(act_lo[:, f], v[:, f % 2], act_hi[:, f], ALU.subtract
                                                        ).then_inc(lo_ready, 1)
                        lower(G + l + 1)
                        results(e, G)

                    hold(dve, small_in, 48 * (l + 1))
                    lower(first_tile(dve) + l)
                    each_expert(dve, tile)

                def phase_c(l):
                    def step(b, u, uses, rows=P):
                        combine(dve, l, b, u, uses + (SECOND if u else FIRST) * l, rows)
                        dve.drain()
                        parts_of_block(dve, NB * (l + 1) + b, b, u)
                    with dve.Fori(0, TRIPS) as i:
                        for u in range(2):
                            step(2 * i + u, u, i)
                    step(NB - 1, 0, TRIPS, LROWS)

                layers(phase_a, phase_b, phase_c, dve)

            @block.tensor
            def _(pe):
                slow = pe.value_load(slow_flag[0:1, 0:1], min_val=0, max_val=1)
                pe.sem_inc(at_used[0], 1)
                pe.sem_inc(at_used[1], 1)
                pe.sem_inc(low_used, 1)
                pe.sem_inc(up_used, 1)
                pe.sem_inc(xT_done, 1)

                def phase_a(l):
                    def transpose_mean(b, u):
                        n = NB * l + b
                        pe.wait_ge(agg_ready, n + 3)
                        hold(pe, aT_ready, n + 1)
                        for k in range(KH):
                            last = nc.tensor.transpose(bank[2 + u][:, k * P:(k + 1) * P], agg[:, u, k * P:(k + 1) * P],
                                                       identf[:])
                        last.then_inc(aT_done, 1)

                    def logits(b, u):
                        n = NB * l + b
                        hold(pe, aT_ready, n + 3)
                        hold(pe, lg_taken, n + 1)
                        for k in range(KH):
                            last = nc.tensor.matmul(bank[4][:, 0:NE1], aT[:, u, k, :],
                                                    route_sb[:, bass.ds(l, 1), KH + k, :].rearrange("p o e -> p (o e)"),
                                                    start=(k == 0), stop=(k == KH - 1))
                        last.then_inc(lg_done, 1)

                    def ranks(b):
                        hold(pe, member_ready, NB * l + b + 1)
                        nc.tensor.matmul(bank[5][:, 0:NE], before_b[:], member[:], start=True, stop=True)
                        nc.tensor.matmul(bank[5][:, NE:2 * NE], onesb[:], member[:], start=True, stop=True
                                         ).then_inc(rank_done, 1)

                    def aggregate(b, u, uses, both, previous):
                        n = NB * l + b
                        pe.wait_ge(agg_ready, n + 1)
                        for a in range(2 if both else 1):
                            if not both:
                                arrived, use, used, tile = at_in[u], uses, at_used[u], at_in_sb[:, u]
                            elif a == 0:
                                arrived, use, used, tile = low_in, n, low_used, at_in_sb[:, 0]
                            else:
                                arrived, use, used = up_in, n, up_used
                                tile = at_in_sb[:, 1].rearrange("p s d -> p (s d)").bitcast(BF16).rearrange(
                                    "p (s d) -> p s d", d=P)
                            hold(pe, arrived, 16 * (use + 1))
                            for s in range(NB):
                                for k in range(3):
                                    last = nc.tensor.matmul(bank[u][:, 0:H], tile[:, s, :], hparts[:, s, k, :],
                                                            start=(a + s + k == 0),
                                                            stop=(a == int(both) and s == NB - 1 and k == 2))
                                if previous and a == 0:
                                    if s == 6:
                                        transpose_mean(b - 1, 1 - u)
                                    elif s == 9:
                                        logits(b - 1, 1 - u)
                                    elif s == 21:
                                        ranks(b - 1)
                            last.then_inc(used, 1)
                        pe.drain().then_inc(agg_done, 1)

                    def blocks(both):
                        aggregate(0, 0, FIRST * l, both, False)
                        with pe.Fori(0, TRIPS) as i:
                            aggregate(2 * i + 1, 1, SECOND * l + i, both, True)
                            aggregate(2 * i + 2, 0, FIRST * l + i + 1, both, True)

                    with pe.If(slow == 0):
                        blocks(False)
                    with pe.Else():
                        blocks(True)
                    pe.nop()
                    transpose_mean(NB - 1, 0)
                    logits(NB - 1, 0)
                    ranks(NB - 1)

                def phase_b(l):
                    def transposes(X):
                        hold(pe, x_in2, 16 * (X + 1))
                        for k in range(KH):
                            for s in range(2):
                                last = nc.tensor.transpose(bank[0][:, k * TOK + s * P:k * TOK + (s + 1) * P],
                                                           x_rows[:, s, k * P:(k + 1) * P], identf[:])
                        last.then_inc(xT_done, 1)

                    def tile(e, t, G, S):
                        X = G + l
                        pe.wait_ge(xl_ready, X + 1)
                        if e < NWEAK:
                            transposes(X + 1)
                            for s in range(2):
                                hold(pe, y_ready, 2 * G + s + 1)
                                terms = [(a, w, k) for k in range(KH)
                                         for a, w in ((x_hi, w_hi), (x_hi, w_lo), (x_lo, w_hi))]
                                for j, (a, w, k) in enumerate(terms):
                                    last = nc.tensor.matmul(bank[3 + s][:, 0:H], a[:, k, s * P:(s + 1) * P],
                                                            w[:, e, k * H:(k + 1) * H], start=(j == 0), stop=(j == 5))
                                last.then_inc(y_done, 1)
                            return
                        for f in range(KF):
                            hold(pe, hi_ready, KF * S + f + 1)
                            terms = [(w, a, k) for k in range(KH)
                                     for w, a in ((w_hi, x_hi), (w_hi, x_lo), (w_lo, x_hi))]
                            for j, (w, a, k) in enumerate(terms):
                                last = nc.tensor.matmul(bank[unit_bank[f]][:, 0:TOK],
                                                        w[:, NWEAK + KH * (e - NWEAK) + k, f * P:(f + 1) * P],
                                                        a[:, k, :], start=(j == 0), stop=(j == 5))
                            last.then_inc(unit_done, 1)
                        transposes(X + 1)
                        for s in range(2):
                            hold(pe, y_ready, 2 * G + s + 1)
                            for f in range(KF):
                                if s == 0:
                                    hold(pe, lo_ready, KF * S + f + 3)
                                q = NWEAK + KH * NSTRONG + (e - NWEAK) * (KF // 2) + f // 2
                                cols = slice((f % 2) * H, (f % 2 + 1) * H)
                                for j, (a, w) in enumerate(((act_hi, w_hi), (act_lo, w_hi), (act_hi, w_lo))):
                                    last = nc.tensor.matmul(bank[3 + s][:, 0:H], a[:, f, s * P:(s + 1) * P],
                                                            w[:, q, cols], start=(f + j == 0),
                                                            stop=(f == KF - 1 and j == 2))
                            last.then_inc(y_done, 1)

                    transposes(first_tile(pe) + l)
                    each_expert(pe, tile)

                def phase_c(l):
                    def step(b, u, uses):
                        n = NB * (l + 1) + b
                        transpose_block(pe, n, u)
                        logits_of_block(pe, n, u, l + 1)
                    in_pairs(pe, step)

                layers(phase_a, phase_b, phase_c, pe)

        with ExitStack() as c3:
            L = LAYERS - 1
            x_all = sb("x_out", [P, NB, OUT], F32, c3)
            w_out_sb = sb("w_out_sb", [P, KH, OUT], F32, c3)
            b_out_sb = sb("b_out_sb", [P, OUT], F32, c3)
            o_in = sem("o_in")
            o_done = sem("o_done")
            o_ready = sem("o_ready")
            o_stored = sem("o_stored")
            block = c3.enter_context(nc.Block())
            GROUP = 6
            assert (NB - 1) % GROUP == 0

            @block.sync
            def _(sp):
                sp.dma_start(x_all[:, 0:NB - 1], x[0:(NB - 1) * P, :].rearrange("(b p) f -> p b f", p=P)).then_inc(o_in, 16)
                sp.dma_start(x_all[0:LROWS, NB - 1], x[(NB - 1) * P:N, :]).then_inc(o_in, 16)
                sp.dma_start(w_out_sb[:], w_out).then_inc(o_in, 16)
                sp.dma_start(b_out_sb[:], b_out.rearrange("(o f) -> o f", o=1).to_broadcast([P, OUT])).then_inc(o_in, 16)
                for g in range((NB - 1) // GROUP):
                    sp.wait_ge(o_ready, GROUP * (g + 1) + 2)
                    sp.dma_start(out[g * GROUP * P:(g + 1) * GROUP * P, :].rearrange("(b p) f -> p b f", p=P),
                                 x_all[:, g * GROUP:(g + 1) * GROUP]).then_inc(o_stored, 16)
                sp.wait_ge(o_ready, NB + 2)
                sp.dma_start(out[(NB - 1) * P:N, :], x_all[0:LROWS, NB - 1]).then_inc(o_stored, 16)
                sp.wait_ge(o_stored, 16 * ((NB - 1) // GROUP + 1))

            @block.gpsimd
            def _(pool):
                with pool.Fori(0, TRIPS) as i:
                    for u in range(2):
                        collect(pool, L, 2 * i + u, u, i)
                collect(pool, L, NB - 1, 0, TRIPS, LROWS)

            @block.scalar
            def _(act):
                def keep(b, u, uses):
                    n = NB * LAYERS + b
                    act.wait_ge(hT_done, n + 3)
                    act.wait_ge(o_ready, b + 1)
                    nc.scalar.activation(hT[:, u].rearrange("p k n -> p (k n)"), bank[6 + u][:, 0:H], ACT.Copy
                                         ).then_inc(hT_ready, 1)
                    act.sem_inc(kept, 1)
                in_pairs(act, keep)

            @block.vector
            def _(dve):
                dve.sem_inc(o_ready, 2)
                dve.wait_ge(o_in, 64)
                for b in range(NB):
                    R = slice(0, LROWS if b == NB - 1 else P)
                    nc.vector.tensor_tensor(x_all[R, b], x_all[R, b], b_out_sb[R], ALU.add)
                dve.drain()

                def finish(b, u, rows=P):
                    hold(dve, o_done, b + 1)
                    at = x_all[0:rows, bass.ds(b, 1)].rearrange("p o f -> p (o f)")
                    nc.vector.tensor_tensor(at, at, bank[4 + u][0:rows, 0:OUT], ALU.add).then_inc(o_ready, 1)

                combine(dve, L, 0, 0, FIRST * L)
                with dve.Fori(0, TRIPS - 1) as i:
                    combine(dve, L, 2 * i + 1, 1, SECOND * L + i)
                    finish(2 * i, 0)
                    combine(dve, L, 2 * i + 2, 0, FIRST * L + i + 1)
                    finish(2 * i + 1, 1)
                combine(dve, L, NB - 2, 1, SECOND * L + TRIPS - 1)
                finish(NB - 3, 0)
                combine(dve, L, NB - 1, 0, FIRST * L + TRIPS, LROWS)
                finish(NB - 2, 1)
                finish(NB - 1, 0, LROWS)

            @block.tensor
            def _(pe):
                pe.wait_ge(o_in, 64)

                def project(b, u, uses):
                    n = NB * LAYERS + b
                    transpose_block(pe, n, u)
                    pe.wait_ge(hT_ready, n + 3)
                    hold(pe, o_ready, b + 1)
                    for k in range(KH):
                        last = nc.tensor.matmul(bank[4 + u][:, 0:OUT], hT[:, u, k, :], w_out_sb[:, k, :],
                                                start=(k == 0), stop=(k == KH - 1))
                    last.then_inc(o_done, 1)
                in_pairs(pe, project)


def kernel(**inputs):
    import numpy as np
    import concourse.bacc as bacc
    from concourse.bass_utils import run_bass_kernel_spmd

    a = {k.replace("L0_gnn_", ""): np.asarray(v) for k, v in inputs.items()}
    L, NS, H, F = a["strong_W1"].shape
    NW = a["weak_W"].shape[1]
    NE = NW + NS
    conf = np.concatenate([a["conf_W"], np.zeros_like(a["conf_W"])], axis=1)
    route_w = np.concatenate([a["router_W"], conf], axis=2).reshape(L, 2 * H // P, P, NE + 1).transpose(0, 2, 1, 3)
    route_b = np.concatenate([a["router_b"], a["conf_b"]], axis=1)
    weak = a["weak_W"].reshape(L, NW, 2, P, H).transpose(0, 1, 3, 2, 4).reshape(L, NW, P, 2 * H)
    first = a["strong_W1"].reshape(L, NS * 2, P, F)
    second = a["strong_W2"].reshape(L, NS * F // (2 * P), 2, P, H).transpose(0, 1, 3, 2, 4).reshape(L, -1, P, 2 * H)
    arrays = {
        "x": a["x"],
        "edges": np.stack([a["src"], a["dst"]], axis=1),
        "dst": a["dst"],
        "w_in": a["W_in"],
        "b_in": a["b_in"],
        "route_w": route_w,
        "route_b": route_b,
        "pieces": np.concatenate([weak, first, second], axis=1),
        "weak_b": a["weak_b"],
        "b1": a["strong_b1"].reshape(L, -1, P).transpose(0, 2, 1),
        "b2": a["strong_b2"],
        "w_out": a["W_out"].reshape(H // P, P, -1).transpose(1, 0, 2),
        "b_out": a["b_out"],
    }
    arrays = {f"in_{k}": np.ascontiguousarray(v) for k, v in arrays.items()}
    nc = bacc.Bacc("TRN2", target_bir_lowering=False, num_devices=1)
    args = [nc.dram_tensor(k, v.shape, mybir.dt.from_np(v.dtype), kind="ExternalInput").ap() for k, v in arrays.items()]
    args.append(nc.dram_tensor("out_0", a["x"].shape, mybir.dt.float32, kind="ExternalOutput").ap())
    gnn_program(nc, *args)
    r = run_bass_kernel_spmd(nc, [arrays], core_ids=[0])
    return r.results[0]["out_0"]
```

```python
import concourse.bass as bass
from concourse import mybir
from contextlib import ExitStack

F32 = mybir.dt.float32
F32R = mybir.dt.float32r
BF16 = mybir.dt.bfloat16
F16 = mybir.dt.float16
I32 = mybir.dt.int32
U32 = mybir.dt.uint32
ACT = mybir.ActivationFunctionType
ALU = mybir.AluOpType
AX = mybir.AxisListType

P = 128
EPS = 1e-5


def gnn_program(nc, x, edges, dst, w_in, b_in, route_w, route_b, pieces, weak_b, b1, b2, w_out, b_out, out):
    N, IN = x.shape
    E = edges.shape[0]
    LAYERS, _, KR, NE1 = route_w.shape
    NE = NE1 - 1
    NWEAK = weak_b.shape[1]
    NSTRONG = NE - NWEAK
    WQ = pieces.shape[1]
    KH = KR // 2
    H = KH * P
    KF = b1.shape[2] // NSTRONG
    OUT = w_out.shape[2]
    NB = (N + P - 1) // P
    LROWS = N - (NB - 1) * P
    WIN = 16
    CH = 5
    PCH = 2
    CAP = CH * P
    GROUPS = (N + WIN - 1) // WIN
    GP = P // WIN
    GBODY = 2 * GP
    SLOTS = GBODY * CH
    MW = NB * WIN
    ROWS = 125
    ROWLEN = E // ROWS
    TOK = 2 * P
    PAIR = 2 * TOK
    REGION = -(-N // PAIR) * PAIR
    TRIPS = (NB - 1) // 2
    XR = -(-(NE * REGION + TOK) // (2 * TRIPS * P))
    XROWS = XR * 2 * TRIPS * P
    LPAIRS = (2 * N + NE * (PAIR - 1)) // PAIR
    YR = -(-(LPAIRS * PAIR + TOK) // (2 * TRIPS * P))
    YROWS = YR * 2 * TRIPS * P
    assert ROWS * ROWLEN == E and NB % 2 == 1 and KH == 2 and WQ <= 2 * TRIPS and WQ % 2 == 0

    at_dram = nc.dram_tensor("at_scratch", (NB, P, NB * P), F16)
    starts_dram = nc.dram_tensor("starts_scratch", (2 * P,), I32)
    at_upper_dram = nc.dram_tensor("at_upper_scratch", (NB, P, NB * P), BF16)
    slot_x = nc.dram_tensor("slot_inputs", (XROWS, H), F32)
    slot_y = nc.dram_tensor("slot_results", (YROWS, H), F32)

    with ExitStack() as ctx:
        def sb(name, shape, dt, c=ctx):
            return c.enter_context(nc.sbuf_tensor(name, list(shape), dt))

        def sem(name):
            return ctx.enter_context(nc.semaphore(name))

        h_hi = sb("h_hi", [P, NB, H], F32R)
        h_lo = sb("h_lo", [P, NB, H], F32R)
        h_logits = sb("h_logits", [P, NB, NE1], F32)
        rdeg = sb("rdeg", [P, NB], F32)
        route_sb = sb("route_sb", [P, LAYERS, KR, NE1], F32)
        route_b_sb = sb("route_b_sb", [1, LAYERS, NE1], F32)
        identf = sb("identf", [P, P], F32)
        onesb = sb("onesb", [P, P], BF16)
        before_b = sb("before_b", [P, P], BF16)
        ones_row = sb("ones_row", [1, P], F32)
        expert_no = sb("expert_no", [P, NE], F32)
        region_0 = sb("region_0", [P, NE], F32)
        slow_flag = sb("slow_flag", [1, 1], I32)
        h_new = sb("h_new", [P, 2, H], F32)
        hT = sb("hT", [P, 2, KH, P], F32)
        bank = [ctx.enter_context(nc.psum_tensor(f"bank{i}", [P, 512], F32)) for i in range(8)]

        held = sem("held")

        def hold(eng, s, value):
            eng.wait_ge(s, value)
            eng.sem_inc(held, 1)

        new_ready = sem("new_ready")
        parts_done = sem("parts_done")
        hT_done = sem("hT_done")
        hT_ready = sem("hT_ready")
        hl_done = sem("hl_done")
        hl_kept = sem("hl_kept")

        def parts_of_block(dve, b, u):
            hi, lo = (t[:, bass.ds(b, 1)].rearrange("p o f -> p (o f)") for t in (h_hi, h_lo))
            nc.vector.tensor_copy(hi, h_new[:, u])
            dve.drain()
            nc.vector.tensor_tensor(lo, h_new[:, u], hi, ALU.subtract).then_inc(parts_done, 1)

        def keep_block(act, n, b, u, logits=True):
            act.wait_ge(hT_done, n + 3)
            act.wait_ge(hl_done, n + 1)
            nc.scalar.activation(hT[:, u].rearrange("p k n -> p (k n)"), bank[6 + u][:, 0:H], ACT.Copy
                                 ).then_inc(hT_ready, 1)
            if logits:
                hold(act, hl_done, n + 3)
                nc.scalar.activation(h_logits[:, bass.ds(b, 1)].rearrange("p o e -> p (o e)"),
                                     bank[4 + u][:, 0:NE1], ACT.Copy).then_inc(hl_kept, 1)

        def transpose_block(pe, n, u):
            pe.wait_ge(new_ready, n + 1)
            pe.wait_ge(hT_ready, n + 1)
            for k in range(KH):
                last = nc.tensor.transpose(bank[6 + u][:, k * P:(k + 1) * P], h_new[:, u, k * P:(k + 1) * P], identf[:])
            last.then_inc(hT_done, 1)

        def logits_of_block(pe, n, u, layer):
            pe.wait_ge(hT_ready, n + 3)
            hold(pe, hl_kept, n + 1)
            for k in range(KH):
                nc.tensor.matmul(bank[4 + u][:, 0:NE1], hT[:, u, k, :],
                                 route_sb[:, bass.ds(layer, 1), k, :].rearrange("p o e -> p (o e)"),
                                 start=(k == 0), stop=False)
            nc.tensor.matmul(bank[4 + u][:, 0:NE1], ones_row[:],
                             route_b_sb[:, bass.ds(layer, 1)].rearrange("p o e -> p (o e)"), start=False, stop=True
                             ).then_inc(hl_done, 1)

        with ExitStack() as c1:
            def sb1(name, shape, dt):
                return sb(name, shape, dt, c1)

            x_all = sb1("x_all", [P, NB, IN], F32)
            stats = sb1("stats", [P, NB, 6], F32)
            mv = sb1("mv", [P, NB, 2], F32)
            std = sb1("std", [P, NB], F32)
            rstd = sb1("rstd", [P, NB], F32)
            epsc = sb1("epsc", [P, 1], F32)
            h0 = sb1("h0", [P, 2, P], F32)
            w_in_sb = sb1("w_in_sb", [P, H], F32)
            b_in_sb = sb1("b_in_sb", [P, H], F32)
            iota_s = sb1("iota_s", [P, P], F16)
            iota_m = sb1("iota_m", [P, MW], F16)
            gidx = sb1("gidx", [P, GROUPS, CH], F32)
            thr = sb1("thr", [P, 2 * P], F32)
            thrcol = sb1("thrcol", [P, 2], F32)
            ones1 = sb1("ones1", [P, 1], F32)
            last_i = sb1("last_i", [P, 1], I32)
            last_f = sb1("last_f", [P, 1], F32)
            before = sb1("before", [P, 2 * P], F32)
            full_rows = sb1("full_rows", [P, 2], F32)
            row_idx = sb1("row_idx", [P, 2], U32)
            rows_i = sb1("rows_i", [P, 2, ROWLEN], I32)
            rows_f = sb1("rows_f", [P, 2, ROWLEN], F32)
            cnt = sb1("cnt", [P, 2], F32)
            start_f = sb1("start_f", [P, 2], F32)
            start_i = sb1("start_i", [P, 2], I32)
            start_row = sb1("start_row", [1, 2 * P], I32)
            ed = sb1("ed", [P, 2, SLOTS, 2], I32)
            src_hi = sb1("src_hi", [P, SLOTS], I32)
            src_lo = sb1("src_lo", [P, SLOTS], I32)
            dst_lo = sb1("dst_lo", [P, SLOTS], I32)
            dst_hi = sb1("dst_hi", [P, SLOTS], I32)
            col = sb1("col", [P, SLOTS], F32)
            valid = sb1("valid", [P, SLOTS], F32)
            key_m = sb1("key_m", [P, SLOTS], F32)
            key_s = sb1("key_s", [P, 2, SLOTS], F32)
            key_s16 = sb1("key_s16", [P, 2, SLOTS], F16)
            vsum = sb1("vsum", [P, 1], F32)
            vtotal = sb1("vtotal", [P, 1], F32)
            oh_s = sb1("oh_s", [P, 4, CH, P], F16)
            oh_m = sb1("oh_m", [P, 2, CH, MW], F16)
            piece = sb1("piece", [P, 2, NB, P], F16)
            zero = sb1("zero", [P, H], F32)
            junk = sb1("junk", [P, ROWLEN], F32)

            s_const = sem("s_const")
            s_zero = sem("s_zero")
            s_cleared = sem("s_cleared")
            s_wait = sem("s_wait")
            s_last = sem("s_last")
            x_in = sem("x_in")
            var_ready = sem("var_ready")
            std_ready = sem("std_ready")
            y_ready = sem("y_ready")
            yT_done = sem("yT_done")
            h0_ready = sem("h0_ready")
            proj_done = sem("proj_done")
            before_ready = sem("before_ready")
            full_done = sem("full_done")
            idx_ready = sem("idx_ready")
            rows_in = [sem("rows_in0"), sem("rows_in1")]
            start_ready = sem("start_ready")
            start_out = sem("start_out")
            start_in = sem("start_in")
            ed_in = [sem("ed_in0"), sem("ed_in1")]
            keys_ready = sem("keys_ready")
            hot_s_ready = sem("hot_s_ready")
            hot_m_ready = sem("hot_m_ready")
            win_done = sem("win_done")
            win_evac = sem("win_evac")
            deg_done = sem("deg_done")
            rdeg_ready = sem("rdeg_ready")
            at_stored = [sem("at_stored0"), sem("at_stored1")]
            piece_free = sem("piece_free")
            vtotal_ready = sem("vtotal_ready")
            vsum_done = sem("vsum_done")
            flag_ready = sem("flag_ready")

            block = c1.enter_context(nc.Block())
            LASTG = GROUPS - 2 * TRIPS * GP
            BODIES = TRIPS

            @block.sync
            def _(sp):
                sp.dma_start(x_all[:, 0:NB - 1], x[0:(NB - 1) * P, :].rearrange("(b p) f -> p b f", p=P)).then_inc(x_in, 16)
                sp.wait_ge(s_zero, 1)
                sp.dma_start(x_all[0:LROWS, NB - 1], x[(NB - 1) * P:N, :]).then_inc(x_in, 16)
                with nc.allow_non_contiguous_dma(reason="one word a row"):
                    sp.dma_start(last_i[0:ROWS, :], dst.rearrange("(p k) -> p k", p=ROWS)[:, ROWLEN - 1:ROWLEN]
                                 ).then_inc(s_last, 16)
                sp.dma_start(w_in_sb[:], w_in).then_inc(s_wait, 16)
                sp.dma_start(b_in_sb[:], b_in.rearrange("(o f) -> o f", o=1).to_broadcast([P, H])).then_inc(s_wait, 16)
                sp.dma_start(route_sb[:], route_w.rearrange("l p k e -> p l k e")).then_inc(s_wait, 16)
                sp.dma_start(route_b_sb[:], route_b.rearrange("(o l) e -> o l e", o=1)).then_inc(s_wait, 16)

                sp.wait_ge(start_ready, 1)
                for k in range(2):
                    sp.dma_start(starts_dram[k * P:(k + 1) * P].rearrange("(p o) -> p o", o=1),
                                 start_i[:, k:k + 1]).then_inc(start_out, 16)
                sp.wait_ge(start_out, 32)
                sp.dma_start(start_row[:, :], starts_dram[:].rearrange("(o g) -> o g", o=1)).then_inc(start_in, 16)
                sp.wait_ge(start_in, 16)

                def fetch(b, par, count):
                    hold(sp, keys_ready, b + 1)
                    with sp.Fori(0, count) as g:
                        first = sp.value_load(start_row[0:1, bass.ds(b * GBODY + g, 1)], min_val=0, max_val=E - CAP)
                        sp.dma_start(ed[:, par, bass.ds(g * CH, CH), :],
                                     edges[bass.ds(first, CAP), :].rearrange("(p k) two -> p k two", k=CH)
                                     ).then_inc(ed_in[par], 16)

                def store(k, slot, uses):
                    hold(sp, rdeg_ready, k + 3)
                    sp.dma_start(at_dram[bass.ds(k, 1)].rearrange("o p c -> p (o c)"),
                                 piece[:, slot].rearrange("p s d -> p (s d)")).then_inc(at_stored[slot], 16)
                    hold(sp, at_stored[slot], 16 * uses)
                    sp.sem_inc(piece_free, 1)

                sp.sem_inc(piece_free, 2)
                fetch(0, 0, GBODY // 2)
                fetch(1, 1, GBODY // 2)
                with sp.Fori(0, BODIES // 2 - 1) as i:
                    for par in range(2):
                        store(4 * i + 2 * par, 0, 2 * i + par + 1)
                        store(4 * i + 2 * par + 1, 1, 2 * i + par + 1)
                        hold(sp, ed_in[par], 16 * GBODY * (i + 1))
                        fetch(2 * i + 2 + par, par, GBODY // 2)
                for par in range(2):
                    store(NB - 5 + 2 * par, 0, BODIES - 1 + par)
                    store(NB - 4 + 2 * par, 1, BODIES - 1 + par)
                    if par == 0:
                        sp.wait_ge(ed_in[0], 16 * GBODY * (BODIES // 2))
                        fetch(BODIES, 0, LASTG)
                store(NB - 1, 0, BODIES + 1)

            @block.gpsimd
            def _(pool):
                nc.gpsimd.memset(zero[:], 0.0)
                nc.gpsimd.memset(x_all[:, NB - 1], 0.0)
                pool.drain().then_inc(s_zero, 1)
                nc.gpsimd.memset(identf[:], 0.0)
                nc.gpsimd.memset(onesb[:], 1.0)
                nc.gpsimd.memset(before_b[:], 1.0)
                nc.gpsimd.memset(ones_row[:], 1.0)
                nc.gpsimd.memset(ones1[:], 1.0)
                nc.gpsimd.memset(epsc[:], EPS)
                nc.gpsimd.memset(piece[:], 0.0)
                nc.gpsimd.memset(last_f[:], 1e9)
                nc.gpsimd.memset(vtotal[:], 0.0)
                for tile, pattern, base, per_row in (
                        (iota_s, [[1, P]], 0, 0), (iota_m, [[1, MW]], 1, 0),
                        (gidx, [[1, GROUPS], [0, CH]], 0, 0), (thr, [[WIN, 2 * P]], 0, 0),
                        (thrcol, [[WIN * P, 2]], 0, WIN), (expert_no, [[1, NE]], 0, 0),
                        (region_0, [[REGION, NE]], 0, 0)):
                    nc.gpsimd.iota(tile[:], pattern=pattern, base=base, channel_multiplier=per_row,
                                   allow_small_or_imprecise_dtypes=True)
                pool.drain()
                nc.gpsimd.affine_select(out=identf[:], in_=identf[:], compare_op=ALU.not_equal, fill=1.0,
                                        base=0, pattern=[[-1, P]], channel_multiplier=1)
                nc.gpsimd.affine_select(out=before_b[:], in_=before_b[:], compare_op=ALU.is_gt, fill=0.0,
                                        base=0, pattern=[[1, P]], channel_multiplier=-1)
                pool.drain().then_inc(s_const, 1)
                pool.wait_ge(idx_ready, 1)
                for k in range(2):
                    nc.gpsimd.indirect_dma_start(
                        out=rows_i[:, k, :], out_offset=None, in_=dst.rearrange("(p k) -> p k", p=ROWS),
                        in_offset=bass.IndirectOffsetOnAxis(ap=row_idx[:, k:k + 1], axis=0),
                        bounds_check=ROWS - 1, oob_is_err=False).then_inc(rows_in[k], 16)

                def one_hots(n, gi, par):
                    hold(pool, win_done, n + 1)
                    for c in range(PCH):
                        s = gi * CH + c
                        last = nc.gpsimd.tensor_scalar(oh_s[:, gi % 4, c], iota_s[:], key_s[:, par, s:s + 1], None,
                                                       ALU.is_equal)
                    last.then_inc(hot_s_ready, 1)

                with pool.Fori(0, BODIES // 2) as i:
                    for par in range(2):
                        hold(pool, keys_ready, 2 * i + par + 3)
                        for gi in range(GBODY):
                            one_hots((2 * i + par) * GBODY + gi, gi, par)
                hold(pool, keys_ready, BODIES + 3)
                for gi in range(LASTG):
                    one_hots(BODIES * GBODY + gi, gi, 0)

            @block.scalar
            def _(act):
                act.sem_inc(win_evac, 4)
                act.sem_inc(hT_ready, 2)
                act.sem_inc(hl_kept, 2)
                act.sem_inc(h0_ready, 2)
                act.wait_ge(s_const, 1)
                act.wait_ge(var_ready, 1)
                nc.scalar.activation(std[:], mv[:, :, 1], ACT.Sqrt, bias=epsc[:, 0:1]).then_inc(std_ready, 1)

                def relu(b):
                    act.wait_ge(yT_done, b + 1)
                    act.wait_ge(proj_done, b + 1)
                    nc.scalar.activation(h0[:, b % 2], bank[b % 2][:, 0:P], ACT.Relu).then_inc(h0_ready, 1)

                relu(0)
                for b in range(NB):
                    if b + 1 < NB:
                        relu(b + 1)
                    keep_block(act, b, b, b % 2)

                def evacuate(n, gi, slot):
                    act.wait_ge(win_done, n + 5)
                    nc.scalar.activation(piece[:, slot, :, (gi % GP) * WIN:(gi % GP + 1) * WIN],
                                         bank[gi % 4][:, 0:MW].rearrange("p (s d) -> p s d", d=WIN),
                                         ACT.Copy).then_inc(win_evac, 1)

                def clear(slots, per, k):
                    act.dma_start(slots[bass.ds(k * per * P, per * P), :].rearrange("(p r) f -> p r f", p=P),
                                  zero[:].unsqueeze(1).to_broadcast([P, per, H])).then_inc(s_cleared, 16)

                def fetch(b, par, g):
                    first = act.value_load(start_row[0:1, bass.ds(b * GBODY + g, 1)], min_val=0, max_val=E - CAP)
                    act.dma_start(ed[:, par, g * CH:(g + 1) * CH, :],
                                  edges[bass.ds(first, CAP), :].rearrange("(p k) two -> p k two", k=CH)
                                  ).then_inc(ed_in[par], 16)

                act.wait_ge(start_in, 16)
                for par in range(2):
                    for g in range(GBODY // 2, GBODY):
                        fetch(par, par, g)

                def turn(b, par, more):
                    if more:
                        hold(act, keys_ready, b + 3)
                    for k in range(2):
                        clear(slot_x, XR, 2 * b + k)
                        clear(slot_y, YR, 2 * b + k)
                        act.wait_ge(piece_free, 2 * b + k + 1)
                        for gi in range(GP):
                            if more and gi % 2:
                                fetch(b + 2, par, GBODY // 2 + (k * GP + gi) // 2)
                            evacuate((2 * b + k) * GP + gi, gi, k)

                with act.Fori(0, BODIES // 2 - 1) as i:
                    for par in range(2):
                        turn(2 * i + par, par, True)
                for par in range(2):
                    turn(BODIES - 2 + par, par, False)
                act.wait_ge(piece_free, NB)
                for gi in range(LASTG):
                    evacuate(2 * BODIES * GP + gi, gi, 0)
                act.wait_ge(s_cleared, 4 * BODIES * 16)

            @block.vector
            def _(dve):
                dve.sem_inc(keys_ready, 2)
                dve.sem_inc(rdeg_ready, 2)
                dve.wait_ge(x_in, 32)
                for b in range(NB):
                    nc.vector.bn_stats(stats[:, b, :], x_all[:, b, :])
                dve.drain()
                for b in range(NB):
                    nc.vector.bn_aggr(mv[:, b, :], stats[:, b, :])
                dve.drain().then_inc(var_ready, 1)

                dve.wait_ge(s_const, 1)
                dve.wait_ge(s_last, 16)
                nc.vector.tensor_copy(last_f[0:ROWS, :], last_i[0:ROWS, :])
                dve.drain()
                nc.vector.tensor_scalar(before[:], thr[:], last_f[:, 0:1], None, ALU.is_gt).then_inc(before_ready, 1)
                dve.wait_ge(full_done, 1)
                nc.vector.tensor_copy(full_rows[:], bank[3][:, 0:2])
                dve.drain()
                nc.vector.tensor_scalar(row_idx[:], full_rows[:], float(ROWS - 1), None, ALU.min).then_inc(idx_ready, 1)

                dve.wait_ge(std_ready, 1)
                nc.vector.reciprocal(rstd[:], std[:])
                dve.drain()
                for b in range(NB):
                    nc.vector.tensor_scalar(x_all[:, b, :], x_all[:, b, :], mv[:, b, 0:1], rstd[:, b:b + 1],
                                            ALU.subtract, ALU.mult).then_inc(y_ready, 1)

                for k in range(2):
                    dve.wait_ge(rows_in[k], 16)
                    nc.vector.tensor_copy(rows_f[:, k], rows_i[:, k])
                    dve.drain()
                    nc.vector.tensor_scalar(junk[:], rows_f[:, k], thrcol[:, k:k + 1], None, ALU.is_lt, ALU.add,
                                            accum_out=cnt[:, k:k + 1])
                    dve.drain()
                nc.vector.scalar_tensor_tensor(start_f[:], full_rows[:], float(ROWLEN), cnt[:], ALU.mult, ALU.add)
                dve.drain()
                nc.vector.tensor_scalar(start_i[:], start_f[:], float(E - CAP), None, ALU.min).then_inc(start_ready, 1)

                dve.wait_ge(s_wait, 64)
                for b in range(NB):
                    dve.wait_ge(proj_done, b + 3)
                    dve.wait_ge(hT_done, b + 1)
                    nc.vector.tensor_tensor(h_new[:, b % 2], bank[2 + b % 2][:, 0:H], b_in_sb[:], ALU.add
                                            ).then_inc(new_ready, 1)
                    dve.drain()
                    parts_of_block(dve, b, b % 2)

                def keys(b, par, n):
                    e = ed[:, par, 0:n, :]
                    nc.vector.tensor_scalar(src_hi[:, 0:n], e[:, :, 0], 3, 0xFFF0, ALU.logical_shift_right,
                                            ALU.bitwise_and)
                    nc.vector.tensor_scalar(dst_lo[:, 0:n], e[:, :, 1], WIN - 1, None, ALU.bitwise_and)
                    nc.vector.tensor_scalar(dst_hi[:, 0:n], e[:, :, 1], 4, None, ALU.logical_shift_right)
                    nc.vector.tensor_scalar(src_lo[:, 0:n], e[:, :, 0], P - 1, None, ALU.bitwise_and)
                    dve.drain()
                    nc.vector.tensor_tensor(col[:, 0:n], src_hi[:, 0:n], dst_lo[:, 0:n], ALU.add)
                    nc.vector.tensor_tensor(valid[:, 0:n], dst_hi[:, 0:n],
                                            gidx[:].rearrange("p g c -> p (g c)")[:, bass.ds(b * SLOTS, n)],
                                            ALU.is_equal)
                    nc.vector.tensor_copy(key_s[:, par, 0:n], src_lo[:, 0:n])
                    nc.vector.tensor_copy(key_s16[:, par, 0:n], src_lo[:, 0:n])
                    dve.drain().then_inc(keys_ready, 1)
                    nc.vector.scalar_tensor_tensor(key_m[:, 0:n], col[:, 0:n], 1.0, valid[:, 0:n], ALU.add, ALU.mult)
                    nc.vector.tensor_reduce(vsum[:], valid[:, 0:n], AX.X, ALU.add)
                    dve.drain()
                    nc.vector.tensor_tensor(vtotal[:], vtotal[:], vsum[:], ALU.add)
                    dve.drain()

                def one_hots(n, gi, par):
                    dve.wait_ge(win_done, n + 3)
                    s = slice(gi * CH + PCH, (gi + 1) * CH)
                    nc.vector.tensor_tensor(oh_s[:, gi % 4, PCH:CH], iota_s[:].unsqueeze(1).to_broadcast([P, CH - PCH, P]),
                                            key_s16[:, par, s].unsqueeze(2).to_broadcast([P, CH - PCH, P]), ALU.is_equal)
                    for c in range(CH):
                        s = gi * CH + c
                        last = nc.vector.tensor_scalar(oh_m[:, gi % 2, c], iota_m[:], key_m[:, s:s + 1], None,
                                                       ALU.is_equal)
                    last.then_inc(hot_m_ready, 1)

                def reciprocal_degree(k, slot):
                    dve.wait_ge(deg_done, k + 3)
                    nc.vector.tensor_scalar(rdeg[:, bass.ds(k, 1)], bank[4 + slot][:, 0:1], 1.0, None, ALU.max)
                    dve.drain()
                    nc.vector.reciprocal(rdeg[:, bass.ds(k, 1)], rdeg[:, bass.ds(k, 1)]).then_inc(rdeg_ready, 1)

                with dve.Fori(0, BODIES // 2) as i:
                    for par in range(2):
                        dve.wait_ge(ed_in[par], 16 * GBODY * (i + 1))
                        keys(2 * i + par, par, SLOTS)
                        for gi in range(GBODY):
                            one_hots((2 * i + par) * GBODY + gi, gi, par)
                            if gi == GP + 2:
                                reciprocal_degree(4 * i + 2 * par, 0)
                        reciprocal_degree(4 * i + 2 * par + 1, 1)
                dve.wait_ge(ed_in[0], 16 * (GBODY * (BODIES // 2) + LASTG))
                keys(BODIES, 0, LASTG * CH)
                for gi in range(LASTG):
                    one_hots(BODIES * GBODY + gi, gi, 0)
                reciprocal_degree(NB - 1, 0)
                dve.drain().then_inc(vtotal_ready, 1)
                dve.wait_ge(vsum_done, 1)
                nc.vector.tensor_scalar(slow_flag[:], bank[6][0:1, 0:1], float(E), None, ALU.not_equal
                                        ).then_inc(flag_ready, 1)

            @block.tensor
            def _(pe):
                pe.sem_inc(win_done, 4)
                pe.sem_inc(proj_done, 2)
                pe.sem_inc(hT_done, 2)
                pe.sem_inc(hl_done, 2)
                pe.sem_inc(deg_done, 2)
                pe.wait_ge(s_const, 1)
                pe.wait_ge(before_ready, 1)
                for k in range(2):
                    last = nc.tensor.matmul(bank[3][:, k:k + 1], before[:, k * P:(k + 1) * P], ones1[:],
                                            start=True, stop=True)
                last.then_inc(full_done, 1)

                def transpose_x(b):
                    pe.wait_ge(y_ready, b + 1)
                    pe.wait_ge(h0_ready, b + 1)
                    nc.tensor.transpose(bank[b % 2][:, 0:P], x_all[:, b, :], identf[:]).then_inc(yT_done, 1)

                def project(b):
                    pe.wait_ge(h0_ready, b + 3)
                    if b >= 2:
                        pe.wait_ge(new_ready, b - 1)
                    elif b == 1:
                        pe.wait_ge(idx_ready, 1)
                    nc.tensor.matmul(bank[2 + b % 2][:, 0:H], h0[:, b % 2], w_in_sb[:], start=True, stop=True
                                     ).then_inc(proj_done, 1)

                pe.wait_ge(s_wait, 64)
                transpose_x(0)
                project(0)
                for b in range(NB):
                    if b + 1 < NB:
                        transpose_x(b + 1)
                        project(b + 1)
                    transpose_block(pe, b, b % 2)
                    logits_of_block(pe, b, b % 2, 0)
                pe.wait_ge(hl_kept, NB + 2)
                pe.wait_ge(new_ready, NB)

                def window(n, gi):
                    pe.wait_ge(hot_s_ready, n + 1)
                    pe.wait_ge(hot_m_ready, n + 1)
                    pe.wait_ge(win_evac, n + 1)
                    for c in range(CH):
                        last = nc.tensor.matmul(bank[gi % 4][:, 0:MW], oh_s[:, gi % 4, c], oh_m[:, gi % 2, c],
                                                start=(c == 0), stop=(c == CH - 1))
                    last.then_inc(win_done, 1)

                def degrees(k, slot, n):
                    pe.wait_ge(rdeg_ready, k + 1)
                    pe.wait_ge(win_evac, n + 4)
                    for s in range(NB):
                        last = nc.tensor.matmul(bank[4 + slot][:, 0:1], piece[:, slot, s, :], onesb[:, 0:1],
                                                start=(s == 0), stop=(s == NB - 1))
                    last.then_inc(deg_done, 1)

                with pe.Fori(0, BODIES) as i:
                    for k in range(2):
                        for gi in range(GP):
                            window((2 * i + k) * GP + gi, gi)
                        degrees(2 * i + k, k, (2 * i + k + 1) * GP)
                for gi in range(LASTG):
                    window(2 * BODIES * GP + gi, gi)
                degrees(NB - 1, 0, GROUPS)
                pe.wait_ge(vtotal_ready, 1)
                nc.tensor.matmul(bank[6][0:1, 0:1], vtotal[:], ones1[:], start=True, stop=True).then_inc(vsum_done, 1)


        with ExitStack() as cg:
            NCH = ROWLEN
            ROUND = 2048
            BANKS = -(-NB * P // 512)
            g_ed = sb("g_ed", [ROWS, NCH, 2], I32, cg)
            g_a = sb("g_a", [ROWS, NCH], I32, cg)
            g_b = sb("g_b", [ROWS, NCH], I32, cg)
            g_c = sb("g_c", [ROWS, NCH], I32, cg)
            g_src = sb("g_src", [ROWS, NCH], F32, cg)
            g_blk = sb("g_blk", [ROWS, NCH], F32, cg)
            g_dlo = sb("g_dlo", [ROWS, NCH], F32, cg)
            g_col = sb("g_col", [ROWS, NCH], F32, cg)
            g_now = sb("g_now", [P, 1], F32, cg)
            g_key = sb("g_key", [ROWS, NCH], F32, cg)
            g_dkey = sb("g_dkey", [ROWS, NCH], F32, cg)
            g_iota = sb("g_iota", [P, NB * P], F32, cg)
            g_hot_s = sb("g_hot_s", [ROWS, P], BF16, cg)
            g_hot_d = sb("g_hot_d", [ROWS, P], BF16, cg)
            g_hot_m = sb("g_hot_m", [ROWS, NB * P], BF16, cg)
            g_count = sb("g_count", [P, 512], I32, cg)
            g_part = sb("g_part", [P, 512], I32, cg)
            g_low = sb("g_low", [P, NB * P], F16, cg)
            g_up = sb("g_up", [P, NB * P], BF16, cg)
            g_zero = sb("g_zero", [P, 512], BF16, cg)
            g_const = sem("g_const")
            g_in = sem("g_in")
            g_cleared = sem("g_cleared")
            g_hot = sem("g_hot")
            g_mult = sem("g_mult")
            g_sum = sem("g_sum")
            g_taken = sem("g_taken")
            g_low_out = sem("g_low_out")
            g_up_out = sem("g_up_out")
            g_free = sem("g_free")

            block = cg.enter_context(nc.Block())

            @block.sync
            def _(sp):
                slow = sp.value_load(slow_flag[0:1, 0:1], min_val=0, max_val=1)
                with sp.If(slow == 0):
                    sp.nop()
                with sp.Else():
                    sp.dma_start(g_ed[:], edges.rearrange("(p k) two -> p k two", p=ROWS)).then_inc(g_in, 16)
                    sp.sem_inc(g_free, 1)
                    with sp.Fori(0, NB) as b:
                        hold(sp, g_taken, b + 2)
                        sp.dma_start(at_dram[bass.ds(b, 1)].rearrange("o p c -> p (o c)"), g_low[:]).then_inc(g_low_out, 16)
                        sp.dma_start(at_upper_dram[bass.ds(b, 1)].rearrange("o p c -> p (o c)"), g_up[:]
                                     ).then_inc(g_up_out, 16)
                        hold(sp, g_low_out, 16 * (b + 1))
                        hold(sp, g_up_out, 16 * (b + 1))
                        sp.sem_inc(g_free, 1)
                sp.nop()

            @block.gpsimd
            def _(pool):
                slow = pool.value_load(slow_flag[0:1, 0:1], min_val=0, max_val=1)
                with pool.If(slow == 0):
                    pool.nop()
                with pool.Else():
                    nc.gpsimd.iota(g_iota[:], pattern=[[1, NB * P]], base=1, channel_multiplier=0,
                                   allow_small_or_imprecise_dtypes=True)
                    nc.gpsimd.memset(g_now[:], 0.0)
                    nc.gpsimd.memset(g_zero[:], 0.0)
                    pool.drain().then_inc(g_const, 1)
                pool.nop()

            @block.vector
            def _(dve):
                slow = dve.value_load(slow_flag[0:1, 0:1], min_val=0, max_val=1)
                with dve.If(slow == 0):
                    dve.nop()
                with dve.Else():
                    dve.sem_inc(g_taken, 1)
                    dve.wait_ge(g_const, 1)
                    dve.wait_ge(g_in, 16)
                    src, to = g_ed[:, :, 0], g_ed[:, :, 1]
                    nc.vector.tensor_scalar(g_a[:], src, P - 1, None, ALU.bitwise_and)
                    nc.vector.tensor_scalar(g_b[:], to, P - 1, None, ALU.bitwise_and)
                    nc.vector.tensor_scalar(g_c[:], to, 7, None, ALU.logical_shift_right)
                    dve.drain()
                    nc.vector.tensor_scalar(g_src[:], g_a[:], 1.0, None, ALU.add)
                    nc.vector.tensor_scalar(g_dlo[:], g_b[:], 1.0, None, ALU.add)
                    nc.vector.tensor_copy(g_blk[:], g_c[:])
                    dve.drain()
                    nc.vector.tensor_tensor(g_a[:], src, g_a[:], ALU.subtract)
                    dve.drain()
                    nc.vector.tensor_tensor(g_col[:], g_a[:], g_dlo[:], ALU.add)
                    dve.drain()
                    with dve.Fori(0, NB) as b:
                        nc.vector.scalar_tensor_tensor(g_key[:], g_blk[:], g_now[0:ROWS, 0:1], g_col[:], ALU.is_equal, ALU.mult)
                        nc.vector.scalar_tensor_tensor(g_dkey[:], g_blk[:], g_now[0:ROWS, 0:1], g_dlo[:], ALU.is_equal, ALU.mult)
                        dve.drain()
                        with dve.Fori(0, NCH) as c:
                            hold(dve, g_mult, NCH * b + c + 1)
                            nc.vector.tensor_scalar(g_hot_s[:], g_iota[0:ROWS, 0:P], g_src[:, bass.ds(c, 1)], None, ALU.is_equal)
                            nc.vector.tensor_scalar(g_hot_d[:], g_iota[0:ROWS, 0:P], g_dkey[:, bass.ds(c, 1)], None, ALU.is_equal)
                            nc.vector.tensor_scalar(g_hot_m[:], g_iota[0:ROWS, :], g_key[:, bass.ds(c, 1)], None, ALU.is_equal)
                            dve.drain().then_inc(g_hot, 1)
                        hold(dve, g_sum, b + 1)
                        hold(dve, g_free, b + 1)
                        for j in range(BANKS):
                            w = min(512, NB * P - 512 * j)
                            part = slice(512 * j, 512 * j + w)
                            nc.vector.tensor_copy(g_count[:, 0:w], bank[j][:, 0:w])
                            dve.drain()
                            nc.vector.tensor_scalar(g_part[:, 0:w], g_count[:, 0:w], ROUND - 1, None, ALU.bitwise_and)
                            dve.drain()
                            nc.vector.tensor_copy(g_low[:, part], g_part[:, 0:w])
                            nc.vector.tensor_tensor(g_up[:, part], g_count[:, 0:w], g_part[:, 0:w], ALU.subtract)
                            dve.drain()
                        nc.vector.tensor_scalar(rdeg[:, bass.ds(b, 1)], bank[7][:, 0:1], 1.0, None, ALU.max)
                        nc.vector.tensor_scalar(g_now[:], g_now[:], 1.0, None, ALU.add)
                        dve.drain()
                        nc.vector.reciprocal(rdeg[:, bass.ds(b, 1)], rdeg[:, bass.ds(b, 1)])
                        dve.drain().then_inc(g_taken, 1)
                dve.nop()

            @block.tensor
            def _(pe):
                slow = pe.value_load(slow_flag[0:1, 0:1], min_val=0, max_val=1)
                with pe.If(slow == 0):
                    pe.nop()
                with pe.Else():
                    pe.sem_inc(g_mult, 1)
                    hold(pe, g_const, 1)

                    def edge_of_block(start):
                        for j in range(BANKS + 1):
                            w = 1 if j == BANKS else min(512, NB * P - 512 * j)
                            last = nc.tensor.matmul(bank[j][:, 0:w], onesb[:], g_zero[:, 0:w], start=start,
                                                    stop=not start, skip_group_check=True)
                        return last

                    with pe.Fori(0, NB) as b:
                        hold(pe, g_taken, b + 1)
                        edge_of_block(True)
                        with pe.Fori(0, NCH) as c:
                            hold(pe, g_hot, NCH * b + c + 1)
                            for j in range(BANKS):
                                w = min(512, NB * P - 512 * j)
                                nc.tensor.matmul(bank[j][:, 0:w], g_hot_s[:], g_hot_m[:, 512 * j:512 * j + w],
                                                 start=False, stop=False, skip_group_check=True)
                            nc.tensor.matmul(bank[BANKS][:, 0:1], g_hot_d[:], onesb[0:ROWS, 0:1], start=False, stop=False,
                                             skip_group_check=True).then_inc(g_mult, 1)
                        edge_of_block(False).then_inc(g_sum, 1)
                pe.nop()

        slot_here = sem("slot_here")
        combined = sem("combined")
        phase_end = sem("phase_end")
        g_all = sb("g_all", [P, NB, 2], F32)
        slots_all = sb("slots_all", [P, 2 * NB], U32)
        slot_get = sb("slot_get", [P, 4, 2], U32)
        GOT = 4
        assert (NB - 1) % GOT == 0
        got = [sem(f"got{i}") for i in range(GOT)]
        GFIRST, GOTHER = (NB - 1) // GOT + 1, (NB - 1) // GOT
        FIRST, SECOND = TRIPS + 1, TRIPS
        SC = 5
        assert NB % SC == 0

        def join(eng, n):
            eng.drain().then_inc(phase_end, 1)
            hold(eng, phase_end, 5 * n)

        def collect(pool, y_got, l, b, v, rows=P):
            hold(pool, combined, NB * l + b + 1)
            nc.gpsimd.tensor_copy(slot_get[:, v], slots_all[:, bass.ds(2 * b, 2)]).then_inc(slot_here, 1)
            hold(pool, slot_here, NB * l + b + 1)
            for k in range(2):
                nc.gpsimd.indirect_dma_start(
                    out=y_got[0:rows, v, k], out_offset=None, in_=slot_y[:],
                    in_offset=bass.IndirectOffsetOnAxis(ap=slot_get[0:rows, v, k:k + 1], axis=0),
                    bounds_check=YROWS - 1, oob_is_err=False).then_inc(got[v], 16)

        def collect_all(pool, y_got, l):
            with pool.Fori(0, (NB - 1) // GOT) as i:
                for v in range(GOT):
                    collect(pool, y_got, l, GOT * i + v, v)
            collect(pool, y_got, l, NB - 1, 0, LROWS)

        def combine(dve, y_got, l, b, v, i, rows=P):
            n = NB * (l + 1) + b
            R = slice(0, rows)
            hold(dve, got[v], 32 * ((GOTHER if v else GFIRST) * l + i + 1))
            hold(dve, hT_done, n + 1)
            for k, part in enumerate((h_hi, h_lo)):
                nc.vector.scalar_tensor_tensor(y_got[R, v, k], y_got[R, v, k], g_all[R, bass.ds(b, 1), k],
                                               part[R, bass.ds(b, 1)].rearrange("p o f -> p (o f)"), ALU.mult, ALU.add)
            dve.drain()
            nc.vector.tensor_tensor(h_new[R, v % 2], y_got[R, v, 0], y_got[R, v, 1], ALU.add).then_inc(new_ready, 1)

        def in_pairs(eng, step):
            with eng.Fori(0, TRIPS) as i:
                for u in range(2):
                    step(2 * i + u, u, i)
            step(NB - 1, 0, TRIPS)

        with ExitStack() as c2:
            def sb2(name, shape, dt):
                return sb(name, shape, dt, c2)

            at_in_sb = sb2("at_in_sb", [P, 2, NB, P], F16)
            shared = sb2("shared", [P, 2 * NB * P], F32R)
            at_r = shared[:].rearrange("p (u s d) -> p u s d", u=2, d=P)
            parts = shared[:, 0:4 * KH * TOK].rearrange("p (u h k n) -> p u h k n", u=2, h=2, k=KH)
            x_hi, x_lo = parts[:, :, 0], parts[:, :, 1]
            acts = shared[:, 4 * KH * TOK:4 * KH * TOK + 2 * KF * TOK].rearrange("p (h k n) -> p h k n", h=2, k=KF)
            act_hi, act_lo = acts[:, 0], acts[:, 1]
            pool_f = sb2("phase_buffer", [P, 8 * H], F32)
            agg = pool_f[:, 0:2 * H].rearrange("p (u f) -> p u f", u=2)
            aT = pool_f[:, 2 * H:4 * H].rearrange("p (u k n) -> p u k n", u=2, k=KH)
            AGG = 4
            agg_out = pool_f[:, 4 * H:8 * H].rearrange("p (u f) -> p u f", u=AGG)
            y_sb = pool_f[:, 4 * H:8 * H].rearrange("p (u s f) -> p u s f", u=2, s=2)
            y_got = pool_f[:].rearrange("p (u k f) -> p u k f", u=GOT, k=2)
            stage_f = sb2("stage", [P, 2 * 512], F32)
            stage = stage_f[:].rearrange("p (u f) -> p u f", u=2)
            x_rows = stage_f[:, 0:2 * H].rearrange("p (s f) -> p s f", s=2)
            v = stage_f[:, 2 * H:2 * H + 2 * TOK].rearrange("p (u n) -> p u n", u=2)
            w_hi = sb2("w_hi", [P, WQ, 512], F32R)
            w_lo = sb2("w_lo", [P, WQ, 512], F32R)
            bias = sb2("bias", [P, NE, H], F32)
            b1_sb = sb2("b1_sb", [P, NSTRONG * KF], F32)
            lg = sb2("lg", [P, NE1], F32)
            top = sb2("top", [P, 8], F32)
            idx = sb2("idx", [P, 8], U32)
            idx_f = sb2("idx_f", [P, 2], F32)
            dz = sb2("dz", [P, 2], F32)
            ex = sb2("ex", [P, 2], F32)
            den = sb2("den", [P, 2], F32)
            rec = sb2("rec", [P, 2], F32)
            gt = sb2("gt", [P, 2], F32)
            hots = sb2("hots", [P, 2, NE], F32)
            member = sb2("member", [P, NE], BF16)
            next_slot = sb2("next_slot", [P, NE], F32)
            pos = sb2("pos", [P, NE], F32)
            prod = sb2("prod", [P, 2, NE], F32)
            slot_f = sb2("slot_f", [P, 2], F32)
            slot_now = sb2("slot_now", [P, 2, 2], U32)
            idx_all = sb2("idx_all", [P, 2 * NB], F32)
            slots_f = sb2("slots_f", [P, 2 * NB], F32)
            moved = sb2("moved", [P, 2 * NB, NE], F32)
            shift = sb2("shift", [P, NE], F32)
            taken = sb2("taken", [P, NE], F32)
            taken_i = sb2("taken_i", [P, NE], I32)
            sums = [sb2(f"sums{i}", [P, 2 * NE], F32) for i in range(2)]
            tiles_before = sb2("tiles_before", [P, 1], F32)
            strong_shift = sb2("strong_shift", [P, 1], F32)
            plan_f = sb2("plan_f", [P, 4 * NE], F32)
            plan = sb2("plan", [1, 4 * NE], I32)

            zeroed = sem("zeroed")
            at_in = [sem("at_in0"), sem("at_in1")]
            at_used = [sem("at_used0"), sem("at_used1")]
            at_ready = sem("at_ready")
            pass_done = sem("pass_done")
            small_in = sem("small_in")
            w_in_ = [sem("w_in0"), sem("w_in1")]
            w_hi_done = sem("w_hi_done")
            w_split = sem("w_split")
            agg_done = sem("agg_done")
            agg_ready = sem("agg_ready")
            agg_free = sem("agg_free")
            aT_done = sem("aT_done")
            aT_ready = sem("aT_ready")
            lg_done = sem("lg_done")
            lg_taken = sem("lg_taken")
            dz_ready = sem("dz_ready")
            ex_ready = sem("ex_ready")
            member_ready = sem("member_ready")
            rank_done = sem("rank_done")
            slot_ready = sem("slot_ready")
            scattered = sem("scattered")
            x_in2 = sem("x_in2")
            xT_done = sem("xT_done")
            xh_ready = sem("xh_ready")
            xl_ready = sem("xl_ready")
            unit_done = sem("unit_done")
            hi_ready = sem("hi_ready")
            lo_ready = sem("lo_ready")
            y_done = sem("y_done")
            y_ready = sem("y_ready2")
            y_out = [sem("y_out0"), sem("y_out1")]

            x_bank = (0, 7)
            unit_bank = (1, 2, 5, 6)

            block = c2.enter_context(nc.Block())

            def each_expert(eng, tile, last=None):
                def planned(k, e, most):
                    return eng.value_load(plan[0:1, k * NE + e:k * NE + e + 1], min_val=0, max_val=most)

                for e in range(NE):
                    count = eng.value_load(plan[0:1, e:e + 1], min_val=1, max_val=REGION // PAIR)
                    base = planned(1, e, LAYERS * LPAIRS)
                    sbase = planned(2, e, LAYERS * LPAIRS) if e >= NWEAK else 0
                    lbase = planned(3, e, LPAIRS - 1)
                    with eng.Fori(0, count) as t:
                        Y = nc.s_assert_within(lbase + t, 0, LPAIRS - 1, skip_runtime_bounds_check_because=
                                               "the layer's pairs are at most LPAIRS")
                        for p in range(2):
                            tile(e, t, p, 2 * (base + t) + p, 2 * (sbase + t) + p, base + t, Y)
                if last is not None:
                    last(base + count)

            def first_tile(eng):
                return 2 * eng.value_load(plan[0:1, NE:NE + 1], min_val=0, max_val=LAYERS * LPAIRS)

            def layers(phase_a, phase_b, phase_c, eng):
                with eng.Fori(0, LAYERS - 1) as l:
                    phase_a(l)
                    join(eng, 3 * l + 1)
                    phase_b(l, False)
                    join(eng, 3 * l + 2)
                    phase_c(l)
                    join(eng, 3 * l + 3)
                phase_a(LAYERS - 1)
                join(eng, 3 * LAYERS - 2)
                phase_b(LAYERS - 1, True)

            assert TRIPS - 1 == 1 + WQ // 2

            def blocks_of_a(eng, step):
                step(0, 0, 0, None, 0)
                step(0, 1, 1, None, 1)
                with eng.Fori(1, TRIPS - 1) as i:
                    step(i, 2 * i, 0, 2 * i - 2, None)
                    step(i, 2 * i + 1, 1, 2 * i - 1, None)
                step(TRIPS - 1, NB - 3, 0, None, None)
                step(TRIPS - 1, NB - 2, 1, None, None)
                step(TRIPS, NB - 1, 0, None, NB - 1)

            def uses(l, b_turn, u):
                return (SECOND if u else FIRST) * l + b_turn

            @block.sync
            def _(sp):
                slow = sp.value_load(slow_flag[0:1, 0:1], min_val=0, max_val=1)

                def load(b, u, use):
                    hold(sp, at_used[u], use + 1)
                    sp.dma_start(at_in_sb[:, u].rearrange("p s d -> p (s d)"),
                                 at_dram[bass.ds(b, 1)].rearrange("o p c -> p (o c)")).then_inc(at_in[u], 16)

                def load_both(b, n):
                    load(b, 0, n)
                    hold(sp, at_used[1], n + 1)
                    sp.dma_start(at_in_sb[:, 1].rearrange("p s d -> p (s d)").bitcast(BF16),
                                 at_upper_dram[bass.ds(b, 1)].rearrange("o p c -> p (o c)")).then_inc(at_in[1], 16)

                def load_first(l):
                    with sp.If(slow == 0):
                        load(0, 0, uses(l, 0, 0))
                        load(1, 1, uses(l, 0, 1))
                    with sp.Else():
                        load_both(0, NB * l)
                    sp.nop()

                def phase_a(l):
                    def weights(i, u, q):
                        hold(sp, w_split, WQ * l + q + 1)
                        sp.dma_start(stage[:, u], pieces[bass.ds(l, 1), bass.ds(q, 1)].rearrange("o k p f -> p (o k f)")
                                     ).then_inc(w_in_[u], 16)

                    def fast(i, b, u, q, end):
                        if end not in (0, 1):
                            load(b, u, uses(l, i, u))
                        if q is not None:
                            weights(i, u, q)

                    def general(i, b, u, q, end):
                        if end != 0:
                            load_both(b, NB * l + b)
                        if q is not None:
                            weights(i, u, q)

                    with sp.If(slow == 0):
                        blocks_of_a(sp, fast)
                    with sp.Else():
                        blocks_of_a(sp, general)
                    sp.nop()

                def phase_b(l, last):
                    def rows(X, first):
                        hold(sp, xT_done, X + 1)
                        sp.dma_start(x_rows[:], slot_x[bass.ds(first, TOK), :].rearrange("(s p) f -> p s f", p=P)
                                     ).then_inc(x_in2, 16)

                    if not last:
                        load_first(l + 1)
                    each_expert(sp, lambda e, t, p, G, S, pair, Y: rows(G + l, t * PAIR + (REGION * e + p * TOK)),
                                lambda pairs: rows(2 * pairs + l, XROWS - TOK))

                load_first(0)
                layers(phase_a, phase_b, lambda l: None, sp)

            @block.gpsimd
            def _(pool):
                pool.sem_inc(agg_free, AGG)
                nc.gpsimd.memset(pool_f[:], 0.0)
                for t in (sums[0], sums[1], tiles_before, strong_shift, plan_f):
                    nc.gpsimd.memset(t[:], 0.0)
                pool.drain()
                for p in range(2):
                    nc.gpsimd.dma_start(slot_y[YROWS - (2 - p) * P:YROWS - (1 - p) * P, :], y_sb[:, p, 0]
                                        ).then_inc(y_out[p], 16)
                    pool.wait_ge(y_out[p], 16)
                pool.sem_inc(zeroed, 1)

                def phase_a(l):
                    nc.gpsimd.dma_start(bias[:, 0:NWEAK, :], weak_b[bass.ds(l, 1)].to_broadcast([P, NWEAK, H])
                                        ).then_inc(small_in, 16)
                    nc.gpsimd.dma_start(bias[:, NWEAK:NE, :], b2[bass.ds(l, 1)].to_broadcast([P, NSTRONG, H])
                                        ).then_inc(small_in, 16)
                    nc.gpsimd.dma_start(b1_sb[:], b1[bass.ds(l, 1)].rearrange("o p u -> p (o u)")).then_inc(small_in, 16)

                    def scatter(b, v, rows=P):
                        n = NB * l + b
                        hold(pool, slot_ready, n + 1)
                        for k in range(2):
                            nc.gpsimd.indirect_dma_start(
                                out=slot_x[:], out_offset=bass.IndirectOffsetOnAxis(ap=slot_now[0:rows, v % 2, k:k + 1], axis=0),
                                in_=agg_out[0:rows, v], in_offset=None, bounds_check=XROWS - 1, oob_is_err=False
                                ).then_inc(scattered, 16)
                        hold(pool, scattered, 32 * (n + 1))
                        pool.sem_inc(agg_free, 1)

                    with pool.Fori(0, (NB - 1) // AGG) as i:
                        for v in range(AGG):
                            scatter(AGG * i + v, v)
                    scatter(NB - 1, 0, LROWS)

                def phase_b(l, last):
                    def store(e, t, p, G, S, pair, Y):
                        hold(pool, y_ready, 2 * G + 4)
                        nc.gpsimd.dma_start(slot_y[bass.ds(Y * PAIR + p * TOK, TOK), :].rearrange("(s p) f -> p s f", p=P),
                                            y_sb[:, p]).then_inc(y_out[p], 16)

                    def stored(pairs):
                        for p in range(2):
                            hold(pool, y_out[p], 16 * (pairs + 1))
                    each_expert(pool, store, stored)

                layers(phase_a, phase_b, lambda l: collect_all(pool, y_got, l), pool)

            @block.scalar
            def _(act):
                slow = act.value_load(slow_flag[0:1, 0:1], min_val=0, max_val=1)
                act.sem_inc(aT_ready, 2)
                act.sem_inc(hi_ready, KF)
                for u in range(2):
                    act.sem_inc(at_used[u], 1)

                def phase_a(l):
                    def weights(i, u, q):
                        hold(act, w_in_[u], 16 * (WQ // 2 * l + i))
                        nc.scalar.activation(w_hi[:, bass.ds(q, 1)].rearrange("p o f -> p (o f)"), stage[:, u],
                                             ACT.Copy).then_inc(w_hi_done, 1)

                    def convert(m, u, use, upper=False):
                        hold(act, at_in[u], 16 * (use + 1))
                        hold(act, pass_done, m + 1)
                        at = at_in_sb[:, u].rearrange("p s d -> p (s d)")
                        if upper:
                            at = at.bitcast(BF16)
                        for c in range(NB // SC):
                            cols = slice(c * SC * P, (c + 1) * SC * P)
                            last = nc.scalar.activation(at_r[:, u].rearrange("p s d -> p (s d)")[:, cols], at[:, cols],
                                                        ACT.Copy)
                            last.then_inc(at_ready, 1)
                        act.drain().then_inc(at_used[u], 1)

                    def transposed(b, u):
                        hold(act, aT_done, NB * l + b + 1)
                        nc.scalar.activation(aT[:, u].rearrange("p k n -> p (k n)"), bank[2 + u][:, 0:H], ACT.Copy
                                             ).then_inc(aT_ready, 1)

                    def exponentials(b):
                        act.wait_ge(dz_ready, NB * l + b + 1)
                        nc.scalar.activation(ex[:], dz[:], ACT.Exp).then_inc(ex_ready, 1)

                    def fast(i, b, u, q, end):
                        if end != 0:
                            transposed(b - 1, 1 - u)
                        if q is not None:
                            weights(i, u, q)
                        if end != NB - 1:
                            convert(NB * l + b + 1, 1 - u, uses(l, i + u, 1 - u))
                        if end != 0:
                            exponentials(b - 1)

                    def general(i, b, u, q, end):
                        n = NB * l + b
                        convert(2 * n, 0, n)
                        convert(2 * n + 1, 1, n, upper=True)
                        if end != 0:
                            transposed(b - 1, 1 - u)
                            exponentials(b - 1)
                        if q is not None:
                            weights(i, u, q)

                    with act.If(slow == 0):
                        convert(NB * l, 0, uses(l, 0, 0))
                        blocks_of_a(act, fast)
                    with act.Else():
                        blocks_of_a(act, general)
                    act.nop()
                    transposed(NB - 1, 0)
                    exponentials(NB - 1)

                def phase_b(l, last):
                    def upper(X, p):
                        act.wait_ge(xT_done, X + 2)
                        nc.scalar.activation(x_hi[:, p].rearrange("p k n -> p (k n)"), bank[x_bank[p]][:], ACT.Copy
                                             ).then_inc(xh_ready, 1)

                    def tile(e, t, p, G, S, pair, Y):
                        if e < NWEAK:
                            upper(G + l + 1, 1 - p)
                            return
                        for f in range(KF):
                            hold(act, unit_done, KF * S + f + 1)
                            act.wait_ge(lo_ready, KF * S + f + 1)
                            src = bank[unit_bank[f]][:, 0:TOK]
                            col = (e - NWEAK) * KF + f
                            nc.scalar.activation(v[:, f % 2], src, ACT.Relu, bias=b1_sb[:, col:col + 1])
                            nc.scalar.activation(act_hi[:, f], src, ACT.Relu, bias=b1_sb[:, col:col + 1]
                                                 ).then_inc(hi_ready, 1)
                        upper(G + l + 1, 1 - p)

                    hold(act, small_in, 48 * (l + 1))
                    upper(first_tile(act) + l, 0)
                    each_expert(act, tile)

                def phase_c(l):
                    in_pairs(act, lambda b, u, uses: keep_block(act, NB * (l + 1) + b, b, u))

                layers(phase_a, phase_b, phase_c, act)

            @block.vector
            def _(dve):
                dve.sem_inc(combined, GOT)
                dve.sem_inc(w_split, 2)
                dve.sem_inc(agg_ready, 2)
                dve.sem_inc(lg_taken, 1)
                dve.sem_inc(lo_ready, 2)
                dve.sem_inc(y_ready, 2)
                dve.wait_ge(zeroed, 1)

                def phase_a(l):
                    nc.vector.tensor_copy(next_slot[:], region_0[:])
                    dve.drain()

                    def weights(u, q):
                        hold(dve, w_hi_done, WQ * l + q + 1)
                        at = bass.ds(q, 1)
                        nc.vector.tensor_tensor(w_lo[:, at].rearrange("p o f -> p (o f)"), stage[:, u],
                                                w_hi[:, at].rearrange("p o f -> p (o f)"), ALU.subtract).then_inc(w_split, 1)

                    def mean(b, u):
                        n = NB * l + b
                        hold(dve, agg_done, n + 1)
                        hold(dve, agg_free, n + 1)
                        nc.vector.tensor_scalar(agg[:, u], bank[u][:, 0:H], rdeg[:, bass.ds(b, 1)], None, ALU.mult)
                        nc.vector.tensor_scalar(agg_out[:, bass.ds(b % AGG, 1)].rearrange("p o f -> p (o f)"),
                                                bank[u][:, 0:H], rdeg[:, bass.ds(b, 1)], None, ALU.mult
                                                ).then_inc(agg_ready, 1)

                    def choose(b, last=False):
                        n = NB * l + b
                        dve.wait_ge(lg_done, n + 1)
                        nc.vector.tensor_tensor(lg[:], bank[4][:, 0:NE1],
                                                h_logits[:, bass.ds(b, 1)].rearrange("p o e -> p (o e)"), ALU.add
                                                ).then_inc(lg_taken, 1)
                        dve.drain()
                        nc.vector.max(top[:], lg[:, 0:NE])
                        nc.vector.tensor_scalar(dz[:, 1:2], lg[:, NE:NE1], -1.0, None, ALU.mult)
                        dve.drain()
                        nc.vector.max_index(idx[:], top[:], lg[:, 0:NE])
                        nc.vector.tensor_tensor(dz[:, 0:1], top[:, 1:2], top[:, 0:1], ALU.subtract)
                        dve.drain().then_inc(dz_ready, 1)
                        nc.vector.tensor_copy(idx_f[:], idx[:, 0:2])
                        nc.vector.tensor_copy(idx_all[:, bass.ds(2 * b, 2)], idx[:, 0:2])
                        dve.drain()
                        nc.vector.tensor_tensor(hots[:], expert_no[:].unsqueeze(1).to_broadcast([P, 2, NE]),
                                                idx_f[:].unsqueeze(2).to_broadcast([P, 2, NE]), ALU.is_equal)
                        if last:
                            nc.vector.memset(member[:], 0.0)
                        dve.drain()
                        R = slice(0, LROWS if last else P)
                        nc.vector.tensor_tensor(member[R], hots[R, 0], hots[R, 1], ALU.add).then_inc(member_ready, 1)

                    def place(b, u):
                        n = NB * l + b
                        hold(dve, ex_ready, n + 1)
                        nc.vector.tensor_scalar(den[:], ex[:], 1.0, None, ALU.add)
                        dve.drain()
                        nc.vector.reciprocal(rec[:], den[:])
                        dve.drain()
                        nc.vector.tensor_tensor(gt[:, 0:1], rec[:, 0:1], rec[:, 1:2], ALU.mult)
                        hold(dve, rank_done, n + 1)
                        nc.vector.tensor_tensor(pos[:], bank[5][:, 0:NE], next_slot[:], ALU.add)
                        dve.drain()
                        nc.vector.tensor_tensor(gt[:, 1:2], gt[:, 0:1], ex[:, 0:1], ALU.mult)
                        nc.vector.tensor_tensor(prod[:], hots[:], pos[:].unsqueeze(1).to_broadcast([P, 2, NE]), ALU.mult)
                        nc.vector.tensor_tensor(next_slot[:], bank[5][:, NE:2 * NE], next_slot[:], ALU.add)
                        dve.drain()
                        nc.vector.tensor_reduce(slot_f[:], prod[:], AX.X, ALU.add)
                        nc.vector.tensor_copy(g_all[:, bass.ds(b, 1)].rearrange("p o k -> p (o k)"), gt[:])
                        dve.drain()
                        hold(dve, agg_free, n + AGG - 1)
                        nc.vector.tensor_copy(slot_now[:, u], slot_f[:])
                        nc.vector.tensor_copy(slots_f[:, bass.ds(2 * b, 2)], slot_f[:])
                        dve.drain().then_inc(slot_ready, 1)

                    def step(i, b, u, q, end):
                        mean(b, u)
                        if q is not None:
                            weights(u, q)
                        if end != 0:
                            place(b - 1, 1 - u)
                        choose(b, end == NB - 1)

                    blocks_of_a(dve, step)
                    place(NB - 1, 0)

                    nc.vector.tensor_tensor(taken[:], next_slot[:], region_0[:], ALU.subtract)
                    dve.drain()
                    nc.vector.tensor_scalar(taken_i[:], taken[:], float(PAIR - 1), None, ALU.add)
                    dve.drain()
                    nc.vector.tensor_scalar(taken_i[:], taken_i[:], PAIR.bit_length() - 1, None, ALU.logical_shift_right)
                    dve.drain()
                    nc.vector.tensor_scalar(plan_f[:, 0:NE], taken_i[:], 1.0, None, ALU.max)
                    dve.drain()
                    nc.vector.tensor_copy(sums[0][:, NE:2 * NE], plan_f[:, 0:NE])
                    dve.drain()
                    for k, step_ in enumerate((1, 2, 4)):
                        a, b = sums[k % 2], sums[(k + 1) % 2]
                        nc.vector.tensor_tensor(b[:, NE:2 * NE], a[:, NE:2 * NE], a[:, NE - step_:2 * NE - step_], ALU.add)
                        dve.drain()
                    s = sums[1]
                    nc.vector.tensor_scalar(plan_f[:, NE:2 * NE], s[:, NE - 1:2 * NE - 1], tiles_before[:, 0:1], None, ALU.add)
                    nc.vector.tensor_tensor(strong_shift[:], strong_shift[:], s[:, NE + NWEAK - 1:NE + NWEAK], ALU.add)
                    dve.drain()
                    nc.vector.tensor_copy(plan_f[:, 3 * NE:4 * NE], s[:, NE - 1:2 * NE - 1])
                    nc.vector.scalar_tensor_tensor(shift[:], s[:, NE - 1:2 * NE - 1], float(PAIR), region_0[:],
                                                   ALU.mult, ALU.subtract)
                    nc.vector.tensor_scalar(plan_f[:, 2 * NE + NWEAK:3 * NE], plan_f[:, NE + NWEAK:2 * NE],
                                            strong_shift[:, 0:1], None, ALU.subtract)
                    nc.vector.tensor_tensor(tiles_before[:], tiles_before[:], s[:, 2 * NE - 1:2 * NE], ALU.add)
                    dve.drain()
                    nc.vector.tensor_copy(plan[:], plan_f[0:1, :])
                    nc.vector.tensor_tensor(moved[:], expert_no[:].unsqueeze(1).to_broadcast([P, 2 * NB, NE]),
                                            idx_all[:].unsqueeze(2).to_broadcast([P, 2 * NB, NE]), ALU.is_equal)
                    dve.drain()
                    nc.vector.tensor_tensor(moved[:], moved[:], shift[:].unsqueeze(1).to_broadcast([P, 2 * NB, NE]), ALU.mult)
                    dve.drain()
                    nc.vector.tensor_reduce(idx_all[:], moved[:], AX.X, ALU.add)
                    dve.drain()
                    nc.vector.tensor_tensor(slots_all[:], slots_f[:], idx_all[:], ALU.add)

                def phase_b(l, last):
                    def lower(X, p):
                        hold(dve, xh_ready, X + 1)
                        nc.vector.tensor_tensor(x_lo[:, p].rearrange("p k n -> p (k n)"), bank[x_bank[p]][:],
                                                x_hi[:, p].rearrange("p k n -> p (k n)"), ALU.subtract
                                                ).then_inc(xl_ready, 1)

                    def results(e, G, p, pair):
                        hold(dve, y_out[p], 16 * (pair + 1))
                        for s in range(2):
                            hold(dve, y_done, 2 * G + s + 1)
                            i = nc.vector.tensor_tensor(y_sb[:, p, s], bank[3 + s][:, 0:H], bias[:, e], ALU.add)
                            if e < NWEAK:
                                dve.drain()
                                i = nc.vector.tensor_scalar(y_sb[:, p, s], y_sb[:, p, s], 0.0, None, ALU.max)
                            i.then_inc(y_ready, 1)

                    def tile(e, t, p, G, S, pair, Y):
                        if e >= NWEAK:
                            for f in range(KF):
                                hold(dve, hi_ready, KF * S + f + KF + 1)
                                nc.vector.tensor_tensor(act_lo[:, f], v[:, f % 2], act_hi[:, f], ALU.subtract
                                                        ).then_inc(lo_ready, 1)
                        lower(G + l + 1, 1 - p)
                        results(e, G, p, pair)

                    hold(dve, small_in, 48 * (l + 1))
                    lower(first_tile(dve) + l, 0)
                    each_expert(dve, tile)

                def phase_c(l):
                    def step(b, v, i, rows=P):
                        combine(dve, y_got, l, b, v, i, rows)
                        dve.drain().then_inc(combined, 1)
                        parts_of_block(dve, b, v % 2)
                    with dve.Fori(0, (NB - 1) // GOT) as i:
                        for v in range(GOT):
                            step(GOT * i + v, v, i)
                    step(NB - 1, 0, (NB - 1) // GOT, LROWS)

                layers(phase_a, phase_b, phase_c, dve)

            @block.tensor
            def _(pe):
                slow = pe.value_load(slow_flag[0:1, 0:1], min_val=0, max_val=1)
                pe.sem_inc(pass_done, 2)
                pe.sem_inc(xT_done, 1)

                def phase_a(l):
                    def transpose_mean(b, u):
                        n = NB * l + b
                        pe.wait_ge(agg_ready, n + 3)
                        hold(pe, aT_ready, n + 1)
                        for k in range(KH):
                            last = nc.tensor.transpose(bank[2 + u][:, k * P:(k + 1) * P], agg[:, u, k * P:(k + 1) * P],
                                                       identf[:])
                        last.then_inc(aT_done, 1)

                    def logits(b, u):
                        n = NB * l + b
                        hold(pe, aT_ready, n + 3)
                        hold(pe, lg_taken, n + 1)
                        for k in range(KH):
                            last = nc.tensor.matmul(bank[4][:, 0:NE1], aT[:, u, k, :],
                                                    route_sb[:, bass.ds(l, 1), KH + k, :].rearrange("p o e -> p (o e)"),
                                                    start=(k == 0), stop=(k == KH - 1))
                        last.then_inc(lg_done, 1)

                    def ranks(b):
                        hold(pe, member_ready, NB * l + b + 1)
                        nc.tensor.matmul(bank[5][:, 0:NE], before_b[:], member[:], start=True, stop=True)
                        nc.tensor.matmul(bank[5][:, NE:2 * NE], onesb[:], member[:], start=True, stop=True
                                         ).then_inc(rank_done, 1)

                    def aggregate(i, b, u, end, both):
                        n = NB * l + b
                        pe.wait_ge(agg_ready, n + 1)
                        passes = [(2 * n, 0), (2 * n + 1, 1)] if both else [(n, u)]
                        for a, (m, slot) in enumerate(passes):
                            for s in range(NB):
                                if s % SC == 0:
                                    hold(pe, at_ready, NB // SC * m + s // SC + 1)
                                for k, part in enumerate((h_hi, h_lo)):
                                    last = nc.tensor.matmul(bank[u][:, 0:H], at_r[:, slot, s, :], part[:, s, :],
                                                            start=(a + s + k == 0),
                                                            stop=(a == len(passes) - 1 and s == NB - 1 and k == 1))
                                if a == 0 and s == 1 and end not in (0, 1):
                                    ranks(b - 2)
                                elif a == 0 and s == 4 and end != 0:
                                    transpose_mean(b - 1, 1 - u)
                                elif a == 0 and s == 9 and end != 0:
                                    logits(b - 1, 1 - u)
                            pe.drain().then_inc(pass_done, 1)
                        pe.sem_inc(agg_done, 1)

                    with pe.If(slow == 0):
                        blocks_of_a(pe, lambda i, b, u, q, end: aggregate(i, b, u, end, False))
                    with pe.Else():
                        blocks_of_a(pe, lambda i, b, u, q, end: aggregate(i, b, u, end, True))
                    pe.nop()
                    ranks(NB - 2)
                    transpose_mean(NB - 1, 0)
                    logits(NB - 1, 0)
                    ranks(NB - 1)

                def phase_b(l, last):
                    def transposes(X, p):
                        hold(pe, x_in2, 16 * (X + 1))
                        for k in range(KH):
                            for s in range(2):
                                last = nc.tensor.transpose(bank[x_bank[p]][:, k * TOK + s * P:k * TOK + (s + 1) * P],
                                                           x_rows[:, s, k * P:(k + 1) * P], identf[:])
                        last.then_inc(xT_done, 1)

                    def tile(e, t, p, G, S, pair, Y):
                        X = G + l
                        pe.wait_ge(xl_ready, X + 1)
                        if e < NWEAK:
                            transposes(X + 1, 1 - p)
                            for s in range(2):
                                hold(pe, y_ready, 2 * G + s + 1)
                                terms = [(a, w, k) for k in range(KH)
                                         for a, w in ((x_hi[:, p], w_hi), (x_hi[:, p], w_lo), (x_lo[:, p], w_hi))]
                                for j, (a, w, k) in enumerate(terms):
                                    last = nc.tensor.matmul(bank[3 + s][:, 0:H], a[:, k, s * P:(s + 1) * P],
                                                            w[:, e, k * H:(k + 1) * H], start=(j == 0), stop=(j == 5))
                                last.then_inc(y_done, 1)
                            return
                        for f in range(KF):
                            hold(pe, hi_ready, KF * S + f + 1)
                            terms = [(w, a, k) for k in range(KH)
                                     for w, a in ((w_hi, x_hi[:, p]), (w_hi, x_lo[:, p]), (w_lo, x_hi[:, p]))]
                            for j, (w, a, k) in enumerate(terms):
                                last = nc.tensor.matmul(bank[unit_bank[f]][:, 0:TOK],
                                                        w[:, NWEAK + KH * (e - NWEAK) + k, f * P:(f + 1) * P],
                                                        a[:, k, :], start=(j == 0), stop=(j == 5))
                            last.then_inc(unit_done, 1)
                        transposes(X + 1, 1 - p)
                        for s in range(2):
                            hold(pe, y_ready, 2 * G + s + 1)
                            for f in range(KF):
                                if s == 0:
                                    hold(pe, lo_ready, KF * S + f + 3)
                                q = NWEAK + KH * NSTRONG + (e - NWEAK) * (KF // 2) + f // 2
                                cols = slice((f % 2) * H, (f % 2 + 1) * H)
                                for j, (a, w) in enumerate(((act_hi, w_hi), (act_lo, w_hi), (act_hi, w_lo))):
                                    last = nc.tensor.matmul(bank[3 + s][:, 0:H], a[:, f, s * P:(s + 1) * P],
                                                            w[:, q, cols], start=(f + j == 0),
                                                            stop=(f == KF - 1 and j == 2))
                            last.then_inc(y_done, 1)

                    transposes(first_tile(pe) + l, 0)
                    each_expert(pe, tile)

                def phase_c(l):
                    def step(b, u, uses):
                        n = NB * (l + 1) + b
                        transpose_block(pe, n, u)
                        logits_of_block(pe, n, u, l + 1)
                    in_pairs(pe, step)

                layers(phase_a, phase_b, phase_c, pe)

        with ExitStack() as c3:
            L = LAYERS - 1
            x_all = sb("x_out", [P, NB, OUT], F32, c3)
            y_got = sb("y_got", [P, GOT, 2, H], F32, c3)
            w_out_sb = sb("w_out_sb", [P, KH, OUT], F32, c3)
            b_out_sb = sb("b_out_sb", [P, OUT], F32, c3)
            o_in = sem("o_in")
            o_done = sem("o_done")
            o_ready = sem("o_ready")
            o_stored = sem("o_stored")
            block = c3.enter_context(nc.Block())
            GROUP = 6
            assert (NB - 1) % GROUP == 0

            @block.sync
            def _(sp):
                sp.dma_start(x_all[:, 0:NB - 1], x[0:(NB - 1) * P, :].rearrange("(b p) f -> p b f", p=P)).then_inc(o_in, 16)
                sp.dma_start(x_all[0:LROWS, NB - 1], x[(NB - 1) * P:N, :]).then_inc(o_in, 16)
                sp.dma_start(w_out_sb[:], w_out).then_inc(o_in, 16)
                sp.dma_start(b_out_sb[:], b_out.rearrange("(o f) -> o f", o=1).to_broadcast([P, OUT])).then_inc(o_in, 16)
                for g in range((NB - 1) // GROUP):
                    sp.wait_ge(o_ready, GROUP * (g + 1) + 2)
                    sp.dma_start(out[g * GROUP * P:(g + 1) * GROUP * P, :].rearrange("(b p) f -> p b f", p=P),
                                 x_all[:, g * GROUP:(g + 1) * GROUP]).then_inc(o_stored, 16)
                sp.wait_ge(o_ready, NB + 2)
                sp.dma_start(out[(NB - 1) * P:N, :], x_all[0:LROWS, NB - 1]).then_inc(o_stored, 16)
                sp.wait_ge(o_stored, 16 * ((NB - 1) // GROUP + 1))

            @block.gpsimd
            def _(pool):
                collect_all(pool, y_got, L)

            @block.scalar
            def _(act):
                def keep(b, u, uses):
                    n = NB * LAYERS + b
                    act.wait_ge(hT_done, n + 3)
                    act.wait_ge(o_ready, b + 1)
                    nc.scalar.activation(hT[:, u].rearrange("p k n -> p (k n)"), bank[6 + u][:, 0:H], ACT.Copy
                                         ).then_inc(hT_ready, 1)
                in_pairs(act, keep)

            @block.vector
            def _(dve):
                dve.sem_inc(o_ready, 2)
                dve.wait_ge(o_in, 64)
                for b in range(NB):
                    R = slice(0, LROWS if b == NB - 1 else P)
                    nc.vector.tensor_tensor(x_all[R, b], x_all[R, b], b_out_sb[R], ALU.add)
                dve.drain()

                def finish(b, u, rows=P):
                    hold(dve, o_done, b + 1)
                    at = x_all[0:rows, bass.ds(b, 1)].rearrange("p o f -> p (o f)")
                    nc.vector.tensor_tensor(at, at, bank[4 + u][0:rows, 0:OUT], ALU.add).then_inc(o_ready, 1)

                def step(b, v, i, rows=P):
                    combine(dve, y_got, L, b, v, i, rows)
                    dve.drain().then_inc(combined, 1)

                for v in range(GOT):
                    step(v, v, 0)
                    if v:
                        finish(v - 1, (v - 1) % 2)
                with dve.Fori(1, (NB - 1) // GOT) as i:
                    for v in range(GOT):
                        step(GOT * i + v, v, i)
                        finish(GOT * i + v - 1, (v - 1) % 2)
                step(NB - 1, 0, (NB - 1) // GOT, LROWS)
                finish(NB - 2, 1)
                finish(NB - 1, 0, LROWS)

            @block.tensor
            def _(pe):
                pe.wait_ge(o_in, 64)

                def project(b, u, uses):
                    n = NB * LAYERS + b
                    transpose_block(pe, n, u)
                    pe.wait_ge(hT_ready, n + 3)
                    hold(pe, o_ready, b + 1)
                    for k in range(KH):
                        last = nc.tensor.matmul(bank[4 + u][:, 0:OUT], hT[:, u, k, :], w_out_sb[:, k, :],
                                                start=(k == 0), stop=(k == KH - 1))
                    last.then_inc(o_done, 1)
                in_pairs(pe, project)


def kernel(**inputs):
    import numpy as np
    import concourse.bacc as bacc
    from concourse.bass_utils import run_bass_kernel_spmd

    a = {k.replace("L0_gnn_", ""): np.asarray(v) for k, v in inputs.items()}
    L, NS, H, F = a["strong_W1"].shape
    NW = a["weak_W"].shape[1]
    NE = NW + NS
    conf = np.concatenate([a["conf_W"], np.zeros_like(a["conf_W"])], axis=1)
    route_w = np.concatenate([a["router_W"], conf], axis=2).reshape(L, 2 * H // P, P, NE + 1).transpose(0, 2, 1, 3)
    route_b = np.concatenate([a["router_b"], a["conf_b"]], axis=1)
    weak = a["weak_W"].reshape(L, NW, 2, P, H).transpose(0, 1, 3, 2, 4).reshape(L, NW, P, 2 * H)
    first = a["strong_W1"].reshape(L, NS * 2, P, F)
    second = a["strong_W2"].reshape(L, NS * F // (2 * P), 2, P, H).transpose(0, 1, 3, 2, 4).reshape(L, -1, P, 2 * H)
    arrays = {
        "x": a["x"],
        "edges": np.stack([a["src"], a["dst"]], axis=1),
        "dst": a["dst"],
        "w_in": a["W_in"],
        "b_in": a["b_in"],
        "route_w": route_w,
        "route_b": route_b,
        "pieces": np.concatenate([weak, first, second], axis=1),
        "weak_b": a["weak_b"],
        "b1": a["strong_b1"].reshape(L, -1, P).transpose(0, 2, 1),
        "b2": a["strong_b2"],
        "w_out": a["W_out"].reshape(H // P, P, -1).transpose(1, 0, 2),
        "b_out": a["b_out"],
    }
    arrays = {f"in_{k}": np.ascontiguousarray(v) for k, v in arrays.items()}
    nc = bacc.Bacc("TRN2", target_bir_lowering=False, num_devices=1)
    args = [nc.dram_tensor(k, v.shape, mybir.dt.from_np(v.dtype), kind="ExternalInput").ap() for k, v in arrays.items()]
    args.append(nc.dram_tensor("out_0", a["x"].shape, mybir.dt.float32, kind="ExternalOutput").ap())
    gnn_program(nc, *args)
    r = run_bass_kernel_spmd(nc, [arrays], core_ids=[0])
    return r.results[0]["out_0"]
```

```python
import concourse.bass as bass
from concourse import mybir
from contextlib import ExitStack

F32 = mybir.dt.float32
F32R = mybir.dt.float32r
BF16 = mybir.dt.bfloat16
F16 = mybir.dt.float16
I32 = mybir.dt.int32
U32 = mybir.dt.uint32
ACT = mybir.ActivationFunctionType
ALU = mybir.AluOpType
AX = mybir.AxisListType

P = 128
EPS = 1e-5


def gnn_program(nc, x, edges, dst, w_in, b_in, route_w, route_b, pieces, weak_b, b1, b2, w_out, b_out, out):
    N, IN = x.shape
    E = edges.shape[0]
    LAYERS, _, KR, NE1 = route_w.shape
    NE = NE1 - 1
    NWEAK = weak_b.shape[1]
    NSTRONG = NE - NWEAK
    WQ = pieces.shape[1]
    KH = KR // 2
    H = KH * P
    KF = b1.shape[2] // NSTRONG
    OUT = w_out.shape[2]
    NB = (N + P - 1) // P
    LROWS = N - (NB - 1) * P
    WIN = 16
    CH = 5
    CAP = CH * P
    GROUPS = (N + WIN - 1) // WIN
    GP = P // WIN
    GBODY = 2 * GP
    SLOTS = GBODY * CH
    MW = NB * WIN
    ROWS = 125
    ROWLEN = E // ROWS
    TOK = 2 * P
    PAIR = 2 * TOK
    REGION = -(-N // PAIR) * PAIR
    TRIPS = (NB - 1) // 2
    XR = -(-(NE * REGION + TOK) // (2 * TRIPS * P))
    XROWS = XR * 2 * TRIPS * P
    LPAIRS = (2 * N + NE * (PAIR - 1)) // PAIR
    YR = -(-(LPAIRS * PAIR + TOK) // (2 * TRIPS * P))
    YROWS = YR * 2 * TRIPS * P
    assert ROWS * ROWLEN == E and NB % 2 == 1 and KH == 2 and WQ <= 2 * TRIPS and WQ % 2 == 0

    at_dram = nc.dram_tensor("at_scratch", (NB, P, NB * P), F16)
    starts_dram = nc.dram_tensor("starts_scratch", (2 * P,), I32)
    at_upper_dram = nc.dram_tensor("at_upper_scratch", (NB, P, NB * P), BF16)
    slot_x = nc.dram_tensor("slot_inputs", (XROWS, H), F32)
    slot_y = nc.dram_tensor("slot_results", (YROWS, H), F32)

    with ExitStack() as ctx:
        def sb(name, shape, dt, c=ctx):
            return c.enter_context(nc.sbuf_tensor(name, list(shape), dt))

        def sem(name):
            return ctx.enter_context(nc.semaphore(name))

        h_hi = sb("h_hi", [P, NB, H], F32R)
        h_lo = sb("h_lo", [P, NB, H], F32R)
        h_logits = sb("h_logits", [P, NB, NE1], F32)
        rdeg = sb("rdeg", [P, NB], F32)
        route_sb = sb("route_sb", [P, LAYERS, KR, NE1], F32)
        route_b_sb = sb("route_b_sb", [1, LAYERS, NE1], F32)
        identf = sb("identf", [P, P], F32)
        onesb = sb("onesb", [P, P], BF16)
        before_b = sb("before_b", [P, P], BF16)
        ones_row = sb("ones_row", [1, P], F32)
        expert_no = sb("expert_no", [P, NE], F32)
        region_0 = sb("region_0", [P, NE], F32)
        slow_flag = sb("slow_flag", [1, 1], I32)
        h_new = sb("h_new", [P, 2, H], F32)
        hT = sb("hT", [P, 2, KH, P], F32)
        bank = [ctx.enter_context(nc.psum_tensor(f"bank{i}", [P, 512], F32)) for i in range(8)]

        held = sem("held")

        def hold(eng, s, value):
            eng.wait_ge(s, value)
            eng.sem_inc(held, 1)

        new_ready = sem("new_ready")
        hi_kept = sem("hi_kept")
        hT_done = sem("hT_done")
        hT_ready = sem("hT_ready")
        hl_done = sem("hl_done")
        hl_kept = sem("hl_kept")

        def pool_chunks(gi):
            return 2 + gi % 2

        def parts_of_block(dve, b, u):
            hi, lo = (t[:, bass.ds(b, 1)].rearrange("p o f -> p (o f)") for t in (h_hi, h_lo))
            nc.vector.tensor_copy(hi, h_new[:, u])
            dve.drain()
            nc.vector.tensor_tensor(lo, h_new[:, u], hi, ALU.subtract)

        def keep_transpose(act, n, u):
            act.wait_ge(hT_done, n + 3)
            hold(act, hl_done, n + 1)
            nc.scalar.activation(hT[:, u].rearrange("p k n -> p (k n)"), bank[6 + u][:, 0:H], ACT.Copy
                                 ).then_inc(hT_ready, 1)

        def keep_logits(act, n, b, u):
            hold(act, hl_done, n + 3)
            nc.scalar.activation(h_logits[:, bass.ds(b, 1)].rearrange("p o e -> p (o e)"),
                                 bank[4 + u][:, 0:NE1], ACT.Copy).then_inc(hl_kept, 1)

        def transpose_block(pe, n, u):
            pe.wait_ge(new_ready, n + 1)
            pe.wait_ge(hT_ready, n + 1)
            for k in range(KH):
                last = nc.tensor.transpose(bank[6 + u][:, k * P:(k + 1) * P], h_new[:, u, k * P:(k + 1) * P], identf[:])
            last.then_inc(hT_done, 1)

        def logits_of_block(pe, n, u, layer):
            pe.wait_ge(hT_ready, n + 3)
            hold(pe, hl_kept, n + 1)
            for k in range(KH):
                nc.tensor.matmul(bank[4 + u][:, 0:NE1], hT[:, u, k, :],
                                 route_sb[:, bass.ds(layer, 1), k, :].rearrange("p o e -> p (o e)"),
                                 start=(k == 0), stop=False)
            nc.tensor.matmul(bank[4 + u][:, 0:NE1], ones_row[:],
                             route_b_sb[:, bass.ds(layer, 1)].rearrange("p o e -> p (o e)"), start=False, stop=True
                             ).then_inc(hl_done, 1)

        with ExitStack() as c1:
            def sb1(name, shape, dt):
                return sb(name, shape, dt, c1)

            x_all = sb1("x_all", [P, NB, IN], F32)
            stats = sb1("stats", [P, NB, 6], F32)
            mv = sb1("mv", [P, NB, 2], F32)
            std = sb1("std", [P, NB], F32)
            rstd = sb1("rstd", [P, NB], F32)
            epsc = sb1("epsc", [P, 1], F32)
            h0 = sb1("h0", [P, 2, P], F32)
            w_in_sb = sb1("w_in_sb", [P, H], F32)
            b_in_sb = sb1("b_in_sb", [P, H], F32)
            iota_s = sb1("iota_s", [P, P], F16)
            iota_m = sb1("iota_m", [P, MW], F16)
            gidx = sb1("gidx", [P, GROUPS, CH], F32)
            thr = sb1("thr", [P, 2 * P], F32)
            thrcol = sb1("thrcol", [P, 2], F32)
            ones1 = sb1("ones1", [P, 1], F32)
            last_i = sb1("last_i", [P, 1], I32)
            last_f = sb1("last_f", [P, 1], F32)
            before = sb1("before", [P, 2 * P], F32)
            full_rows = sb1("full_rows", [P, 2], F32)
            row_idx = sb1("row_idx", [P, 2], U32)
            rows_i = sb1("rows_i", [P, 2, ROWLEN], I32)
            rows_f = sb1("rows_f", [P, 2, ROWLEN], F32)
            cnt = sb1("cnt", [P, 2], F32)
            start_f = sb1("start_f", [P, 2], F32)
            start_i = sb1("start_i", [P, 2], I32)
            start_row = sb1("start_row", [1, 2 * P], I32)
            ed = sb1("ed", [P, 2, SLOTS, 2], I32)
            src_hi = sb1("src_hi", [P, SLOTS], I32)
            src_lo = sb1("src_lo", [P, SLOTS], I32)
            dst_lo = sb1("dst_lo", [P, SLOTS], I32)
            dst_hi = sb1("dst_hi", [P, SLOTS], I32)
            col = sb1("col", [P, SLOTS], F32)
            valid = sb1("valid", [P, SLOTS], F32)
            key_m = sb1("key_m", [P, 2, SLOTS], F32)
            key_s = sb1("key_s", [P, 2, SLOTS], F32)
            key_s16 = sb1("key_s16", [P, 2, SLOTS], F16)
            vsum = sb1("vsum", [P, 1], F32)
            vtotal = sb1("vtotal", [P, 1], F32)
            oh_s = sb1("oh_s", [P, 4, CH, P], F16)
            oh_m = sb1("oh_m", [P, 2, CH, MW], F16)
            piece = sb1("piece", [P, 2, NB, P], F16)
            zero = sb1("zero", [P, H], F32)
            junk = sb1("junk", [P, ROWLEN], F32)

            s_const = sem("s_const")
            s_zero = sem("s_zero")
            s_cleared = sem("s_cleared")
            s_wait = sem("s_wait")
            s_last = sem("s_last")
            x_in = sem("x_in")
            var_ready = sem("var_ready")
            std_ready = sem("std_ready")
            y_ready = sem("y_ready")
            yT_done = sem("yT_done")
            h0_ready = sem("h0_ready")
            proj_done = sem("proj_done")
            before_ready = sem("before_ready")
            full_done = sem("full_done")
            idx_ready = sem("idx_ready")
            rows_in = [sem("rows_in0"), sem("rows_in1")]
            start_ready = sem("start_ready")
            start_out = sem("start_out")
            start_in = sem("start_in")
            ed_in = [sem("ed_in0"), sem("ed_in1")]
            keys_ready = sem("keys_ready")
            hot_s_ready = sem("hot_s_ready")
            hot_m_ready = sem("hot_m_ready")
            win_done = sem("win_done")
            win_evac = sem("win_evac")
            deg_done = sem("deg_done")
            rdeg_ready = sem("rdeg_ready")
            at_stored = [sem("at_stored0"), sem("at_stored1")]
            piece_free = sem("piece_free")
            vtotal_ready = sem("vtotal_ready")
            vsum_done = sem("vsum_done")
            flag_ready = sem("flag_ready")

            block = c1.enter_context(nc.Block())
            LASTG = GROUPS - 2 * TRIPS * GP
            BODIES = TRIPS

            @block.sync
            def _(sp):
                sp.dma_start(x_all[:, 0:NB - 1], x[0:(NB - 1) * P, :].rearrange("(b p) f -> p b f", p=P)).then_inc(x_in, 16)
                sp.wait_ge(s_zero, 1)
                sp.dma_start(x_all[0:LROWS, NB - 1], x[(NB - 1) * P:N, :]).then_inc(x_in, 16)
                with nc.allow_non_contiguous_dma(reason="one word a row"):
                    sp.dma_start(last_i[0:ROWS, :], dst.rearrange("(p k) -> p k", p=ROWS)[:, ROWLEN - 1:ROWLEN]
                                 ).then_inc(s_last, 16)
                sp.dma_start(w_in_sb[:], w_in).then_inc(s_wait, 16)
                sp.dma_start(b_in_sb[:], b_in.rearrange("(o f) -> o f", o=1).to_broadcast([P, H])).then_inc(s_wait, 16)
                sp.dma_start(route_sb[:], route_w.rearrange("l p k e -> p l k e")).then_inc(s_wait, 16)
                sp.dma_start(route_b_sb[:], route_b.rearrange("(o l) e -> o l e", o=1)).then_inc(s_wait, 16)

                sp.wait_ge(start_ready, 1)
                for k in range(2):
                    sp.dma_start(starts_dram[k * P:(k + 1) * P].rearrange("(p o) -> p o", o=1),
                                 start_i[:, k:k + 1]).then_inc(start_out, 16)
                sp.wait_ge(start_out, 32)
                sp.dma_start(start_row[:, :], starts_dram[:].rearrange("(o g) -> o g", o=1)).then_inc(start_in, 16)
                sp.wait_ge(start_in, 16)

                def fetch(b, par, count):
                    hold(sp, keys_ready, b + 1)
                    with sp.Fori(0, count) as g:
                        first = sp.value_load(start_row[0:1, bass.ds(b * GBODY + g, 1)], min_val=0, max_val=E - CAP)
                        sp.dma_start(ed[:, par, bass.ds(g * CH, CH), :],
                                     edges[bass.ds(first, CAP), :].rearrange("(p k) two -> p k two", k=CH)
                                     ).then_inc(ed_in[par], 16)

                def store(k, slot, uses):
                    hold(sp, rdeg_ready, k + 3)
                    sp.dma_start(at_dram[bass.ds(k, 1)].rearrange("o p c -> p (o c)"),
                                 piece[:, slot].rearrange("p s d -> p (s d)")).then_inc(at_stored[slot], 16)
                    hold(sp, at_stored[slot], 16 * uses)
                    sp.sem_inc(piece_free, 1)

                sp.sem_inc(piece_free, 2)
                fetch(0, 0, GBODY // 2)
                fetch(1, 1, GBODY // 2)
                with sp.Fori(0, BODIES // 2 - 1) as i:
                    for par in range(2):
                        store(4 * i + 2 * par, 0, 2 * i + par + 1)
                        hold(sp, ed_in[par], 16 * GBODY * (i + 1))
                        fetch(2 * i + 2 + par, par, GBODY // 2)
                        store(4 * i + 2 * par + 1, 1, 2 * i + par + 1)
                for par in range(2):
                    store(NB - 5 + 2 * par, 0, BODIES - 1 + par)
                    if par == 0:
                        sp.wait_ge(ed_in[0], 16 * GBODY * (BODIES // 2))
                        fetch(BODIES, 0, LASTG)
                    store(NB - 4 + 2 * par, 1, BODIES - 1 + par)
                store(NB - 1, 0, BODIES + 1)

            @block.gpsimd
            def _(pool):
                nc.gpsimd.memset(zero[:], 0.0)
                nc.gpsimd.memset(x_all[:, NB - 1], 0.0)
                pool.drain().then_inc(s_zero, 1)
                nc.gpsimd.memset(identf[:], 0.0)
                nc.gpsimd.memset(onesb[:], 1.0)
                nc.gpsimd.memset(before_b[:], 1.0)
                nc.gpsimd.memset(ones_row[:], 1.0)
                nc.gpsimd.memset(ones1[:], 1.0)
                nc.gpsimd.memset(epsc[:], EPS)
                nc.gpsimd.memset(piece[:], 0.0)
                nc.gpsimd.memset(last_f[:], 1e9)
                nc.gpsimd.memset(vtotal[:], 0.0)
                for tile, pattern, base, per_row in (
                        (iota_s, [[1, P]], 0, 0), (iota_m, [[1, MW]], 1, 0),
                        (gidx, [[1, GROUPS], [0, CH]], 0, 0), (thr, [[WIN, 2 * P]], 0, 0),
                        (thrcol, [[WIN * P, 2]], 0, WIN), (expert_no, [[1, NE]], 0, 0),
                        (region_0, [[REGION, NE]], 0, 0)):
                    nc.gpsimd.iota(tile[:], pattern=pattern, base=base, channel_multiplier=per_row,
                                   allow_small_or_imprecise_dtypes=True)
                pool.drain()
                nc.gpsimd.affine_select(out=identf[:], in_=identf[:], compare_op=ALU.not_equal, fill=1.0,
                                        base=0, pattern=[[-1, P]], channel_multiplier=1)
                nc.gpsimd.affine_select(out=before_b[:], in_=before_b[:], compare_op=ALU.is_gt, fill=0.0,
                                        base=0, pattern=[[1, P]], channel_multiplier=-1)
                pool.drain().then_inc(s_const, 1)
                pool.wait_ge(idx_ready, 1)
                for k in range(2):
                    nc.gpsimd.indirect_dma_start(
                        out=rows_i[:, k, :], out_offset=None, in_=dst.rearrange("(p k) -> p k", p=ROWS),
                        in_offset=bass.IndirectOffsetOnAxis(ap=row_idx[:, k:k + 1], axis=0),
                        bounds_check=ROWS - 1, oob_is_err=False).then_inc(rows_in[k], 16)

                def one_hots(n, gi, par):
                    hold(pool, win_done, n + 1)
                    for c in range(pool_chunks(gi)):
                        s = gi * CH + c
                        last = nc.gpsimd.tensor_scalar(oh_s[:, gi % 4, c], iota_s[:], key_s[:, par, s:s + 1], None,
                                                       ALU.is_equal)
                    last.then_inc(hot_s_ready, 1)

                with pool.Fori(0, BODIES // 2) as i:
                    for par in range(2):
                        hold(pool, keys_ready, 2 * i + par + 3)
                        for gi in range(GBODY):
                            one_hots((2 * i + par) * GBODY + gi, gi, par)
                hold(pool, keys_ready, BODIES + 3)
                for gi in range(LASTG):
                    one_hots(BODIES * GBODY + gi, gi, 0)

            @block.scalar
            def _(act):
                act.sem_inc(win_evac, 4)
                act.sem_inc(hT_ready, 2)
                act.sem_inc(hl_kept, 2)
                act.sem_inc(h0_ready, 2)
                act.wait_ge(s_const, 1)
                act.wait_ge(var_ready, 1)
                nc.scalar.activation(std[:], mv[:, :, 1], ACT.Sqrt, bias=epsc[:, 0:1]).then_inc(std_ready, 1)

                def relu(b):
                    act.wait_ge(yT_done, b + 1)
                    act.wait_ge(proj_done, b + 1)
                    nc.scalar.activation(h0[:, b % 2], bank[b % 2][:, 0:P], ACT.Relu).then_inc(h0_ready, 1)

                for b in range(NB + 3):
                    if b < NB:
                        relu(b)
                    if 2 <= b < NB + 2:
                        keep_transpose(act, b - 2, b % 2)
                    if b >= 3:
                        keep_logits(act, b - 3, b - 3, (b - 3) % 2)

                def evacuate(n, gi, slot):
                    act.wait_ge(win_done, n + 5)
                    nc.scalar.activation(piece[:, slot, :, (gi % GP) * WIN:(gi % GP + 1) * WIN],
                                         bank[gi % 4][:, 0:MW].rearrange("p (s d) -> p s d", d=WIN),
                                         ACT.Copy).then_inc(win_evac, 1)

                def clear(slots, per, k):
                    act.dma_start(slots[bass.ds(k * per * P, per * P), :].rearrange("(p r) f -> p r f", p=P),
                                  zero[:].unsqueeze(1).to_broadcast([P, per, H])).then_inc(s_cleared, 16)

                def fetch(b, par, g):
                    first = act.value_load(start_row[0:1, bass.ds(b * GBODY + g, 1)], min_val=0, max_val=E - CAP)
                    act.dma_start(ed[:, par, g * CH:(g + 1) * CH, :],
                                  edges[bass.ds(first, CAP), :].rearrange("(p k) two -> p k two", k=CH)
                                  ).then_inc(ed_in[par], 16)

                act.wait_ge(start_in, 16)
                for par in range(2):
                    for g in range(GBODY // 2, GBODY):
                        fetch(par, par, g)

                def turn(b, par, more):
                    if more:
                        hold(act, keys_ready, b + 3)
                    for k in range(2):
                        clear(slot_x, XR, 2 * b + k)
                        clear(slot_y, YR, 2 * b + k)
                        act.wait_ge(piece_free, 2 * b + k + 1)
                        for gi in range(GP):
                            if more and gi % 2:
                                fetch(b + 2, par, GBODY // 2 + (k * GP + gi) // 2)
                            evacuate((2 * b + k) * GP + gi, gi, k)

                with act.Fori(0, BODIES // 2 - 1) as i:
                    for par in range(2):
                        turn(2 * i + par, par, True)
                for par in range(2):
                    turn(BODIES - 2 + par, par, False)
                act.wait_ge(piece_free, NB)
                for gi in range(LASTG):
                    evacuate(2 * BODIES * GP + gi, gi, 0)
                act.wait_ge(s_cleared, 4 * BODIES * 16)

            @block.vector
            def _(dve):
                dve.sem_inc(keys_ready, 2)
                dve.sem_inc(rdeg_ready, 2)
                dve.wait_ge(x_in, 32)
                for b in range(NB):
                    nc.vector.bn_stats(stats[:, b, :], x_all[:, b, :])
                dve.drain()
                for b in range(NB):
                    nc.vector.bn_aggr(mv[:, b, :], stats[:, b, :])
                dve.drain().then_inc(var_ready, 1)

                dve.wait_ge(s_const, 1)
                dve.wait_ge(s_last, 16)
                nc.vector.tensor_copy(last_f[0:ROWS, :], last_i[0:ROWS, :])
                dve.drain()
                nc.vector.tensor_scalar(before[:], thr[:], last_f[:, 0:1], None, ALU.is_gt).then_inc(before_ready, 1)
                dve.wait_ge(full_done, 1)
                nc.vector.tensor_copy(full_rows[:], bank[3][:, 0:2])
                dve.drain()
                nc.vector.tensor_scalar(row_idx[:], full_rows[:], float(ROWS - 1), None, ALU.min).then_inc(idx_ready, 1)

                dve.wait_ge(std_ready, 1)
                nc.vector.reciprocal(rstd[:], std[:])
                dve.drain()
                for b in range(NB):
                    nc.vector.tensor_scalar(x_all[:, b, :], x_all[:, b, :], mv[:, b, 0:1], rstd[:, b:b + 1],
                                            ALU.subtract, ALU.mult).then_inc(y_ready, 1)

                for k in range(2):
                    dve.wait_ge(rows_in[k], 16)
                    nc.vector.tensor_copy(rows_f[:, k], rows_i[:, k])
                    dve.drain()
                    nc.vector.tensor_scalar(junk[:], rows_f[:, k], thrcol[:, k:k + 1], None, ALU.is_lt, ALU.add,
                                            accum_out=cnt[:, k:k + 1])
                    dve.drain()
                nc.vector.scalar_tensor_tensor(start_f[:], full_rows[:], float(ROWLEN), cnt[:], ALU.mult, ALU.add)
                dve.drain()
                nc.vector.tensor_scalar(start_i[:], start_f[:], float(E - CAP), None, ALU.min).then_inc(start_ready, 1)

                dve.wait_ge(s_wait, 64)
                for b in range(NB):
                    dve.wait_ge(proj_done, b + 3)
                    dve.wait_ge(hT_done, b + 1)
                    nc.vector.tensor_tensor(h_new[:, b % 2], bank[2 + b % 2][:, 0:H], b_in_sb[:], ALU.add
                                            ).then_inc(new_ready, 1)
                    dve.drain()
                    parts_of_block(dve, b, b % 2)

                def keys(b, par, n):
                    e = ed[:, par, 0:n, :]
                    nc.vector.tensor_scalar(src_hi[:, 0:n], e[:, :, 0], 3, 0xFFF0, ALU.logical_shift_right,
                                            ALU.bitwise_and)
                    nc.vector.tensor_scalar(dst_lo[:, 0:n], e[:, :, 1], WIN - 1, None, ALU.bitwise_and)
                    nc.vector.tensor_scalar(dst_hi[:, 0:n], e[:, :, 1], 4, None, ALU.logical_shift_right)
                    nc.vector.tensor_scalar(src_lo[:, 0:n], e[:, :, 0], P - 1, None, ALU.bitwise_and)
                    dve.drain()
                    nc.vector.tensor_tensor(col[:, 0:n], src_hi[:, 0:n], dst_lo[:, 0:n], ALU.add)
                    nc.vector.tensor_tensor(valid[:, 0:n], dst_hi[:, 0:n],
                                            gidx[:].rearrange("p g c -> p (g c)")[:, bass.ds(b * SLOTS, n)],
                                            ALU.is_equal)
                    nc.vector.tensor_copy(key_s[:, par, 0:n], src_lo[:, 0:n])
                    nc.vector.tensor_copy(key_s16[:, par, 0:n], src_lo[:, 0:n])
                    dve.drain().then_inc(keys_ready, 1)
                    nc.vector.scalar_tensor_tensor(key_m[:, par, 0:n], col[:, 0:n], 1.0, valid[:, 0:n], ALU.add, ALU.mult)
                    nc.vector.tensor_reduce(vsum[:], valid[:, 0:n], AX.X, ALU.add)
                    dve.drain()
                    nc.vector.tensor_tensor(vtotal[:], vtotal[:], vsum[:], ALU.add)
                    dve.drain()

                def one_hots(n, gi, par):
                    dve.wait_ge(win_done, n + 3)
                    p = pool_chunks(gi)
                    w = slice(gi * CH + p, (gi + 1) * CH)
                    nc.vector.tensor_tensor(oh_s[:, gi % 4, p:CH], iota_s[:].unsqueeze(1).to_broadcast([P, CH - p, P]),
                                            key_s16[:, par, w].unsqueeze(2).to_broadcast([P, CH - p, P]), ALU.is_equal)
                    for c in range(CH):
                        s = gi * CH + c
                        last = nc.vector.tensor_scalar(oh_m[:, gi % 2, c], iota_m[:], key_m[:, par, s:s + 1], None,
                                                       ALU.is_equal)
                    last.then_inc(hot_m_ready, 1)

                def reciprocal_degree(k, slot):
                    dve.wait_ge(deg_done, k + 3)
                    nc.vector.tensor_scalar(rdeg[:, bass.ds(k, 1)], bank[4 + slot][:, 0:1], 1.0, None, ALU.max)
                    dve.drain()
                    nc.vector.reciprocal(rdeg[:, bass.ds(k, 1)], rdeg[:, bass.ds(k, 1)]).then_inc(rdeg_ready, 1)

                def turn(i, par, first=False, last=False):
                    for gi in range(GBODY):
                        one_hots((2 * i + par) * GBODY + gi, gi, par)
                        if gi == 1 and not first:
                            reciprocal_degree(4 * i + 2 * par - 1, 1)
                        elif gi == GP + 1:
                            reciprocal_degree(4 * i + 2 * par, 0)
                        elif gi == GBODY - 4:
                            if par == 0:
                                dve.wait_ge(ed_in[1], 16 * GBODY * (i + 1))
                                keys(2 * i + 1, 1, SLOTS)
                            elif last:
                                dve.wait_ge(ed_in[0], 16 * (GBODY * (BODIES // 2) + LASTG))
                                keys(BODIES, 0, LASTG * CH)
                            else:
                                dve.wait_ge(ed_in[0], 16 * GBODY * (i + 2))
                                keys(2 * i + 2, 0, SLOTS)

                dve.wait_ge(ed_in[0], 16 * GBODY)
                keys(0, 0, SLOTS)
                turn(0, 0, first=True)
                turn(0, 1)
                with dve.Fori(1, BODIES // 2 - 1) as i:
                    for par in range(2):
                        turn(i, par)
                turn(BODIES // 2 - 1, 0)
                turn(BODIES // 2 - 1, 1, last=True)
                for gi in range(LASTG):
                    one_hots(BODIES * GBODY + gi, gi, 0)
                    if gi == 1:
                        reciprocal_degree(NB - 2, 1)
                reciprocal_degree(NB - 1, 0)
                dve.drain().then_inc(vtotal_ready, 1)
                dve.wait_ge(vsum_done, 1)
                nc.vector.tensor_scalar(slow_flag[:], bank[6][0:1, 0:1], float(E), None, ALU.not_equal
                                        ).then_inc(flag_ready, 1)

            @block.tensor
            def _(pe):
                pe.sem_inc(win_done, 4)
                pe.sem_inc(proj_done, 2)
                pe.sem_inc(hT_done, 2)
                pe.sem_inc(hl_done, 2)
                pe.sem_inc(deg_done, 2)
                pe.wait_ge(s_const, 1)
                pe.wait_ge(before_ready, 1)
                for k in range(2):
                    last = nc.tensor.matmul(bank[3][:, k:k + 1], before[:, k * P:(k + 1) * P], ones1[:],
                                            start=True, stop=True)
                last.then_inc(full_done, 1)

                def transpose_x(b):
                    pe.wait_ge(y_ready, b + 1)
                    pe.wait_ge(h0_ready, b + 1)
                    nc.tensor.transpose(bank[b % 2][:, 0:P], x_all[:, b, :], identf[:]).then_inc(yT_done, 1)

                def project(b):
                    pe.wait_ge(h0_ready, b + 3)
                    if b >= 2:
                        pe.wait_ge(new_ready, b - 1)
                    elif b == 1:
                        pe.wait_ge(idx_ready, 1)
                    nc.tensor.matmul(bank[2 + b % 2][:, 0:H], h0[:, b % 2], w_in_sb[:], start=True, stop=True
                                     ).then_inc(proj_done, 1)

                pe.wait_ge(s_wait, 64)
                for b in range(NB + 3):
                    if b < NB:
                        transpose_x(b)
                    if 1 <= b < NB + 1:
                        project(b - 1)
                    if 2 <= b < NB + 2:
                        transpose_block(pe, b - 2, b % 2)
                    if b >= 3:
                        logits_of_block(pe, b - 3, (b - 3) % 2, 0)
                pe.wait_ge(hl_kept, NB + 2)
                pe.wait_ge(new_ready, NB)

                def window(n, gi):
                    pe.wait_ge(hot_s_ready, n + 1)
                    pe.wait_ge(hot_m_ready, n + 1)
                    pe.wait_ge(win_evac, n + 1)
                    for c in range(CH):
                        last = nc.tensor.matmul(bank[gi % 4][:, 0:MW], oh_s[:, gi % 4, c], oh_m[:, gi % 2, c],
                                                start=(c == 0), stop=(c == CH - 1))
                    last.then_inc(win_done, 1)

                def degrees(k, slot, n):
                    pe.wait_ge(rdeg_ready, k + 1)
                    pe.wait_ge(win_evac, n + 4)
                    for s in range(NB):
                        last = nc.tensor.matmul(bank[4 + slot][:, 0:1], piece[:, slot, s, :], onesb[:, 0:1],
                                                start=(s == 0), stop=(s == NB - 1))
                    last.then_inc(deg_done, 1)

                with pe.Fori(0, BODIES) as i:
                    for k in range(2):
                        for gi in range(GP):
                            window((2 * i + k) * GP + gi, gi)
                        degrees(2 * i + k, k, (2 * i + k + 1) * GP)
                for gi in range(LASTG):
                    window(2 * BODIES * GP + gi, gi)
                degrees(NB - 1, 0, GROUPS)
                pe.wait_ge(vtotal_ready, 1)
                nc.tensor.matmul(bank[6][0:1, 0:1], vtotal[:], ones1[:], start=True, stop=True).then_inc(vsum_done, 1)


        with ExitStack() as cg:
            NCH = ROWLEN
            ROUND = 2048
            BANKS = -(-NB * P // 512)
            g_ed = sb("g_ed", [ROWS, NCH, 2], I32, cg)
            g_a = sb("g_a", [ROWS, NCH], I32, cg)
            g_b = sb("g_b", [ROWS, NCH], I32, cg)
            g_c = sb("g_c", [ROWS, NCH], I32, cg)
            g_src = sb("g_src", [ROWS, NCH], F32, cg)
            g_blk = sb("g_blk", [ROWS, NCH], F32, cg)
            g_dlo = sb("g_dlo", [ROWS, NCH], F32, cg)
            g_col = sb("g_col", [ROWS, NCH], F32, cg)
            g_now = sb("g_now", [P, 1], F32, cg)
            g_key = sb("g_key", [ROWS, NCH], F32, cg)
            g_dkey = sb("g_dkey", [ROWS, NCH], F32, cg)
            g_iota = sb("g_iota", [P, NB * P], F32, cg)
            g_hot_s = sb("g_hot_s", [ROWS, P], BF16, cg)
            g_hot_d = sb("g_hot_d", [ROWS, P], BF16, cg)
            g_hot_m = sb("g_hot_m", [ROWS, NB * P], BF16, cg)
            g_count = sb("g_count", [P, 512], I32, cg)
            g_part = sb("g_part", [P, 512], I32, cg)
            g_low = sb("g_low", [P, NB * P], F16, cg)
            g_up = sb("g_up", [P, NB * P], BF16, cg)
            g_zero = sb("g_zero", [P, 512], BF16, cg)
            g_const = sem("g_const")
            g_in = sem("g_in")
            g_hot = sem("g_hot")
            g_mult = sem("g_mult")
            g_sum = sem("g_sum")
            g_taken = sem("g_taken")
            g_low_out = sem("g_low_out")
            g_up_out = sem("g_up_out")
            g_free = sem("g_free")

            block = cg.enter_context(nc.Block())

            @block.sync
            def _(sp):
                slow = sp.value_load(slow_flag[0:1, 0:1], min_val=0, max_val=1)
                with sp.If(slow == 0):
                    sp.nop()
                with sp.Else():
                    sp.dma_start(g_ed[:], edges.rearrange("(p k) two -> p k two", p=ROWS)).then_inc(g_in, 16)
                    sp.sem_inc(g_free, 1)
                    with sp.Fori(0, NB) as b:
                        hold(sp, g_taken, b + 2)
                        sp.dma_start(at_dram[bass.ds(b, 1)].rearrange("o p c -> p (o c)"), g_low[:]).then_inc(g_low_out, 16)
                        sp.dma_start(at_upper_dram[bass.ds(b, 1)].rearrange("o p c -> p (o c)"), g_up[:]
                                     ).then_inc(g_up_out, 16)
                        hold(sp, g_low_out, 16 * (b + 1))
                        hold(sp, g_up_out, 16 * (b + 1))
                        sp.sem_inc(g_free, 1)
                sp.nop()

            @block.gpsimd
            def _(pool):
                slow = pool.value_load(slow_flag[0:1, 0:1], min_val=0, max_val=1)
                with pool.If(slow == 0):
                    pool.nop()
                with pool.Else():
                    nc.gpsimd.iota(g_iota[:], pattern=[[1, NB * P]], base=1, channel_multiplier=0,
                                   allow_small_or_imprecise_dtypes=True)
                    nc.gpsimd.memset(g_now[:], 0.0)
                    nc.gpsimd.memset(g_zero[:], 0.0)
                    pool.drain().then_inc(g_const, 1)
                pool.nop()

            @block.vector
            def _(dve):
                slow = dve.value_load(slow_flag[0:1, 0:1], min_val=0, max_val=1)
                with dve.If(slow == 0):
                    dve.nop()
                with dve.Else():
                    dve.sem_inc(g_taken, 1)
                    dve.wait_ge(g_const, 1)
                    dve.wait_ge(g_in, 16)
                    src, to = g_ed[:, :, 0], g_ed[:, :, 1]
                    nc.vector.tensor_scalar(g_a[:], src, P - 1, None, ALU.bitwise_and)
                    nc.vector.tensor_scalar(g_b[:], to, P - 1, None, ALU.bitwise_and)
                    nc.vector.tensor_scalar(g_c[:], to, 7, None, ALU.logical_shift_right)
                    dve.drain()
                    nc.vector.tensor_scalar(g_src[:], g_a[:], 1.0, None, ALU.add)
                    nc.vector.tensor_scalar(g_dlo[:], g_b[:], 1.0, None, ALU.add)
                    nc.vector.tensor_copy(g_blk[:], g_c[:])
                    dve.drain()
                    nc.vector.tensor_tensor(g_a[:], src, g_a[:], ALU.subtract)
                    dve.drain()
                    nc.vector.tensor_tensor(g_col[:], g_a[:], g_dlo[:], ALU.add)
                    dve.drain()
                    with dve.Fori(0, NB) as b:
                        nc.vector.scalar_tensor_tensor(g_key[:], g_blk[:], g_now[0:ROWS, 0:1], g_col[:], ALU.is_equal, ALU.mult)
                        nc.vector.scalar_tensor_tensor(g_dkey[:], g_blk[:], g_now[0:ROWS, 0:1], g_dlo[:], ALU.is_equal, ALU.mult)
                        dve.drain()
                        with dve.Fori(0, NCH) as c:
                            hold(dve, g_mult, NCH * b + c + 1)
                            nc.vector.tensor_scalar(g_hot_s[:], g_iota[0:ROWS, 0:P], g_src[:, bass.ds(c, 1)], None, ALU.is_equal)
                            nc.vector.tensor_scalar(g_hot_d[:], g_iota[0:ROWS, 0:P], g_dkey[:, bass.ds(c, 1)], None, ALU.is_equal)
                            nc.vector.tensor_scalar(g_hot_m[:], g_iota[0:ROWS, :], g_key[:, bass.ds(c, 1)], None, ALU.is_equal)
                            dve.drain().then_inc(g_hot, 1)
                        hold(dve, g_sum, b + 1)
                        hold(dve, g_free, b + 1)
                        for j in range(BANKS):
                            w = min(512, NB * P - 512 * j)
                            part = slice(512 * j, 512 * j + w)
                            nc.vector.tensor_copy(g_count[:, 0:w], bank[j][:, 0:w])
                            dve.drain()
                            nc.vector.tensor_scalar(g_part[:, 0:w], g_count[:, 0:w], ROUND - 1, None, ALU.bitwise_and)
                            dve.drain()
                            nc.vector.tensor_copy(g_low[:, part], g_part[:, 0:w])
                            nc.vector.tensor_tensor(g_up[:, part], g_count[:, 0:w], g_part[:, 0:w], ALU.subtract)
                            dve.drain()
                        nc.vector.tensor_scalar(rdeg[:, bass.ds(b, 1)], bank[7][:, 0:1], 1.0, None, ALU.max)
                        nc.vector.tensor_scalar(g_now[:], g_now[:], 1.0, None, ALU.add)
                        dve.drain()
                        nc.vector.reciprocal(rdeg[:, bass.ds(b, 1)], rdeg[:, bass.ds(b, 1)])
                        dve.drain().then_inc(g_taken, 1)
                dve.nop()

            @block.tensor
            def _(pe):
                slow = pe.value_load(slow_flag[0:1, 0:1], min_val=0, max_val=1)
                with pe.If(slow == 0):
                    pe.nop()
                with pe.Else():
                    pe.sem_inc(g_mult, 1)
                    hold(pe, g_const, 1)

                    def edge_of_block(start):
                        for j in range(BANKS + 1):
                            w = 1 if j == BANKS else min(512, NB * P - 512 * j)
                            last = nc.tensor.matmul(bank[j][:, 0:w], onesb[:], g_zero[:, 0:w], start=start,
                                                    stop=not start, skip_group_check=True)
                        return last

                    with pe.Fori(0, NB) as b:
                        hold(pe, g_taken, b + 1)
                        edge_of_block(True)
                        with pe.Fori(0, NCH) as c:
                            hold(pe, g_hot, NCH * b + c + 1)
                            for j in range(BANKS):
                                w = min(512, NB * P - 512 * j)
                                nc.tensor.matmul(bank[j][:, 0:w], g_hot_s[:], g_hot_m[:, 512 * j:512 * j + w],
                                                 start=False, stop=False, skip_group_check=True)
                            nc.tensor.matmul(bank[BANKS][:, 0:1], g_hot_d[:], onesb[0:ROWS, 0:1], start=False, stop=False,
                                             skip_group_check=True).then_inc(g_mult, 1)
                        edge_of_block(False).then_inc(g_sum, 1)
                pe.nop()

        slot_here = sem("slot_here")
        combined = sem("combined")
        phase_end = sem("phase_end")
        g_all = sb("g_all", [P, NB, 2], F32)
        slots_all = sb("slots_all", [P, 2 * NB], U32)
        slot_get = sb("slot_get", [P, 2, 8], U32)
        GOT = 4
        TURNS = (NB - 1) // (2 * GOT)
        assert (NB - 1) % (2 * GOT) == 0
        got = [sem(f"got{i}") for i in range(GOT)]
        GFIRST, GOTHER = (NB - 1) // GOT + 1, (NB - 1) // GOT
        FIRST, SECOND = TRIPS + 1, TRIPS
        SC = 5
        assert NB % SC == 0

        def join(eng, n):
            eng.drain().then_inc(phase_end, 1)
            hold(eng, phase_end, 5 * n)

        def collect_all(pool, y_got, l):
            def places(b, h, blocks, copies):
                hold(pool, combined, NB * l + b + 1)
                nc.gpsimd.tensor_copy(slot_get[:, h, 0:2 * blocks], slots_all[:, bass.ds(2 * b, 2 * blocks)]
                                      ).then_inc(slot_here, 1)
                hold(pool, slot_here, copies)

            def collect(b, v, h, rows=P):
                hold(pool, combined, NB * l + b + 1)
                for k in range(2):
                    nc.gpsimd.indirect_dma_start(
                        out=y_got[0:rows, v, k], out_offset=None, in_=slot_y[:],
                        in_offset=bass.IndirectOffsetOnAxis(ap=slot_get[0:rows, h, 2 * v + k:2 * v + k + 1], axis=0),
                        bounds_check=YROWS - 1, oob_is_err=False).then_inc(got[v], 16)

            before = (2 * TURNS + 1) * l
            with pool.Fori(0, TURNS) as i:
                for h in range(2):
                    places(2 * GOT * i + GOT * h, h, GOT, before + 2 * i + h + 1)
                    for v in range(GOT):
                        collect(2 * GOT * i + GOT * h + v, v, h)
            places(NB - 1, 0, 1, before + 2 * TURNS + 1)
            collect(NB - 1, 0, 0, LROWS)

        def combine(dve, y_got, l, b, v, i, rows=P):
            n = NB * (l + 1) + b
            R = slice(0, rows)
            hold(dve, got[v], 32 * ((GOTHER if v else GFIRST) * l + i + 1))
            hold(dve, hT_done, n + 1)
            for k, part in enumerate((h_hi, h_lo)):
                nc.vector.scalar_tensor_tensor(y_got[R, v, k], y_got[R, v, k], g_all[R, bass.ds(b, 1), k],
                                               part[R, bass.ds(b, 1)].rearrange("p o f -> p (o f)"), ALU.mult, ALU.add)
            dve.drain()
            nc.vector.tensor_tensor(h_new[R, v % 2], y_got[R, v, 0], y_got[R, v, 1], ALU.add).then_inc(new_ready, 1)
            return dve.drain()

        def in_pairs(eng, step):
            with eng.Fori(0, TRIPS) as i:
                for u in range(2):
                    step(2 * i + u, u, i)
            step(NB - 1, 0, TRIPS)

        with ExitStack() as c2:
            def sb2(name, shape, dt):
                return sb(name, shape, dt, c2)

            at_in_sb = sb2("at_in_sb", [P, 2, NB, P], F16)
            shared = sb2("shared", [P, 2 * NB * P], F32R)
            at_r = shared[:].rearrange("p (u s d) -> p u s d", u=2, d=P)
            parts = shared[:, 0:4 * KH * TOK].rearrange("p (u h k n) -> p u h k n", u=2, h=2, k=KH)
            x_hi, x_lo = parts[:, :, 0], parts[:, :, 1]
            acts = shared[:, 4 * KH * TOK:4 * KH * TOK + 2 * KF * TOK].rearrange("p (h k n) -> p h k n", h=2, k=KF)
            act_hi, act_lo = acts[:, 0], acts[:, 1]
            pool_f = sb2("phase_buffer", [P, 8 * H], F32)
            agg = pool_f[:, 0:2 * H].rearrange("p (u f) -> p u f", u=2)
            aT = pool_f[:, 2 * H:4 * H].rearrange("p (u k n) -> p u k n", u=2, k=KH)
            AGG = 4
            agg_out = pool_f[:, 4 * H:8 * H].rearrange("p (u f) -> p u f", u=AGG)
            y_sb = pool_f[:, 4 * H:8 * H].rearrange("p (u s f) -> p u s f", u=2, s=2)
            y_got = pool_f[:].rearrange("p (u k f) -> p u k f", u=GOT, k=2)
            stage_f = sb2("stage", [P, 6 * H], F32)
            stage = stage_f[:, 0:2 * 512].rearrange("p (u f) -> p u f", u=2)
            x_rows = stage_f[:, 0:4 * H].rearrange("p (u s f) -> p u s f", u=2, s=2)
            v = stage_f[:, 4 * H:4 * H + 2 * TOK].rearrange("p (u n) -> p u n", u=2)
            w_hi = sb2("w_hi", [P, WQ, 512], F32R)
            w_lo = sb2("w_lo", [P, WQ, 512], F32R)
            bias = sb2("bias", [P, NE, H], F32)
            b1_sb = sb2("b1_sb", [P, NSTRONG * KF], F32)
            lg = sb2("lg", [P, NE1], F32)
            top = sb2("top", [P, 8], F32)
            idx = sb2("idx", [P, 8], U32)
            idx_f = sb2("idx_f", [P, 2], F32)
            dz = sb2("dz", [P, 2], F32)
            ex = sb2("ex", [P, 2], F32)
            den = sb2("den", [P, 2], F32)
            rec = sb2("rec", [P, 2], F32)
            gt = sb2("gt", [P, 2], F32)
            hots = sb2("hots", [P, 2, NE], F32)
            member = sb2("member", [P, NE], BF16)
            next_slot = sb2("next_slot", [P, NE], F32)
            pos = sb2("pos", [P, NE], F32)
            prod = sb2("prod", [P, 2, NE], F32)
            slot_f = sb2("slot_f", [P, 2], F32)
            slot_now = sb2("slot_now", [P, 2, 2], U32)
            idx_all = sb2("idx_all", [P, 2 * NB], F32)
            slots_f = sb2("slots_f", [P, 2 * NB], F32)
            moved = sb2("moved", [P, 2 * NB, NE], F32)
            shift = sb2("shift", [P, NE], F32)
            taken = sb2("taken", [P, NE], F32)
            taken_i = sb2("taken_i", [P, NE], I32)
            sums = [sb2(f"sums{i}", [P, 2 * NE], F32) for i in range(2)]
            tiles_before = sb2("tiles_before", [P, 1], F32)
            weak_pairs = sb2("weak_pairs", [P, 1], F32)
            strong_pairs = sb2("strong_pairs", [P, 1], F32)
            plan_f = sb2("plan_f", [P, 4 * NE], F32)
            plan = sb2("plan", [1, 4 * NE], I32)

            zeroed = sem("zeroed")
            at_in = [sem("at_in0"), sem("at_in1")]
            at_used = [sem("at_used0"), sem("at_used1")]
            at_ready = sem("at_ready")
            small_in = sem("small_in")
            w_in_ = [sem("w_in0"), sem("w_in1")]
            w_hi_done = sem("w_hi_done")
            w_split = sem("w_split")
            agg_done = sem("agg_done")
            agg_ready = sem("agg_ready")
            agg_free = sem("agg_free")
            aT_done = sem("aT_done")
            aT_ready = sem("aT_ready")
            lg_done = sem("lg_done")
            lg_taken = sem("lg_taken")
            dz_ready = sem("dz_ready")
            ex_ready = sem("ex_ready")
            member_ready = sem("member_ready")
            rank_done = sem("rank_done")
            slot_ready = sem("slot_ready")
            scattered = sem("scattered")
            x_in = [sem("x_in20"), sem("x_in21")]
            xT_done = sem("xT_done")
            xh_ready = sem("xh_ready")
            xl_ready = sem("xl_ready")
            unit_done = sem("unit_done")
            hi_ready = sem("hi_ready")
            lo_ready = sem("lo_ready")
            y_done = sem("y_done")
            y_ready = sem("y_ready2")
            y_relu = sem("y_relu")
            y_out = [sem("y_out0"), sem("y_out1")]

            x_bank = (0, 7)
            unit_bank = (1, 2, 5, 6)

            block = c2.enter_context(nc.Block())

            def each_expert(eng, tile, last=None, kind=True, place=True, at_once=False):
                def planned(k, e, most):
                    return eng.value_load(plan[0:1, k * NE + e:k * NE + e + 1], min_val=0, max_val=most)

                def read(e):
                    return (eng.value_load(plan[0:1, e:e + 1], min_val=1, max_val=REGION // PAIR),
                            planned(1, e, LAYERS * LPAIRS),
                            planned(2, e, LAYERS * LPAIRS) if kind else 0,
                            planned(3, e, LPAIRS - 1) if place else 0)

                ahead = [read(e) for e in range(NE)] if at_once else None
                for e in range(NE):
                    count, base, sbase, lbase = ahead[e] if at_once else read(e)
                    with eng.Fori(0, count) as t:
                        Y = None
                        if place:
                            Y = nc.s_assert_within(lbase + t, 0, LPAIRS - 1, skip_runtime_bounds_check_because=
                                                   "the layer's pairs are at most LPAIRS")
                        for p in range(2):
                            tile(e, t, p, 2 * (base + t) + p, 2 * (sbase + t) + p, base + t, Y)
                if last is not None:
                    last(base + count)

            def first_pair(eng):
                return eng.value_load(plan[0:1, NE:NE + 1], min_val=0, max_val=LAYERS * LPAIRS)

            def layers(phase_a, phase_b, phase_c, eng):
                with eng.Fori(0, LAYERS - 1) as l:
                    phase_a(l)
                    join(eng, 3 * l + 1)
                    phase_b(l, False)
                    join(eng, 3 * l + 2)
                    phase_c(l)
                    join(eng, 3 * l + 3)
                phase_a(LAYERS - 1)
                join(eng, 3 * LAYERS - 2)
                phase_b(LAYERS - 1, True)

            assert TRIPS - 1 == 1 + WQ // 2 and WQ % 4 == 0

            def blocks_of_a(eng, step):
                step(0, 0, 0, None, 0)
                step(0, 1, 1, None, 1)
                with eng.Fori(0, WQ // 4) as j:
                    for k in range(4):
                        step(2 * j + 1 + k // 2, 4 * j + 2 + k, k % 2, 4 * j + k, None)
                step(TRIPS - 1, NB - 3, 0, None, None)
                step(TRIPS - 1, NB - 2, 1, None, None)
                step(TRIPS, NB - 1, 0, None, NB - 1)

            def uses(l, b_turn, u):
                return (SECOND if u else FIRST) * l + b_turn

            @block.sync
            def _(sp):
                slow = sp.value_load(slow_flag[0:1, 0:1], min_val=0, max_val=1)

                def load(b, u, use):
                    hold(sp, at_used[u], use + 1)
                    sp.dma_start(at_in_sb[:, u].rearrange("p s d -> p (s d)"),
                                 at_dram[bass.ds(b, 1)].rearrange("o p c -> p (o c)")).then_inc(at_in[u], 16)

                def load_both(b, n):
                    load(b, 0, n)
                    hold(sp, at_used[1], n + 1)
                    sp.dma_start(at_in_sb[:, 1].rearrange("p s d -> p (s d)").bitcast(BF16),
                                 at_upper_dram[bass.ds(b, 1)].rearrange("o p c -> p (o c)")).then_inc(at_in[1], 16)

                def load_first(l):
                    with sp.If(slow == 0):
                        load(0, 0, uses(l, 0, 0))
                        load(1, 1, uses(l, 0, 1))
                    with sp.Else():
                        load_both(0, NB * l)
                    sp.nop()

                def phase_a(l):
                    def weights(i, u, q):
                        hold(sp, w_split, WQ * l + q + 1)
                        sp.dma_start(stage[:, u], pieces[bass.ds(l, 1), bass.ds(q, 1)].rearrange("o k p f -> p (o k f)")
                                     ).then_inc(w_in_[u], 16)

                    def fast(i, b, u, q, end):
                        if end not in (0, 1):
                            load(b, u, uses(l, i, u))
                        if q is not None:
                            weights(i, u, q)

                    def general(i, b, u, q, end):
                        if end != 0:
                            load_both(b, NB * l + b)
                        if q is not None:
                            weights(i, u, q)

                    with sp.If(slow == 0):
                        blocks_of_a(sp, fast)
                    with sp.Else():
                        blocks_of_a(sp, general)
                    sp.nop()

                def phase_b(l, last):
                    def rows(X, p, first):
                        hold(sp, xT_done, X + 1)
                        sp.dma_start(x_rows[:, p], slot_x[bass.ds(first, TOK), :].rearrange("(s p) f -> p s f", p=P)
                                     ).then_inc(x_in[p], 16)

                    each_expert(sp, lambda e, t, p, G, S, pair, Y: rows(G + l, p, t * PAIR + (REGION * e + p * TOK)),
                                lambda pairs: rows(2 * pairs + l, 0, XROWS - TOK), kind=False, place=False)
                    if not last:
                        load_first(l + 1)

                load_first(0)
                layers(phase_a, phase_b, lambda l: None, sp)

            @block.gpsimd
            def _(pool):
                pool.sem_inc(agg_free, AGG)
                nc.gpsimd.memset(pool_f[:], 0.0)
                for t in (sums[0], sums[1], tiles_before, weak_pairs, plan_f):
                    nc.gpsimd.memset(t[:], 0.0)
                pool.drain()
                for p in range(2):
                    nc.gpsimd.dma_start(slot_y[YROWS - (2 - p) * P:YROWS - (1 - p) * P, :], y_sb[:, p, 0]
                                        ).then_inc(y_out[p], 16)
                    pool.wait_ge(y_out[p], 16)
                pool.sem_inc(zeroed, 1)

                def phase_a(l):
                    nc.gpsimd.dma_start(bias[:, 0:NWEAK, :], weak_b[bass.ds(l, 1)].to_broadcast([P, NWEAK, H])
                                        ).then_inc(small_in, 16)
                    nc.gpsimd.dma_start(bias[:, NWEAK:NE, :], b2[bass.ds(l, 1)].to_broadcast([P, NSTRONG, H])
                                        ).then_inc(small_in, 16)
                    nc.gpsimd.dma_start(b1_sb[:], b1[bass.ds(l, 1)].rearrange("o p u -> p (o u)")).then_inc(small_in, 16)

                    def scatter(b, v, rows=P):
                        n = NB * l + b
                        hold(pool, slot_ready, n + 1)
                        for k in range(2):
                            nc.gpsimd.indirect_dma_start(
                                out=slot_x[:], out_offset=bass.IndirectOffsetOnAxis(ap=slot_now[0:rows, v % 2, k:k + 1], axis=0),
                                in_=agg_out[0:rows, v], in_offset=None, bounds_check=XROWS - 1, oob_is_err=False
                                ).then_inc(scattered, 16)
                        hold(pool, scattered, 32 * (n + 1))
                        pool.sem_inc(agg_free, 1)

                    with pool.Fori(0, (NB - 1) // AGG) as i:
                        for v in range(AGG):
                            scatter(AGG * i + v, v)
                    scatter(NB - 1, 0, LROWS)

                def phase_b(l, last):
                    def store(e, t, p, G, S, pair, Y):
                        if e < NWEAK:
                            hold(pool, y_relu, 2 * S + 2)
                        else:
                            hold(pool, y_ready, 2 * G + 4)
                        nc.gpsimd.dma_start(slot_y[bass.ds(Y * PAIR + p * TOK, TOK), :].rearrange("(s p) f -> p s f", p=P),
                                            y_sb[:, p]).then_inc(y_out[p], 16)

                    def stored(pairs):
                        for p in range(2):
                            hold(pool, y_out[p], 16 * (pairs + 1))
                    each_expert(pool, store, stored)

                layers(phase_a, phase_b, lambda l: collect_all(pool, y_got, l), pool)

            @block.scalar
            def _(act):
                slow = act.value_load(slow_flag[0:1, 0:1], min_val=0, max_val=1)
                act.sem_inc(aT_ready, 2)
                act.sem_inc(hi_ready, KF)
                for u in range(2):
                    act.sem_inc(at_used[u], 1)

                def convert(before, u, use, upper=False):
                    hold(act, at_in[u], 16 * (use + 1))
                    hold(act, agg_done, before + 2)
                    at = at_in_sb[:, u].rearrange("p s d -> p (s d)")
                    if upper:
                        at = at.bitcast(BF16)
                    for c in range(NB // SC):
                        cols = slice(c * SC * P, (c + 1) * SC * P)
                        last = nc.scalar.activation(at_r[:, u].rearrange("p s d -> p (s d)")[:, cols], at[:, cols],
                                                    ACT.Copy)
                        last.then_inc(at_ready, 1)
                    act.drain().then_inc(at_used[u], 1)

                def phase_a(l):
                    def weights(i, u, q):
                        hold(act, w_in_[u], 16 * (WQ // 2 * l + i))
                        nc.scalar.activation(w_hi[:, bass.ds(q, 1)].rearrange("p o f -> p (o f)"), stage[:, u],
                                             ACT.Copy).then_inc(w_hi_done, 1)

                    def transposed(b, u):
                        hold(act, aT_done, NB * l + b + 1)
                        nc.scalar.activation(aT[:, u].rearrange("p k n -> p (k n)"), bank[2 + u][:, 0:H], ACT.Copy
                                             ).then_inc(aT_ready, 1)

                    def exponentials(b):
                        act.wait_ge(dz_ready, NB * l + b + 1)
                        nc.scalar.activation(ex[:], dz[:], ACT.Exp).then_inc(ex_ready, 1)

                    def fast(i, b, u, q, end):
                        if end != 0:
                            transposed(b - 1, 1 - u)
                        if q is not None:
                            weights(i, u, q)
                        if end != NB - 1:
                            convert(NB * l + b, 1 - u, uses(l, i + u, 1 - u))
                        if end != 0:
                            exponentials(b - 1)

                    def general(i, b, u, q, end):
                        n = NB * l + b
                        convert(n, 0, n)
                        convert(n, 1, n, upper=True)
                        if end != 0:
                            transposed(b - 1, 1 - u)
                            exponentials(b - 1)
                        if q is not None:
                            weights(i, u, q)

                    with act.If(slow == 0):
                        convert(NB * l, 0, uses(l, 0, 0))
                        blocks_of_a(act, fast)
                    with act.Else():
                        blocks_of_a(act, general)
                    act.nop()
                    transposed(NB - 1, 0)
                    exponentials(NB - 1)

                def phase_b(l, last):
                    def upper(X, p):
                        act.wait_ge(xT_done, X + 3)
                        nc.scalar.activation(x_hi[:, p].rearrange("p k n -> p (k n)"), bank[x_bank[p]][:], ACT.Copy
                                             ).then_inc(xh_ready, 1)

                    def tile(e, t, p, G, S, pair, Y):
                        if e < NWEAK:
                            upper(G + l + 1, 1 - p)
                            for s in range(2):
                                act.wait_ge(y_ready, 2 * G + s + 3)
                                nc.scalar.activation(y_sb[:, p, s], y_sb[:, p, s], ACT.Relu).then_inc(y_relu, 1)
                            return
                        for f in range(KF):
                            hold(act, unit_done, KF * S + f + 1)
                            act.wait_ge(lo_ready, KF * S + f + 1)
                            src = bank[unit_bank[f]][:, 0:TOK]
                            col = (e - NWEAK) * KF + f
                            nc.scalar.activation(v[:, f % 2], src, ACT.Relu, bias=b1_sb[:, col:col + 1])
                            nc.scalar.activation(act_hi[:, f], src, ACT.Relu, bias=b1_sb[:, col:col + 1]
                                                 ).then_inc(hi_ready, 1)
                        upper(G + l + 1, 1 - p)

                    hold(act, small_in, 48 * (l + 1))
                    upper(2 * first_pair(act) + l, 0)
                    each_expert(act, tile, place=False, at_once=True)

                def phase_c(l):
                    def keep(b, u, first=False):
                        n = NB * (l + 1) + b
                        hold(act, new_ready, n + 1)
                        nc.scalar.activation(h_hi[:, bass.ds(b, 1)].rearrange("p o f -> p (o f)"), h_new[:, u], ACT.Copy
                                             ).then_inc(hi_kept, 1)
                        keep_transpose(act, n, u)
                        if not first:
                            keep_logits(act, n - 1, b - 1, 1 - u)

                    keep(0, 0, True)
                    with act.Fori(0, TRIPS) as i:
                        for k in range(2):
                            keep(2 * i + 1 + k, 1 - k)
                    keep_logits(act, NB * (l + 2) - 1, NB - 1, 0)
                layers(phase_a, phase_b, phase_c, act)

            @block.vector
            def _(dve):
                dve.sem_inc(combined, GOT)
                dve.sem_inc(w_split, 2)
                dve.sem_inc(agg_ready, 2)
                dve.sem_inc(lg_taken, 1)
                dve.sem_inc(lo_ready, 2)
                dve.sem_inc(y_ready, 2)
                dve.wait_ge(zeroed, 1)

                def phase_a(l):
                    nc.vector.tensor_copy(next_slot[:], region_0[:])
                    dve.drain()

                    def weights(u, q):
                        hold(dve, w_hi_done, WQ * l + q + 1)
                        at = bass.ds(q, 1)
                        nc.vector.tensor_tensor(w_lo[:, at].rearrange("p o f -> p (o f)"), stage[:, u],
                                                w_hi[:, at].rearrange("p o f -> p (o f)"), ALU.subtract).then_inc(w_split, 1)

                    def mean(b, u):
                        n = NB * l + b
                        hold(dve, agg_done, n + 3)
                        hold(dve, agg_free, n + 1)
                        nc.vector.tensor_scalar(agg[:, u], bank[u][:, 0:H], rdeg[:, bass.ds(b, 1)], None, ALU.mult)
                        nc.vector.tensor_scalar(agg_out[:, bass.ds(b % AGG, 1)].rearrange("p o f -> p (o f)"),
                                                bank[u][:, 0:H], rdeg[:, bass.ds(b, 1)], None, ALU.mult
                                                ).then_inc(agg_ready, 1)

                    def choose(b, last=False):
                        n = NB * l + b
                        dve.wait_ge(lg_done, n + 1)
                        nc.vector.tensor_tensor(lg[:], bank[4][:, 0:NE1],
                                                h_logits[:, bass.ds(b, 1)].rearrange("p o e -> p (o e)"), ALU.add
                                                ).then_inc(lg_taken, 1)
                        dve.drain()
                        nc.vector.max(top[:], lg[:, 0:NE])
                        nc.vector.tensor_scalar(dz[:, 1:2], lg[:, NE:NE1], -1.0, None, ALU.mult)
                        dve.drain()
                        nc.vector.max_index(idx[:], top[:], lg[:, 0:NE])
                        nc.vector.tensor_tensor(dz[:, 0:1], top[:, 1:2], top[:, 0:1], ALU.subtract)
                        dve.drain().then_inc(dz_ready, 1)
                        nc.vector.tensor_copy(idx_f[:], idx[:, 0:2])
                        nc.vector.tensor_copy(idx_all[:, bass.ds(2 * b, 2)], idx[:, 0:2])
                        dve.drain()
                        nc.vector.tensor_tensor(hots[:], expert_no[:].unsqueeze(1).to_broadcast([P, 2, NE]),
                                                idx_f[:].unsqueeze(2).to_broadcast([P, 2, NE]), ALU.is_equal)
                        if last:
                            nc.vector.memset(member[:], 0.0)
                        dve.drain()
                        R = slice(0, LROWS if last else P)
                        nc.vector.tensor_tensor(member[R], hots[R, 0], hots[R, 1], ALU.add).then_inc(member_ready, 1)

                    def place(b, u):
                        n = NB * l + b
                        hold(dve, ex_ready, n + 1)
                        nc.vector.tensor_scalar(den[:], ex[:], 1.0, None, ALU.add)
                        dve.drain()
                        nc.vector.reciprocal(rec[:], den[:])
                        dve.drain()
                        nc.vector.tensor_tensor(gt[:, 0:1], rec[:, 0:1], rec[:, 1:2], ALU.mult)
                        hold(dve, rank_done, n + 1)
                        nc.vector.tensor_tensor(pos[:], bank[5][:, 0:NE], next_slot[:], ALU.add)
                        dve.drain()
                        nc.vector.tensor_tensor(gt[:, 1:2], gt[:, 0:1], ex[:, 0:1], ALU.mult)
                        nc.vector.tensor_tensor(prod[:], hots[:], pos[:].unsqueeze(1).to_broadcast([P, 2, NE]), ALU.mult)
                        nc.vector.tensor_tensor(next_slot[:], bank[5][:, NE:2 * NE], next_slot[:], ALU.add)
                        dve.drain()
                        nc.vector.tensor_reduce(slot_f[:], prod[:], AX.X, ALU.add)
                        nc.vector.tensor_copy(g_all[:, bass.ds(b, 1)].rearrange("p o k -> p (o k)"), gt[:])
                        dve.drain()
                        hold(dve, agg_free, n + AGG - 1)
                        nc.vector.tensor_copy(slot_now[:, u], slot_f[:])
                        nc.vector.tensor_copy(slots_f[:, bass.ds(2 * b, 2)], slot_f[:])
                        dve.drain().then_inc(slot_ready, 1)

                    def step(i, b, u, q, end):
                        mean(b, u)
                        if q is not None:
                            weights(u, q)
                        if end != 0:
                            place(b - 1, 1 - u)
                        choose(b, end == NB - 1)

                    blocks_of_a(dve, step)
                    place(NB - 1, 0)

                    nc.vector.tensor_tensor(taken[:], next_slot[:], region_0[:], ALU.subtract)
                    dve.drain()
                    nc.vector.tensor_scalar(taken_i[:], taken[:], float(PAIR - 1), None, ALU.add)
                    dve.drain()
                    nc.vector.tensor_scalar(taken_i[:], taken_i[:], PAIR.bit_length() - 1, None, ALU.logical_shift_right)
                    dve.drain()
                    nc.vector.tensor_scalar(plan_f[:, 0:NE], taken_i[:], 1.0, None, ALU.max)
                    dve.drain()
                    nc.vector.tensor_copy(sums[0][:, NE:2 * NE], plan_f[:, 0:NE])
                    dve.drain()
                    for k, step_ in enumerate((1, 2, 4)):
                        a, b = sums[k % 2], sums[(k + 1) % 2]
                        nc.vector.tensor_tensor(b[:, NE:2 * NE], a[:, NE:2 * NE], a[:, NE - step_:2 * NE - step_], ALU.add)
                        dve.drain()
                    s = sums[1]
                    nc.vector.tensor_scalar(plan_f[:, NE:2 * NE], s[:, NE - 1:2 * NE - 1], tiles_before[:, 0:1], None, ALU.add)
                    nc.vector.tensor_tensor(strong_pairs[:], tiles_before[:], weak_pairs[:], ALU.subtract)
                    dve.drain()
                    nc.vector.tensor_tensor(weak_pairs[:], weak_pairs[:], s[:, NE + NWEAK - 1:NE + NWEAK], ALU.add)
                    nc.vector.tensor_scalar(plan_f[:, 2 * NE:2 * NE + NWEAK], plan_f[:, NE:NE + NWEAK],
                                            strong_pairs[:, 0:1], None, ALU.subtract)
                    dve.drain()
                    nc.vector.tensor_copy(plan_f[:, 3 * NE:4 * NE], s[:, NE - 1:2 * NE - 1])
                    nc.vector.scalar_tensor_tensor(shift[:], s[:, NE - 1:2 * NE - 1], float(PAIR), region_0[:],
                                                   ALU.mult, ALU.subtract)
                    nc.vector.tensor_scalar(plan_f[:, 2 * NE + NWEAK:3 * NE], plan_f[:, NE + NWEAK:2 * NE],
                                            weak_pairs[:, 0:1], None, ALU.subtract)
                    nc.vector.tensor_tensor(tiles_before[:], tiles_before[:], s[:, 2 * NE - 1:2 * NE], ALU.add)
                    dve.drain()
                    nc.vector.tensor_copy(plan[:], plan_f[0:1, :])
                def phase_b(l, last):
                    def lower(X, p):
                        hold(dve, xh_ready, X + 1)
                        nc.vector.tensor_tensor(x_lo[:, p].rearrange("p k n -> p (k n)"), bank[x_bank[p]][:],
                                                x_hi[:, p].rearrange("p k n -> p (k n)"), ALU.subtract
                                                ).then_inc(xl_ready, 1)

                    def results(e, G, p, pair):
                        hold(dve, y_out[p], 16 * (pair + 1))
                        for s in range(2):
                            hold(dve, y_done, 2 * G + s + 1)
                            nc.vector.tensor_tensor(y_sb[:, p, s], bank[3 + s][:, 0:H], bias[:, e], ALU.add
                                                    ).then_inc(y_ready, 1)

                    def tile(e, t, p, G, S, pair, Y):
                        if e >= NWEAK:
                            for f in range(KF):
                                hold(dve, hi_ready, KF * S + f + KF + 1)
                                nc.vector.tensor_tensor(act_lo[:, f], v[:, f % 2], act_hi[:, f], ALU.subtract
                                                        ).then_inc(lo_ready, 1)
                        lower(G + l + 1, 1 - p)
                        results(e, G, p, pair)

                    nc.vector.tensor_tensor(moved[:], expert_no[:].unsqueeze(1).to_broadcast([P, 2 * NB, NE]),
                                            idx_all[:].unsqueeze(2).to_broadcast([P, 2 * NB, NE]), ALU.is_equal)
                    dve.drain()
                    nc.vector.tensor_tensor(moved[:], moved[:], shift[:].unsqueeze(1).to_broadcast([P, 2 * NB, NE]), ALU.mult)
                    dve.drain()
                    nc.vector.tensor_reduce(idx_all[:], moved[:], AX.X, ALU.add)
                    dve.drain()
                    nc.vector.tensor_tensor(slots_all[:], slots_f[:], idx_all[:], ALU.add)
                    hold(dve, small_in, 48 * (l + 1))
                    lower(2 * first_pair(dve) + l, 0)
                    each_expert(dve, tile, place=False, at_once=True)

                def phase_c(l):
                    def lower(b, u):
                        at = bass.ds(b, 1)
                        hold(dve, hi_kept, NB * l + b + 1)
                        nc.vector.tensor_tensor(h_lo[:, at].rearrange("p o f -> p (o f)"), h_new[:, u],
                                                h_hi[:, at].rearrange("p o f -> p (o f)"), ALU.subtract)

                    def step(b, v, i, rows=P):
                        combine(dve, y_got, l, b, v, i, rows).then_inc(combined, 1)
                        lower(b - 1, (v - 1) % 2)

                    combine(dve, y_got, l, 0, 0, 0).then_inc(combined, 1)
                    turns = (NB - 1) // GOT
                    with dve.Fori(0, turns - 1) as i:
                        for k in range(GOT):
                            step(GOT * i + 1 + k, (k + 1) % GOT, i + (k + 1) // GOT)
                    for k in range(GOT):
                        b = GOT * (turns - 1) + 1 + k
                        step(b, (k + 1) % GOT, b // GOT, P if b < NB - 1 else LROWS)
                    lower(NB - 1, 0)

                layers(phase_a, phase_b, phase_c, dve)

            @block.tensor
            def _(pe):
                slow = pe.value_load(slow_flag[0:1, 0:1], min_val=0, max_val=1)
                pe.sem_inc(agg_done, 2)
                pe.sem_inc(xT_done, 2)

                def phase_a(l):
                    def transpose_mean(b, u):
                        n = NB * l + b
                        pe.wait_ge(agg_ready, n + 3)
                        hold(pe, aT_ready, n + 1)
                        for k in range(KH):
                            last = nc.tensor.transpose(bank[2 + u][:, k * P:(k + 1) * P], agg[:, u, k * P:(k + 1) * P],
                                                       identf[:])
                        last.then_inc(aT_done, 1)

                    def logits(b, u):
                        n = NB * l + b
                        hold(pe, aT_ready, n + 3)
                        hold(pe, lg_taken, n + 1)
                        for k in range(KH):
                            last = nc.tensor.matmul(bank[4][:, 0:NE1], aT[:, u, k, :],
                                                    route_sb[:, bass.ds(l, 1), KH + k, :].rearrange("p o e -> p (o e)"),
                                                    start=(k == 0), stop=(k == KH - 1))
                        last.then_inc(lg_done, 1)

                    def ranks(b):
                        hold(pe, member_ready, NB * l + b + 1)
                        nc.tensor.matmul(bank[5][:, 0:NE], before_b[:], member[:], start=True, stop=True)
                        nc.tensor.matmul(bank[5][:, NE:2 * NE], onesb[:], member[:], start=True, stop=True
                                         ).then_inc(rank_done, 1)

                    def aggregate(i, b, u, end, both):
                        n = NB * l + b
                        pe.wait_ge(agg_ready, n + 1)
                        passes = [(2 * n, 0), (2 * n + 1, 1)] if both else [(n, u)]
                        for a, (m, slot) in enumerate(passes):
                            for s in range(NB):
                                if s % SC == 0:
                                    hold(pe, at_ready, NB // SC * m + s // SC + 1)
                                for k, part in enumerate((h_hi, h_lo)):
                                    last = nc.tensor.matmul(bank[u][:, 0:H], at_r[:, slot, s, :], part[:, s, :],
                                                            start=(a + s + k == 0),
                                                            stop=(a == len(passes) - 1 and s == NB - 1 and k == 1))
                                if a == 0 and s == 1 and end not in (0, 1):
                                    ranks(b - 2)
                                elif a == 0 and s == 6 and end != 0:
                                    transpose_mean(b - 1, 1 - u)
                                elif a == 0 and s == 12 and end != 0:
                                    logits(b - 1, 1 - u)
                        last.then_inc(agg_done, 1)

                    with pe.If(slow == 0):
                        blocks_of_a(pe, lambda i, b, u, q, end: aggregate(i, b, u, end, False))
                    with pe.Else():
                        blocks_of_a(pe, lambda i, b, u, q, end: aggregate(i, b, u, end, True))
                    pe.nop()
                    ranks(NB - 2)
                    transpose_mean(NB - 1, 0)
                    logits(NB - 1, 0)
                    ranks(NB - 1)

                def phase_b(l, last):
                    def transposes(p, loads):
                        hold(pe, x_in[p], 16 * loads)
                        for k in range(KH):
                            for s in range(2):
                                last = nc.tensor.transpose(bank[x_bank[p]][:, k * TOK + s * P:k * TOK + (s + 1) * P],
                                                           x_rows[:, p, s, k * P:(k + 1) * P], identf[:])
                        last.then_inc(xT_done, 1)

                    def tile(e, t, p, G, S, pair, Y):
                        X = G + l
                        pe.wait_ge(xl_ready, X + 1)
                        if e < NWEAK:
                            transposes(1 - p, pair + 1 if p == 0 else pair + l + 2)
                            for s in range(2):
                                hold(pe, y_ready, 2 * G + s + 1)
                                terms = [(a, w, k) for k in range(KH)
                                         for a, w in ((x_hi[:, p], w_hi), (x_hi[:, p], w_lo), (x_lo[:, p], w_hi))]
                                for j, (a, w, k) in enumerate(terms):
                                    last = nc.tensor.matmul(bank[3 + s][:, 0:H], a[:, k, s * P:(s + 1) * P],
                                                            w[:, e, k * H:(k + 1) * H], start=(j == 0), stop=(j == 5))
                                last.then_inc(y_done, 1)
                            return
                        for f in range(KF):
                            hold(pe, hi_ready, KF * S + f + 1)
                            terms = [(w, a, k) for k in range(KH)
                                     for w, a in ((w_hi, x_hi[:, p]), (w_hi, x_lo[:, p]), (w_lo, x_hi[:, p]))]
                            for j, (w, a, k) in enumerate(terms):
                                last = nc.tensor.matmul(bank[unit_bank[f]][:, 0:TOK],
                                                        w[:, NWEAK + KH * (e - NWEAK) + k, f * P:(f + 1) * P],
                                                        a[:, k, :], start=(j == 0), stop=(j == 5))
                            last.then_inc(unit_done, 1)
                        transposes(1 - p, pair + 1 if p == 0 else pair + l + 2)
                        for fs in (range(KF // 2), range(KF // 2, KF)):
                            for s in range(2):
                                if fs[0] == 0:
                                    hold(pe, y_ready, 2 * G + s + 1)
                                for f in fs:
                                    if s == 0:
                                        hold(pe, lo_ready, KF * S + f + 3)
                                    q = NWEAK + KH * NSTRONG + (e - NWEAK) * (KF // 2) + f // 2
                                    cols = slice((f % 2) * H, (f % 2 + 1) * H)
                                    for j, (a, w) in enumerate(((act_hi, w_hi), (act_lo, w_hi), (act_hi, w_lo))):
                                        last = nc.tensor.matmul(bank[3 + s][:, 0:H], a[:, f, s * P:(s + 1) * P],
                                                                w[:, q, cols], start=(f + j == 0),
                                                                stop=(f == KF - 1 and j == 2))
                                if fs[-1] == KF - 1:
                                    last.then_inc(y_done, 1)

                    transposes(0, first_pair(pe) + l + 1)
                    each_expert(pe, tile, place=False, at_once=True)

                def phase_c(l):
                    def step(b, u):
                        n = NB * (l + 1) + b
                        transpose_block(pe, n, u)
                        logits_of_block(pe, n - 1, 1 - u, l + 1)

                    transpose_block(pe, NB * (l + 1), 0)
                    with pe.Fori(0, TRIPS) as i:
                        for k in range(2):
                            step(2 * i + 1 + k, 1 - k)
                    logits_of_block(pe, NB * (l + 2) - 1, 0, l + 1)

                layers(phase_a, phase_b, phase_c, pe)

        with ExitStack() as c3:
            L = LAYERS - 1
            x_all = sb("x_out", [P, NB, OUT], F32, c3)
            y_got = sb("y_got", [P, GOT, 2, H], F32, c3)
            w_out_sb = sb("w_out_sb", [P, KH, OUT], F32, c3)
            b_out_sb = sb("b_out_sb", [P, OUT], F32, c3)
            o_in = sem("o_in")
            o_done = sem("o_done")
            o_ready = sem("o_ready")
            o_stored = sem("o_stored")
            block = c3.enter_context(nc.Block())
            GROUP = 6
            assert (NB - 1) % GROUP == 0

            @block.sync
            def _(sp):
                sp.dma_start(x_all[:, 0:NB - 1], x[0:(NB - 1) * P, :].rearrange("(b p) f -> p b f", p=P)).then_inc(o_in, 16)
                sp.dma_start(x_all[0:LROWS, NB - 1], x[(NB - 1) * P:N, :]).then_inc(o_in, 16)
                sp.dma_start(w_out_sb[:], w_out).then_inc(o_in, 16)
                sp.dma_start(b_out_sb[:], b_out.rearrange("(o f) -> o f", o=1).to_broadcast([P, OUT])).then_inc(o_in, 16)
                for g in range((NB - 1) // GROUP):
                    sp.wait_ge(o_ready, GROUP * (g + 1) + 2)
                    sp.dma_start(out[g * GROUP * P:(g + 1) * GROUP * P, :].rearrange("(b p) f -> p b f", p=P),
                                 x_all[:, g * GROUP:(g + 1) * GROUP]).then_inc(o_stored, 16)
                sp.wait_ge(o_ready, NB + 2)
                sp.dma_start(out[(NB - 1) * P:N, :], x_all[0:LROWS, NB - 1]).then_inc(o_stored, 16)
                sp.wait_ge(o_stored, 16 * ((NB - 1) // GROUP + 1))

            @block.gpsimd
            def _(pool):
                collect_all(pool, y_got, L)

            @block.scalar
            def _(act):
                def keep(b, u, uses):
                    n = NB * LAYERS + b
                    act.wait_ge(hT_done, n + 3)
                    act.wait_ge(o_ready, b + 1)
                    nc.scalar.activation(hT[:, u].rearrange("p k n -> p (k n)"), bank[6 + u][:, 0:H], ACT.Copy
                                         ).then_inc(hT_ready, 1)
                in_pairs(act, keep)

            @block.vector
            def _(dve):
                dve.sem_inc(o_ready, 2)
                dve.wait_ge(o_in, 64)
                for b in range(NB):
                    R = slice(0, LROWS if b == NB - 1 else P)
                    nc.vector.tensor_tensor(x_all[R, b], x_all[R, b], b_out_sb[R], ALU.add)
                dve.drain()

                def finish(b, u, rows=P):
                    hold(dve, o_done, b + 1)
                    at = x_all[0:rows, bass.ds(b, 1)].rearrange("p o f -> p (o f)")
                    nc.vector.tensor_tensor(at, at, bank[4 + u][0:rows, 0:OUT], ALU.add).then_inc(o_ready, 1)

                def step(b, v, i, rows=P):
                    combine(dve, y_got, L, b, v, i, rows).then_inc(combined, 1)

                for v in range(GOT):
                    step(v, v, 0)
                    if v:
                        finish(v - 1, (v - 1) % 2)
                with dve.Fori(1, (NB - 1) // GOT) as i:
                    for v in range(GOT):
                        step(GOT * i + v, v, i)
                        finish(GOT * i + v - 1, (v - 1) % 2)
                step(NB - 1, 0, (NB - 1) // GOT, LROWS)
                finish(NB - 2, 1)
                finish(NB - 1, 0, LROWS)

            @block.tensor
            def _(pe):
                pe.wait_ge(o_in, 64)

                def project(b, u, uses):
                    n = NB * LAYERS + b
                    transpose_block(pe, n, u)
                    pe.wait_ge(hT_ready, n + 3)
                    hold(pe, o_ready, b + 1)
                    for k in range(KH):
                        last = nc.tensor.matmul(bank[4 + u][:, 0:OUT], hT[:, u, k, :], w_out_sb[:, k, :],
                                                start=(k == 0), stop=(k == KH - 1))
                    last.then_inc(o_done, 1)
                in_pairs(pe, project)


def kernel(**inputs):
    import numpy as np
    import concourse.bacc as bacc
    from concourse.bass_utils import run_bass_kernel_spmd

    a = {k.replace("L0_gnn_", ""): np.asarray(v) for k, v in inputs.items()}
    L, NS, H, F = a["strong_W1"].shape
    NW = a["weak_W"].shape[1]
    NE = NW + NS
    conf = np.concatenate([a["conf_W"], np.zeros_like(a["conf_W"])], axis=1)
    route_w = np.concatenate([a["router_W"], conf], axis=2).reshape(L, 2 * H // P, P, NE + 1).transpose(0, 2, 1, 3)
    route_b = np.concatenate([a["router_b"], a["conf_b"]], axis=1)
    weak = a["weak_W"].reshape(L, NW, 2, P, H).transpose(0, 1, 3, 2, 4).reshape(L, NW, P, 2 * H)
    first = a["strong_W1"].reshape(L, NS * 2, P, F)
    second = a["strong_W2"].reshape(L, NS * F // (2 * P), 2, P, H).transpose(0, 1, 3, 2, 4).reshape(L, -1, P, 2 * H)
    arrays = {
        "x": a["x"],
        "edges": np.stack([a["src"], a["dst"]], axis=1),
        "dst": a["dst"],
        "w_in": a["W_in"],
        "b_in": a["b_in"],
        "route_w": route_w,
        "route_b": route_b,
        "pieces": np.concatenate([weak, first, second], axis=1),
        "weak_b": a["weak_b"],
        "b1": a["strong_b1"].reshape(L, -1, P).transpose(0, 2, 1),
        "b2": a["strong_b2"],
        "w_out": a["W_out"].reshape(H // P, P, -1).transpose(1, 0, 2),
        "b_out": a["b_out"],
    }
    arrays = {f"in_{k}": np.ascontiguousarray(v) for k, v in arrays.items()}
    nc = bacc.Bacc("TRN2", target_bir_lowering=False, num_devices=1)
    args = [nc.dram_tensor(k, v.shape, mybir.dt.from_np(v.dtype), kind="ExternalInput").ap() for k, v in arrays.items()]
    args.append(nc.dram_tensor("out_0", a["x"].shape, mybir.dt.float32, kind="ExternalOutput").ap())
    gnn_program(nc, *args)
    r = run_bass_kernel_spmd(nc, [arrays], core_ids=[0])
    return r.results[0]["out_0"]
```
